# Optimizing a Trainium2 kernel written in Bass

```python
import numpy as np
import jax
import jax.numpy as jnp

def _softmax(x, axis=-1):
    return jax.nn.softmax(x, axis=axis)

def _gelu(x):
    return jax.nn.gelu(x, approximate=True)

def _silu(x):
    return jax.nn.silu(x)

def _sigmoid(x):
    return jax.nn.sigmoid(x)

def _layernorm(x, axis=-1, eps=1e-05):
    m = jnp.mean(x, axis=axis, keepdims=True)
    v = jnp.var(x, axis=axis, keepdims=True)
    return (x - m) / jnp.sqrt(v + eps)

def _scatter_add(tgt, idx, src, axis=0):
    return tgt.at[idx].add(src)

def _segment_sum(src, seg, n):
    return jax.ops.segment_sum(src, seg, n)
kernel_name = 'mk_decoder_preln_d1_seqx_r4_21a4c3'

def setup_inputs(seed: int=0):
    np.random.seed(seed)
    _w = jnp.asarray

    def _rec_inputs():
        import jax
        import jax.numpy as jnp
        _rk = jax.random.key(seed)
        x = 0.0003765 + 1 * jax.random.normal(jax.random.fold_in(_rk, 1), (16, 256, 512), jnp.float32)
        _lenS = 256 - jax.random.randint(jax.random.fold_in(_rk, 7), (16,), 0, max(1, 256 // 4) + 1, jnp.int32)
        _lenS2 = 256 - jax.random.randint(jax.random.fold_in(_rk, 8), (16,), 0, max(1, 256 // 4) + 1, jnp.int32)
        _ctx_2048P = jax.random.normal(jax.random.fold_in(_rk, 11), (16, 16, 512), jnp.float32)
        _ctx_2048c = jax.random.dirichlet(jax.random.fold_in(_rk, 511), 0.3 * jnp.ones((16,), jnp.float32), (16, 256))
        _ctx_2048t = jnp.einsum('bsk,bkd->bsd', _ctx_2048c, _ctx_2048P)
        _ctx_2048t = _ctx_2048t * jax.lax.rsqrt(jnp.mean(jnp.square(_ctx_2048t)) + 1e-12) * 0.953939
        ctx_2048 = -0.000292821 + 1.00034 * (_ctx_2048t + 0.3 * jax.random.normal(jax.random.fold_in(_rk, 611), (16, 256, 512), jnp.float32))
        return (x, ctx_2048)
    x, ctx_2048 = _rec_inputs()

    def _L0_attn_setup():
        import jax, jax.numpy as jnp
        import numpy as np
        B, T, C, H = (2, 512, 512, 16)
        HD = C // H
        BASE = 10000.0

        def _rope_tables(seq_len, d):
            p = jnp.arange(d // 2, dtype=jnp.float32)
            theta = jnp.power(BASE, -2.0 ** p / d)
            pos = jnp.arange(1, seq_len + 1, dtype=jnp.float32)[:, None]
            c = pos * theta
            ang = jnp.concatenate([c, c], axis=-1)
            return (jnp.cos(ang), jnp.sin(ang))

        def _rope(x):
            d = x.shape[-1]
            cos, sin = _rope_tables(x.shape[-2], d)
            half = d // 2
            x_rot = jnp.concatenate([-x[..., half:], x[..., :half]], axis=-1)
            return x * cos + x_rot * sin
        key = jax.random.key(seed)
        k1, k2, k3 = jax.random.split(key, 3)
        x = jax.random.normal(k1, (B, T, C), dtype=jnp.float32)
        Wqkv = jax.random.normal(k2, (3 * C, C), dtype=jnp.float32) * 0.02
        bqkv = jnp.zeros((3 * C,), dtype=jnp.float32)
        Wo = jax.random.normal(k3, (C, C), dtype=jnp.float32) * 0.02
        bo = jnp.zeros((C,), dtype=jnp.float32)
        return {'x': x, 'Wqkv': Wqkv, 'bqkv': bqkv, 'Wo': Wo, 'bo': bo}
    _L0_attn_all = _L0_attn_setup()
    _L0_attn_in = {k: v for k, v in _L0_attn_all.items() if k in ('Wqkv', 'bqkv', 'Wo', 'bo')}
    del _L0_attn_all

    def _L0_xattn_setup():
        import jax, jax.numpy as jnp
        import numpy as np
        key = jax.random.key(seed)
        k1, k2, k3, k4, k5 = jax.random.split(key, 5)
        B, D_MODEL, L = (2, 256, 512)
        HEAD_DIM = 8
        H = D_MODEL // HEAD_DIM
        return {'k': jax.random.normal(k1, (B, D_MODEL, L), dtype=jnp.float32), 'v': jax.random.normal(k2, (B, D_MODEL, L), dtype=jnp.float32), 'q': jax.random.normal(k3, (B, D_MODEL, L), dtype=jnp.float32), 'ssm_kernel': jax.random.normal(k4, (H, L), dtype=jnp.float32), 'D': jax.random.normal(k5, (H,), dtype=jnp.float32), 'head_dim': HEAD_DIM}
    _L0_xattn_all = _L0_xattn_setup()
    _L0_xattn_in = {k: v for k, v in _L0_xattn_all.items() if k in ('ssm_kernel', 'D')}
    del _L0_xattn_all

    def _L0_ffn_setup():
        import jax, jax.numpy as jnp
        import numpy as np
        B, S, D = (2, 1024, 512)
        E, DFF = (8, 2048)
        TOP_K = 2
        key = jax.random.key(seed)
        ks = jax.random.split(key, 4)
        scale_in = 1.0 / np.sqrt(D)
        scale_ff = 1.0 / np.sqrt(DFF)
        return {'hidden_states': jax.random.normal(ks[0], (B, S, D), dtype=jnp.float32), 'gate_w': jax.random.normal(ks[1], (E, D), dtype=jnp.float32) * scale_in, 'w1': jax.random.normal(ks[2], (E, D, DFF), dtype=jnp.float32) * scale_in, 'b1': jnp.zeros((E, DFF), dtype=jnp.float32), 'w2': jax.random.normal(ks[3], (E, DFF, D), dtype=jnp.float32) * scale_ff, 'b2': jnp.zeros((E, D), dtype=jnp.float32)}
    _L0_ffn_all = _L0_ffn_setup()
    _L0_ffn_in = {k: v for k, v in _L0_ffn_all.items() if k in ('gate_w', 'w1', 'b1', 'w2', 'b2')}
    del _L0_ffn_all
    return {'x': x, 'ctx_2048': ctx_2048, 'L0_attn_Wqkv': _L0_attn_in['Wqkv'], 'L0_attn_bqkv': _L0_attn_in['bqkv'], 'L0_attn_Wo': _L0_attn_in['Wo'], 'L0_attn_bo': _L0_attn_in['bo'], 'L0_xattn_ssm_kernel': _L0_xattn_in['ssm_kernel'], 'L0_xattn_D': _L0_xattn_in['D'], 'L0_ffn_gate_w': _L0_ffn_in['gate_w'], 'L0_ffn_w1': _L0_ffn_in['w1'], 'L0_ffn_b1': _L0_ffn_in['b1'], 'L0_ffn_w2': _L0_ffn_in['w2'], 'L0_ffn_b2': _L0_ffn_in['b2']}

def reference(x, ctx_2048, L0_attn_Wqkv, L0_attn_bqkv, L0_attn_Wo, L0_attn_bo, L0_xattn_ssm_kernel, L0_xattn_D, L0_ffn_gate_w, L0_ffn_w1, L0_ffn_b1, L0_ffn_w2, L0_ffn_b2):
    import jax
    import jax.numpy as jnp

    def _L0_attn_ref(x, Wqkv, bqkv, Wo, bo):
        import jax, jax.numpy as jnp
        import numpy as np
        B, T, C, H = (2, 512, 512, 16)
        HD = C // H
        BASE = 10000.0

        def _rope_tables(seq_len, d):
            p = jnp.arange(d // 2, dtype=jnp.float32)
            theta = jnp.power(BASE, -2.0 ** p / d)
            pos = jnp.arange(1, seq_len + 1, dtype=jnp.float32)[:, None]
            c = pos * theta
            ang = jnp.concatenate([c, c], axis=-1)
            return (jnp.cos(ang), jnp.sin(ang))

        def _rope(x):
            d = x.shape[-1]
            cos, sin = _rope_tables(x.shape[-2], d)
            half = d // 2
            x_rot = jnp.concatenate([-x[..., half:], x[..., :half]], axis=-1)
            return x * cos + x_rot * sin
        b, t, c = x.shape
        qkv = x @ Wqkv.T + bqkv
        q, k, v = jnp.split(qkv, 3, axis=-1)

        def to_heads(z):
            return z.reshape(b, t, H, HD).transpose(0, 2, 1, 3)
        q, k, v = (to_heads(q), to_heads(k), to_heads(v))
        q = _rope(q)
        k = _rope(k)
        scale = 1.0 / jnp.sqrt(jnp.float32(HD))
        att = jnp.einsum('bhqd,bhkd->bhqk', q, k) * scale
        causal = jnp.tril(jnp.ones((t, t), dtype=bool))
        att = jnp.where(causal, att, -jnp.inf)
        att = jax.nn.softmax(att, axis=-1)
        y = jnp.einsum('bhqk,bhkd->bhqd', att, v)
        y = y.transpose(0, 2, 1, 3).reshape(b, t, c)
        y = y @ Wo.T + bo
        return y

    def _L0_xattn_ref(k, v, q, ssm_kernel, D, head_dim):
        import jax, jax.numpy as jnp
        import numpy as np
        B, HD, L = k.shape
        H = HD // head_dim
        fft_size = 2 * L
        k_ = k.reshape(B, H, head_dim, L)
        v_ = v.reshape(B, H, head_dim, L)
        q_ = q.reshape(B, H, head_dim, L)
        kv = jnp.einsum('bhil,bhjl->bijhl', k_, v_)
        kv_f = jnp.fft.rfft(kv, n=fft_size)
        kernel_f = jnp.fft.rfft(ssm_kernel, n=fft_size)
        y = jnp.fft.irfft(kv_f * kernel_f, n=fft_size)[..., :L]
        out = y + kv * D[None, None, None, :, None]
        out = jnp.einsum('bijhl,bhil->bjhl', out, q_)
        out = jnp.transpose(out, (0, 2, 1, 3)).reshape(B, H * head_dim, L)
        return out.astype(k.dtype)

    def _L0_ffn_ref(hidden_states, gate_w, w1, b1, w2, b2):
        import jax, jax.numpy as jnp
        import numpy as np
        B, S, D = (2, 1024, 512)
        E, DFF = (8, 2048)
        TOP_K = 2
        b, s, d = hidden_states.shape
        x = hidden_states.reshape(-1, d)
        router_logits = x @ gate_w.T
        _, sel = jax.lax.top_k(router_logits.sum(axis=0), TOP_K)
        rw = jax.nn.softmax(router_logits[:, sel].astype(jnp.float32), axis=1)
        rw = rw.astype(x.dtype)
        w1s, b1s = (w1[sel], b1[sel])
        w2s, b2s = (w2[sel], b2[sel])
        h = jax.nn.gelu(jnp.einsum('nd,kdf->knf', x, w1s) + b1s[:, None, :])
        y = jnp.einsum('knf,kfd->knd', h, w2s) + b2s[:, None, :]
        out = jnp.einsum('nk,knd->nd', rw, y)
        return out.reshape(b, s, -1)
    x = x + _L0_attn_ref(_layernorm(x, axis=-1), L0_attn_Wqkv, L0_attn_bqkv, L0_attn_Wo, L0_attn_bo)
    x = x + _L0_xattn_ref(ctx_2048, ctx_2048, _layernorm(x, axis=-1), L0_xattn_ssm_kernel, L0_xattn_D, 8)
    x = x + _L0_ffn_ref(_layernorm(x, axis=-1), L0_ffn_gate_w, L0_ffn_w1, L0_ffn_b1, L0_ffn_w2, L0_ffn_b2)
    return x

_drawn_inputs = setup_inputs


def setup_inputs(seed=0):
    import zlib

    import numpy as np

    out = dict(_drawn_inputs(seed))
    spreads = {'L0_attn_bqkv': (0.0, 0.1),
     'L0_attn_bo': (0.0, 0.1),
     'L0_ffn_b1': (0.0, 0.8),
     'L0_ffn_b2': (0.0, 2.0)}
    factors = {'L0_ffn_gate_w': 7.551, 'L0_ffn_w1': 6.721, 'L0_ffn_w2': 6.051}
    for name, (base, spread) in spreads.items():
        noise = np.random.default_rng([zlib.crc32(name.encode()), seed]).standard_normal(out[name].shape)
        drawn = base * np.exp(spread * noise) if base else spread * noise
        out[name] = jnp.asarray(drawn.astype(out[name].dtype))
    for name, factor in factors.items():
        out[name] = (out[name] * factor).astype(out[name].dtype)
    return out
```

```python
from contextlib import ExitStack

import concourse.bass as bass
from concourse import mybir

F32 = mybir.dt.float32
F32R = mybir.dt.float32r
BF16 = mybir.dt.bfloat16
I32 = mybir.dt.int32
U32 = mybir.dt.uint32
ALU = mybir.AluOpType
ACT = mybir.ActivationFunctionType
AX = mybir.AxisListType

P = 128
B, T, C = 16, 256, 512
KT = C // P
NT = T // P
NHEAD, HD = 16, 32
GH = P // HD
SCALE = float(HD) ** -0.5
EPS = 1e-5
MAGIC = float(0x5F3759DF)
MASKED = -1.0e30


def view(ap, offset, dims):
    return bass.AP(tensor=ap.tensor, offset=ap.offset + offset, ap=[list(ap.ap[0])] + [list(d) for d in dims])


def ge(eng, sem, count):
    if isinstance(count, int) and count <= 0:
        return
    eng.wait_ge(sem, count)


def wait_apart(eng, sem, count, passed):
    eng.wait_ge(sem, count)
    if not isinstance(count, int):
        eng.sem_inc(passed, 1)


def newton_rsqrt(pool, sem, passed, base, y, v, a):
    n = 0
    for _ in range(3):
        for op in range(4):
            if op == 0:
                ins = pool.tensor_tensor(a, y, y, ALU.mult)
            elif op == 1:
                ins = pool.tensor_tensor(a, a, v, ALU.mult)
            elif op == 2:
                ins = pool.tensor_scalar(a, a, -0.5, 1.5, ALU.mult, ALU.add)
            else:
                ins = pool.tensor_tensor(y, y, a, ALU.mult)
            n += 1
            ins.then_inc(sem, 1)
            if n < NEWTON:
                wait_apart(pool, sem, base + n, passed)


NEWTON = 12


CH, CI = 32, 8
TAPW = C + P
KX = CI * B + 64
PAIR = 576
HALVES = ((0, 320), (320, 576))
TERM = 9 * P
CONST_LOADS = 3 + 3 * KT


class Batch:

    def __init__(self, k, parity):
        self.k, self.parity = k, parity
        self.n = k * 2 + parity


def batches(n):
    return [Batch(b // 2, b % 2) if 0 <= b < B else None for b in (n + 1, n, n - 1, n - 2)]


def schedule(eng, body):
    for n in (0, 1, 2, 3):
        body(*batches(n))
    with eng.Fori(1, 6) as i:
        body(Batch(i + 1, 1), Batch(i + 1, 0), Batch(i, 1), Batch(i, 0))
        body(Batch(i + 2, 0), Batch(i + 1, 1), Batch(i + 1, 0), Batch(i, 1))
    for n in (14, 15, 16, 17):
        body(*batches(n))


def attention(nc, x, Wqkv, bqkv, Wo, bo, cos_t, sin_t, ssm_kernel, ssm_D, x_mid, taps_d):
    with ExitStack() as ctx:
        def sb(name, shape, dt=F32):
            return ctx.enter_context(nc.sbuf_tensor(name, shape, dt))

        def sem(name):
            return ctx.enter_context(nc.semaphore(name))

        w_stage = sb("w_stage", [P, 4, C])
        y_rows, x_res = w_stage[:, 0:NT, :], w_stage[:, NT:2 * NT, :]
        wT_hi, wT_lo = sb("wT_hi", [P, KT, 3 * C], F32R), sb("wT_lo", [P, KT, 3 * C], F32R)
        woT_hi, woT_lo = sb("woT_hi", [P, KT, C], F32R), sb("woT_lo", [P, KT, C], F32R)
        bias_qk, bias_v, bo_rows = sb("bias_qk", [P, 8]), sb("bias_v", [P, KT]), sb("bo_rows", [P, C])
        cos_s, sin_s = sb("cos_s", [P, T]), sb("sin_s", [P, T])
        ident, ident_b = sb("ident", [P, P]), sb("ident_b", [P, P], BF16)
        mask_b = sb("mask_b", [P, P], BF16)
        x_in = sb("x_in", [P, NT, C])
        stats, mean_var = sb("stats", [P, NT, 6]), sb("mean_var", [P, NT, 2])
        var_eps, rstd, newt = sb("var_eps", [P, NT]), sb("rstd", [P, NT]), sb("newt", [P, NT])
        xT_hi, xT_lo = sb("xT_hi", [P, KT, T], F32R), sb("xT_lo", [P, KT, T], F32R)
        q_rot, q_sin = sb("q_rot", [P, 2, 2, T]), sb("q_sin", [P, 2, 2, T])
        r_hi, r_lo = sb("r_hi", [P, 2, 2 * T], F32R), sb("r_lo", [P, 2, 2 * T], F32R)
        q_stack = [sb(f"q_stack{i}", [P, NHEAD, T], F32R) for i in range(2)]
        k_stack = [sb(f"k_stack{i}", [P, NHEAD, T], F32R) for i in range(2)]
        v_split = [sb(f"v_split{i}", [P, NT, NHEAD, 2, HD], F32R) for i in range(2)]
        row_max, neg_max = sb("row_max", [P, 2, 4]), sb("neg_max", [P, 12, 4])
        row_sum, inv_sum = sb("row_sum", [P, NT, NHEAD]), sb("inv_sum", [P, NT, NHEAD])
        probs = sb("probs", [P, 2, 512])
        p_hi, p_lo = sb("p_hi", [P, 2, 512], F32R), sb("p_lo", [P, 2, 512], F32R)
        y_cross, y_sum = sb("y_cross", [P, NT, GH, HD]), sb("y_sum", [P, NT, GH, HD])
        yT_hi, yT_lo = sb("yT_hi", [P, KT, T], F32R), sb("yT_lo", [P, KT, T], F32R)

        psum = [ctx.enter_context(nc.psum_tensor(f"attn_bank{i}", [P, 512], F32)) for i in range(8)]
        g_bank, s_bank, t_bank, y_bank = psum[0:3], psum[3:5], psum[5:7], psum[7]

        w_loaded = [sem(f"w_loaded{i}") for i in range(4)]
        const_loaded, x_loaded, res_loaded = sem("const_loaded"), sem("x_loaded"), sem("res_loaded")
        taps_zeroed, taps_loaded, taps_built, taps_stored = (sem(nm) for nm in ("taps_zeroed", "taps_loaded", "taps_built", "taps_stored"))
        stacked = [[sem(f"stacked{p_}_{i}") for i in range(4)] for p_ in range(2)]
        x_mid_stored = sem("x_mid_stored")
        zeroed, const_built = sem("zeroed"), sem("const_built")
        w_turned, w_hi_done, w_lo_done = sem("w_turned"), sem("w_hi_done"), sem("w_lo_done")
        stats_chain, guess_done, newton_done, xn_done = sem("stats_chain"), sem("guess_done"), sem("newton_done"), sem("xn_done")
        dve_passed, pool_passed = sem("dve_passed"), sem("pool_passed")
        xt_done, xt_hi_done, xt_lo_done = sem("xt_done"), sem("xt_hi_done"), sem("xt_lo_done")
        qk_done, qk_out = sem("qk_done"), sem("qk_out")
        cos_done, sin_done, rot_done, r_hi_done, r_lo_done = (sem(nm) for nm in ("cos_done", "sin_done", "rot_done", "r_hi_done", "r_lo_done"))
        v_done, v_hi_done, v_lo_done = sem("v_done"), sem("v_hi_done"), sem("v_lo_done")
        yt_done, yt_hi_done, yt_lo_done = sem("yt_done"), sem("yt_hi_done"), sem("yt_lo_done")
        wo_done, res_biased, x_mid_done = sem("wo_done"), sem("res_biased"), sem("x_mid_done")
        scores_done, max_done, neg_done, exp_done = sem("scores_done"), sem("max_done"), sem("neg_done"), sem("exp_done")
        pt_done, p_hi_done, p_lo_done, pv_done = sem("pt_done"), sem("p_hi_done"), sem("p_lo_done"), sem("pv_done")
        cross_out, inv_done, ysum_done, y_done = sem("cross_out"), sem("inv_done"), sem("ysum_done"), sem("y_done")

        def unit(u):
            g, kind = divmod(u, 3)
            heads = range(4) if kind == 0 else range(2 * kind - 2, 2 * kind)
            return g, int(kind > 0), list(heads), P if kind == 0 else T

        def place(g, r):
            return r * 4 + g

        taps = q_rot[0:CH, :, :, :].rearrange("p a b c -> p (a b c)")[:, 0:C]
        taps_backwards = view(taps, C - 1, [[-1, C]])
        taps_D = q_sin[0:CH, 0, 0, 0:1]
        taps_hi = r_hi[0:CH].rearrange("p a b -> p (a b)")[:, 0:TAPW]
        taps_lo = r_lo[0:CH].rearrange("p a b -> p (a b)")[:, 0:TAPW]

        QK_TILES = ((0, 1), (4, 5), (2, 3), (6, 7))
        AFTER_QK = (4, 6, 8, 9)
        ROTATED = (6, 8, 10, 11)
        xm = x_mid

        block = ctx.enter_context(nc.Block())

        @block.sync
        def _(sp):
            sp.dma_start(x_in[:], x[0].rearrange("(t p) c -> p t c", p=P)).then_inc(x_loaded, 16)
            for w in range(16):
                if w >= 4:
                    sp.wait_ge(w_turned, w - 3)
                src = Wqkv[w * P:(w + 1) * P, :] if w < 12 else Wo[(w - 12) * P:(w - 11) * P, :]
                sp.dma_start(w_stage[:, w % 4, :], src).then_inc(w_loaded[w % 4], 16)
                if w == 3:
                    sp.dma_start(taps_D, ssm_D.rearrange("(h o) -> h o", o=1)).then_inc(taps_loaded, 16)
                    sp.dma_start(taps, ssm_kernel).then_inc(taps_loaded, 16)
            sp.wait_ge(taps_built, 3)
            sp.wait_ge(taps_zeroed, 2)
            sp.dma_start(taps_d[0], taps_hi.bitcast(F32)).then_inc(taps_stored, 16)
            sp.dma_start(taps_d[1], taps_lo.bitcast(F32)).then_inc(taps_stored, 16)
            sp.dma_start(cos_s[:], cos_t).then_inc(const_loaded, 16)
            sp.dma_start(sin_s[:], sin_t).then_inc(const_loaded, 16)
            sp.dma_start(bo_rows[:], bo.partition_broadcast(P)).then_inc(const_loaded, 16)
            for k in range(KT):
                src = bqkv[2 * C + k * P:2 * C + (k + 1) * P].rearrange("(p o) -> p o", o=1)
                sp.dma_start(bias_v[:, k:k + 1], src).then_inc(const_loaded, 16)
            for d in range(2 * KT):
                src = bqkv[d * P:(d + 1) * P].rearrange("(r d o) -> d r o", r=GH, o=1)
                sp.dma_start(bias_qk[:, d:d + 1], src, allow_slow_non_contiguous=True).then_inc(const_loaded, 16)

            def body(b0, b1, b2, b3):
                if b3:
                    row3 = sp.snap(b3.n)
                    ge(sp, x_mid_stored, b3.n * 32)
                    sp.dma_start(x_res, x[row3].rearrange("(t p) c -> p t c", p=P)).then_inc(res_loaded, 16)
                if b0:
                    row = sp.snap(b0.n)
                    sp.wait_ge(xt_done, b0.n * 2)
                    sp.dma_start(x_in[:], x[row].rearrange("(t p) c -> p t c", p=P)).then_inc(x_loaded, 16)
                if b1:
                    ge(sp, scores_done, b1.n * 12 - 12)
                    for i in range(4):
                        stack, low, high = (q_stack, 64, (0, 32)) if i % 2 == 0 else (k_stack, 32, (0, 64))
                        g0 = 2 * (i // 2)
                        sp.wait_ge(r_hi_done, b1.n * 4 + (i + 1))
                        sp.wait_ge(r_lo_done, b1.n * 4 + (i + 1))
                        for at, src in ((high[0], r_hi), (high[1], r_hi), (low, r_lo)):
                            dst = stack[b1.parity][at:at + HD].rearrange("d (r g) t -> d r g t", r=GH)[:, :, g0:g0 + 2, :]
                            sp.dma_start(dst.bitcast(F32), src[:, i % 2, :].bitcast(F32)).then_inc(stacked[b1.parity][i], 16)
                if b3:
                    for t in range(NT):
                        sp.wait_ge(x_mid_done, b3.n * 2 + (t + 1))
                        sp.dma_start(xm[t * P:(t + 1) * P, row3, :], x_res[:, t, :]).then_inc(x_mid_stored, 16)

            schedule(sp, body)
            sp.wait_ge(x_mid_stored, 32 * B)

        @block.gpsimd
        def _(pool):
            pool.memset(taps_hi[:, C:TAPW].bitcast(F32), 0.0).then_inc(taps_zeroed, 1)
            pool.memset(taps_lo[:, C:TAPW].bitcast(F32), 0.0).then_inc(taps_zeroed, 1)
            pool.memset(ident[:], 0.0).then_inc(zeroed, 1)
            pool.memset(mask_b[:], 0.0).then_inc(zeroed, 1)
            pool.wait_ge(zeroed, 2)
            pool.affine_select(out=ident[:], in_=ident[:], compare_op=ALU.not_equal, fill=1.0, base=0,
                               pattern=[[-1, P]], channel_multiplier=1).then_inc(zeroed, 1)
            pool.affine_select(out=mask_b[:], in_=mask_b[:], compare_op=ALU.is_ge, fill=MASKED, base=0,
                               pattern=[[-1, P]], channel_multiplier=1).then_inc(const_built, 1)
            pool.wait_ge(zeroed, 3)
            pool.tensor_copy(ident_b[:], ident[:]).then_inc(const_built, 1)

            def newton(b):
                pool.wait_ge(guess_done, b.n + 1)
                newton_rsqrt(pool, newton_done, pool_passed, b.n * NEWTON, rstd[:], var_eps[:], newt[:])

            newton(Batch(0, 0))
            pool.wait_ge(taps_loaded, 32)
            pool.tensor_tensor(taps[:, 0:1], taps[:, 0:1], taps_D, ALU.add).then_inc(taps_built, 1)
            pool.wait_ge(taps_built, 1)
            pool.tensor_copy(taps_hi[:, 0:C], taps_backwards).then_inc(taps_built, 1)
            pool.wait_ge(taps_built, 2)
            pool.tensor_tensor(taps_lo[:, 0:C], taps_backwards, taps_hi[:, 0:C].bitcast(F32), ALU.subtract).then_inc(taps_built, 1)
            pool.wait_ge(const_loaded, 16 * CONST_LOADS)

            def scale_y(b, g):
                pool.wait_ge(ysum_done, b.n * 4 + (g + 1))
                if g == 0:
                    ge(pool, yt_done, b.n * 2)
                out = y_rows.rearrange("p t (h d) -> p t h d", d=HD)[:, :, 4 * g:4 * g + 4, :]
                inv = view(inv_sum[:], 4 * g, [[NHEAD, NT], [1, GH], [0, HD]])
                pool.tensor_tensor(out, y_sum[:], inv, ALU.mult).then_inc(y_done, 1)

            def body(b0, b1, b2, b3):
                for s in range(12):
                    if s == 3 and b3:
                        pool.wait_ge(res_loaded, b3.n * 16 + 16)
                        bo_both = view(bo_rows[:], 0, [[0, NT], [1, C]])
                        pool.tensor_tensor(x_res, x_res, bo_both, ALU.add).then_inc(res_biased, 1)
                    if s == 2 and b3:
                        scale_y(b3, 3)
                    if s in (5, 8, 11) and b2:
                        scale_y(b2, (s - 5) // 3)
                    if s == 4 and b0:
                        newton(b0)
                    if s in AFTER_QK and b1:
                        i = AFTER_QK.index(s)
                        pool.wait_ge(qk_out, b1.n * 4 + (i + 1))
                        pool.wait_ge(sin_done, b1.n * 4 + (i + 1))
                        cos2 = view(cos_s[:], 0, [[0, 2], [1, T]])
                        pool.tensor_tensor(q_rot[:, i % 2], q_rot[:, i % 2], cos2, ALU.mult).then_inc(cos_done, 1)
                        pool.wait_ge(cos_done, b1.n * 4 + (i + 1))
                        pool.tensor_tensor(q_rot[:, i % 2], q_rot[:, i % 2], q_sin[:, i % 2], ALU.add).then_inc(rot_done, 1)

            schedule(pool, body)

        @block.scalar
        def _(act):
            for w in range(16):
                act.wait_ge(w_turned, w + 1)
                dst, src = weight_dst(wT_hi, woT_hi, g_bank, w)
                act.activation(dst, src, ACT.Copy).then_inc(w_hi_done, 1)
            act.wait_ge(const_loaded, 16 * CONST_LOADS)
            act.wait_ge(taps_stored, 32)

            def exps(b, u):
                g, qt, heads, nk = unit(u)
                act.wait_ge(neg_done, b.n * 12 + (u + 1))
                ge(act, pt_done, b.n * 12 + (u - 1))
                if u % 3 == 0:
                    ge(act, inv_done, b.n * 4 + (g - 3))
                for j, r in enumerate(heads):
                    cols = slice(j * nk, (j + 1) * nk)
                    ins = act.activation(probs[:, u % 2, cols], s_bank[u % 2][:, cols], ACT.Exp,
                                         bias=neg_max[:, u, j:j + 1], scale=SCALE,
                                         accum_out=row_sum[:, qt, 4 * g + r:4 * g + r + 1])
                ins.then_inc(exp_done, 1)

            def p_high(b, u):
                act.wait_ge(pt_done, b.n * 12 + (u + 1))
                ge(act, pv_done, b.n * 12 + (u - 1))
                act.activation(p_hi[:, u % 2, :], t_bank[u % 2][:], ACT.Copy).then_inc(p_hi_done, 1)

            def cross(b, g):
                act.wait_ge(pv_done, b.n * 12 + (3 * g + 3))
                ge(act, ysum_done, b.n * 4 + g)
                src = y_bank[:].rearrange("p (t h w d) -> p t h w d", t=NT, h=GH, w=2)[:, :, :, 1, :]
                act.activation(y_cross[:], src, ACT.Copy).then_inc(cross_out, 1)

            def body(b0, b1, b2, b3):
                for s in range(12):
                    bank = g_bank[(s - 1) % 3]
                    if s in ROTATED and b1:
                        i = ROTATED.index(s)
                        act.wait_ge(rot_done, b1.n * 4 + (i + 1))
                        if i < 2:
                            ge(act, stacked[1 - b1.parity][i + 2], (b1.k + b1.parity) * 48)
                        else:
                            act.wait_ge(stacked[b1.parity][i - 2], b1.k * 48 + 48)
                        act.activation(r_hi[:, i % 2, :], q_rot[:, i % 2].rearrange("p m t -> p (m t)"),
                                       ACT.Copy).then_inc(r_hi_done, 1)
                    if s in (1, 2) and b1:
                        t = s - 1
                        act.wait_ge(xt_done, b1.n * 2 + (t + 1))
                        ge(act, v_done, b1.n * 2)
                        act.activation(xT_hi[:, :, t * P:(t + 1) * P], bank[:].rearrange("p (k t) -> p k t", k=KT),
                                       ACT.Copy).then_inc(xt_hi_done, 1)
                    if s in AFTER_QK and b1:
                        i = AFTER_QK.index(s)
                        act.wait_ge(qk_done, b1.n * 4 + (i + 1))
                        ge(act, r_lo_done, b1.n * 4 + (i - 1))
                        for m, tile in enumerate(QK_TILES[i]):
                            ins = act.activation(q_rot[:, i % 2, m, :], bank[:, m * T:(m + 1) * T], ACT.Identity,
                                                 bias=bias_qk[:, tile:tile + 1])
                        ins.then_inc(qk_out, 1)
                    if s in (5, 7) and b3:
                        t = (s - 5) // 2
                        act.wait_ge(yt_done, b3.n * 2 + (t + 1))
                        ge(act, wo_done, b3.n * 2)
                        for k in range(KT):
                            ins = act.activation(yT_hi[:, k, t * P:(t + 1) * P], bank[:, k * P:(k + 1) * P],
                                                 ACT.Identity, bias=bias_v[:, k:k + 1])
                        ins.then_inc(yt_hi_done, 1)
                    if s in (3, 10) and b1:
                        t = (3, 10).index(s)
                        act.wait_ge(v_done, b1.n * 2 + (t + 1))
                        if t == 0:
                            ge(act, pv_done, b1.n * 12 - 12)
                        act.activation(v_split[b1.parity][:, t, :, 0, :], bank[:].rearrange("p (h d) -> p h d", d=HD),
                                       ACT.Copy).then_inc(v_hi_done, 1)
                    if s == 2 and b3:
                        cross(b3, 3)
                    if s in (5, 8, 11) and b2:
                        cross(b2, (s - 5) // 3)
                    if s == 0 and b3:
                        p_high(b3, 11)
                    if s >= 1 and b2:
                        p_high(b2, s - 1)
                    if b2:
                        exps(b2, s)

            schedule(act, body)

        @block.vector
        def _(dve):
            def norm_stats(b):
                dve.wait_ge(x_loaded, b.n * 16 + 16)
                for t in range(NT):
                    dve.bn_stats(stats[:, t, :], x_in[:, t, :]).then_inc(stats_chain, 1)
                for t in range(NT):
                    wait_apart(dve, stats_chain, b.n * 6 + (t + 1), dve_passed)
                    dve.bn_aggr(mean_var[:, t, :], stats[:, t, :]).then_inc(stats_chain, 1)
                dve.wait_ge(stats_chain, b.n * 6 + 4)
                dve.tensor_scalar(var_eps[:], mean_var[:, :, 1], EPS, None, ALU.add).then_inc(stats_chain, 1)
                dve.wait_ge(stats_chain, b.n * 6 + 5)
                dve.tensor_scalar(newt[:].bitcast(I32), var_eps[:].bitcast(I32), 1, None,
                                  ALU.logical_shift_right).then_inc(stats_chain, 1)
                dve.wait_ge(stats_chain, b.n * 6 + 6)
                dve.tensor_scalar(rstd[:].bitcast(I32), newt[:].bitcast(I32), -1.0, MAGIC,
                                  ALU.mult, ALU.add).then_inc(guess_done, 1)

            def norm_apply(b):
                dve.wait_ge(newton_done, b.n * NEWTON + NEWTON)
                for t in range(NT):
                    dve.tensor_scalar(x_in[:, t, :], x_in[:, t, :], mean_var[:, t, 0:1], rstd[:, t:t + 1],
                                      ALU.subtract, ALU.mult).then_inc(xn_done, 1)

            norm_stats(Batch(0, 0))
            for w in range(16):
                dve.wait_ge(w_hi_done, w + 1)
                hi, src = weight_dst(wT_hi, woT_hi, g_bank, w)
                lo, _ = weight_dst(wT_lo, woT_lo, g_bank, w)
                dve.tensor_tensor(lo, src, hi.bitcast(F32), ALU.subtract).then_inc(w_lo_done, 1)
                if w == 2:
                    norm_apply(Batch(0, 0))
            dve.wait_ge(const_loaded, 16 * CONST_LOADS)
            dve.wait_ge(taps_stored, 32)

            def maxima(b, u):
                g, qt, heads, nk = unit(u)
                nh = len(heads)
                dve.wait_ge(scores_done, b.n * 12 + (u + 1))
                dve.tensor_reduce(row_max[:, u % 2, 0:nh], s_bank[u % 2][:].rearrange("p (h k) -> p h k", h=nh),
                                  AX.X, ALU.max).then_inc(max_done, 1)
                dve.wait_ge(max_done, b.n * 12 + (u + 1))
                dve.tensor_scalar(neg_max[:, u, 0:nh], row_max[:, u % 2, 0:nh], -SCALE, None, ALU.mult).then_inc(neg_done, 1)

            def p_low(b, u):
                dve.wait_ge(p_hi_done, b.n * 12 + (u + 1))
                ge(dve, pv_done, b.n * 12 + (u - 1))
                dve.tensor_tensor(p_lo[:, u % 2, :], t_bank[u % 2][:], p_hi[:, u % 2, :].bitcast(F32),
                                  ALU.subtract).then_inc(p_lo_done, 1)

            def combine(b, g):
                if g == 0:
                    ge(dve, y_done, b.n * 4)
                dve.wait_ge(pv_done, b.n * 12 + (3 * g + 3))
                dve.reciprocal(inv_sum[:, :, 4 * g:4 * g + 4], row_sum[:, :, 4 * g:4 * g + 4]).then_inc(inv_done, 1)
                dve.wait_ge(cross_out, b.n * 4 + (g + 1))
                ge(dve, y_done, b.n * 4 + g)
                src = y_bank[:].rearrange("p (t h w d) -> p t h w d", t=NT, h=GH, w=2)[:, :, :, 0, :]
                dve.tensor_tensor(y_sum[:], src, y_cross[:], ALU.add).then_inc(ysum_done, 1)

            def body(b0, b1, b2, b3):
                for s in range(12):
                    if b2:
                        maxima(b2, s)
                    if s == 0 and b3:
                        p_low(b3, 11)
                    if s >= 1 and b2:
                        p_low(b2, s - 1)
                    if s == 2 and b3:
                        combine(b3, 3)
                    if s in (5, 8, 11) and b2:
                        combine(b2, (s - 5) // 3)
                    bank = g_bank[(s - 1) % 3]
                    if s in ROTATED and b1:
                        i = ROTATED.index(s)
                        dve.wait_ge(r_hi_done, b1.n * 4 + (i + 1))
                        dve.tensor_tensor(r_lo[:, i % 2, :], q_rot[:, i % 2].rearrange("p m t -> p (m t)"),
                                          r_hi[:, i % 2, :].bitcast(F32), ALU.subtract).then_inc(r_lo_done, 1)
                    if s in (1, 2) and b1:
                        dve.wait_ge(xt_hi_done, b1.n * 2 + s)
                        cols = slice((s - 1) * P, s * P)
                        dve.tensor_tensor(xT_lo[:, :, cols], bank[:].rearrange("p (k t) -> p k t", k=KT),
                                          xT_hi[:, :, cols].bitcast(F32), ALU.subtract).then_inc(xt_lo_done, 1)
                    if s in AFTER_QK and b1:
                        i = AFTER_QK.index(s)
                        dve.wait_ge(qk_out, b1.n * 4 + (i + 1))
                        ge(dve, rot_done, b1.n * 4 + (i - 1))
                        for half in (0, 64):
                            other = 64 - half
                            sin2 = view(sin_s[other:other + 64], 0, [[0, 2], [1, T]])
                            ins = dve.tensor_tensor(q_sin[half:half + 64, i % 2], q_rot[other:other + 64, i % 2], sin2,
                                                    ALU.mult)
                        ins.then_inc(sin_done, 1)
                    if s in (5, 7) and b3:
                        t = (s - 5) // 2
                        dve.wait_ge(yt_hi_done, b3.n * 2 + (t + 1))
                        for k in range(KT):
                            cols = slice(t * P, (t + 1) * P)
                            ins = dve.scalar_tensor_tensor(out=yT_lo[:, k, cols], in0=bank[:, k * P:(k + 1) * P],
                                                           scalar=bias_v[:, k:k + 1], in1=yT_hi[:, k, cols].bitcast(F32),
                                                           op0=ALU.add, op1=ALU.subtract)
                        ins.then_inc(yt_lo_done, 1)
                    if s in (3, 10) and b1:
                        t = (3, 10).index(s)
                        dve.wait_ge(v_hi_done, b1.n * 2 + (t + 1))
                        vs = v_split[b1.parity]
                        dve.tensor_tensor(vs[:, t, :, 1, :], bank[:].rearrange("p (h d) -> p h d", d=HD),
                                          vs[:, t, :, 0, :].bitcast(F32), ALU.subtract).then_inc(v_lo_done, 1)
                    if s == 3 and b0:
                        norm_stats(b0)
                    if s == 7 and b0:
                        norm_apply(b0)
                    if s == 11 and b3:
                        for t in range(NT):
                            dve.wait_ge(wo_done, b3.n * 2 + (t + 1))
                            dve.wait_ge(res_biased, b3.n + 1)
                            dve.tensor_tensor(x_res[:, t, :], g_bank[(10 + t) % 3][:], x_res[:, t, :],
                                              ALU.add).then_inc(x_mid_done, 1)

            schedule(dve, body)

        @block.tensor
        def _(pe):
            def split_product(out, lhs, rhs, first, last):
                pe.matmul(out, lhs[0], rhs[0], start=first, stop=False)
                pe.matmul(out, lhs[0], rhs[1], start=False, stop=False)
                return pe.matmul(out, lhs[1], rhs[0], start=False, stop=last)

            pe.wait_ge(zeroed, 3)
            for w in range(16):
                pe.wait_ge(w_loaded[w % 4], 16 * (w // 4 + 1))
                if w >= 3:
                    pe.wait_ge(w_lo_done, w - 2)
                for k in range(KT):
                    ins = pe.transpose(g_bank[w % 3][:, k * P:(k + 1) * P], w_stage[:, w % 4, k * P:(k + 1) * P], ident[:])
                ins.then_inc(w_turned, 1)
            pe.wait_ge(w_lo_done, 16)
            pe.wait_ge(const_built, 2)

            def scores(b, u):
                g, qt, heads, nk = unit(u)
                ge(pe, exp_done, b.n * 12 + (u - 1))
                if u % 6 == 0:
                    for i in (u // 3, u // 3 + 1):
                        pe.wait_ge(stacked[b.parity][i], b.k * 48 + 48)
                for j, r in enumerate(heads):
                    h = place(g, r)
                    out = s_bank[u % 2]
                    pe.matmul(out[:, j * nk:(j + 1) * nk], q_stack[b.parity][0:96, h, qt * P:(qt + 1) * P],
                              k_stack[b.parity][0:96, h, 0:nk], start=True, stop=False)
                    ins = pe.matmul(out[:, (j + 1) * nk - P:(j + 1) * nk], ident_b[:], mask_b[:], start=False, stop=True)
                ins.then_inc(scores_done, 1)

            def turn_probs(b, u):
                pe.wait_ge(exp_done, b.n * 12 + (u + 1))
                ge(pe, p_lo_done, b.n * 12 + (u - 1))
                for k in range(4):
                    ins = pe.transpose(t_bank[u % 2][:, k * P:(k + 1) * P], probs[:, u % 2, k * P:(k + 1) * P], ident[:])
                ins.then_inc(pt_done, 1)

            def values(b, u):
                g, qt, heads, nk = unit(u)
                pe.wait_ge(p_lo_done, b.n * 12 + (u + 1))
                if u == 0:
                    pe.wait_ge(v_lo_done, b.n * 2 + 2)
                if u % 3 == 0:
                    ge(pe, ysum_done, b.n * 4 + g)
                v = v_split[b.parity]
                nb = nk // P
                for j, r in enumerate(heads):
                    col = (qt * GH + r) * 2 * HD
                    for k in range(nb):
                        blk = slice((j * nb + k) * P, (j * nb + k + 1) * P)
                        pe.matmul(y_bank[:, col:col + 2 * HD], p_hi[:, u % 2, blk],
                                  v[:, k, 4 * g + r].rearrange("p w d -> p (w d)"), start=(k == 0), stop=False)
                    for k in range(nb):
                        blk = slice((j * nb + k) * P, (j * nb + k + 1) * P)
                        ins = pe.matmul(y_bank[:, col:col + HD], p_lo[:, u % 2, blk], v[:, k, 4 * g + r, 0, :],
                                        start=False, stop=(k == nb - 1))
                ins.then_inc(pv_done, 1)

            def turn_x(b, t):
                pe.wait_ge(xn_done, b.n * 2 + (t + 1))
                for k in range(KT):
                    ins = pe.transpose(g_bank[t][:, k * P:(k + 1) * P], x_in[:, t, k * P:(k + 1) * P], ident[:])
                ins.then_inc(xt_done, 1)

            def project_qk(b, i, bank):
                for m, tile in enumerate(QK_TILES[i]):
                    for k in range(KT):
                        cols = slice(tile * P, (tile + 1) * P)
                        ins = split_product(bank[:, m * T:(m + 1) * T], (wT_hi[:, k, cols], wT_lo[:, k, cols]),
                                            (xT_hi[:, k, :], xT_lo[:, k, :]), k == 0, k == KT - 1)
                ins.then_inc(qk_done, 1)

            def project_rows(lhs, rhs, cols, rcols, bank, done):
                for k in range(KT):
                    ins = split_product(bank[:], (lhs[0][:, k, cols], lhs[1][:, k, cols]),
                                        (rhs[0][:, k, rcols], rhs[1][:, k, rcols]), k == 0, k == KT - 1)
                ins.then_inc(done, 1)

            def general(s, b1, b3):
                bank = g_bank[s % 3]
                if s == 0 and b1:
                    ge(pe, v_lo_done, b1.n * 2)
                    turn_x(b1, 0)
                if s == 1 and b1:
                    ge(pe, qk_out, b1.n * 4)
                    if b3:
                        ge(pe, x_mid_done, b3.n * 2 - 1)
                    turn_x(b1, 1)
                if s in (2, 9) and b1:
                    t = (2, 9).index(s)
                    if b3:
                        ge(pe, x_mid_done, b3.n * 2)
                    if b3 and t:
                        pe.wait_ge(yt_lo_done, b3.n * 2 + 2)
                    pe.wait_ge(xt_lo_done, b1.n * 2 + (t + 1))
                    project_rows((xT_hi, xT_lo), (wT_hi, wT_lo), slice(t * P, (t + 1) * P), slice(2 * C, 3 * C), bank, v_done)
                if s in (3, 5, 7, 8) and b1:
                    i = (3, 5, 7, 8).index(s)
                    pe.wait_ge(xt_lo_done, b1.n * 2 + 2)
                    if i == 1:
                        pe.wait_ge(v_lo_done, b1.n * 2 + 1)
                    if i == 2 and b3:
                        pe.wait_ge(yt_lo_done, b3.n * 2 + 1)
                    if i == 3:
                        pe.wait_ge(qk_out, b1.n * 4 + 2)
                    project_qk(b1, i, bank)
                if s in (4, 6) and b3:
                    t = (4, 6).index(s)
                    if b1 and t == 0:
                        pe.wait_ge(xt_lo_done, b1.n * 2 + 2)
                    if b1 and t == 1:
                        pe.wait_ge(qk_out, b1.n * 4 + 1)
                    if not b1:
                        pe.wait_ge(x_mid_done, b3.n * 2)
                        pe.wait_ge(v_lo_done, 2 * B)
                        pe.wait_ge(yt_lo_done, b3.n * 2)
                    pe.wait_ge(y_done, b3.n * 4 + 4)
                    for k in range(KT):
                        ins = pe.transpose(bank[:, k * P:(k + 1) * P], y_rows[:, t, k * P:(k + 1) * P], ident[:])
                    ins.then_inc(yt_done, 1)
                if s in (10, 11) and b3:
                    t = s - 10
                    pe.wait_ge(yt_lo_done, b3.n * 2 + (t + 1))
                    if b1:
                        pe.wait_ge(qk_out, b1.n * 4 + (t + 3))
                    else:
                        pe.wait_ge(x_mid_done, b3.n * 2)
                    project_rows((yT_hi, yT_lo), (woT_hi, woT_lo), slice(t * P, (t + 1) * P), slice(0, C), bank, wo_done)

            def body(b0, b1, b2, b3):
                for s in range(12):
                    if b2:
                        scores(b2, s)
                    if s == 0 and b3:
                        turn_probs(b3, 11)
                    if s >= 1 and b2:
                        turn_probs(b2, s - 1)
                    general(s, b1, b3)
                    if s <= 1 and b3:
                        values(b3, s + 10)
                    if s >= 2 and b2:
                        values(b2, s - 2)

            schedule(pe, body)


def weight_dst(w_qkv, w_o, g_bank, w):
    if w < 8:
        dst = w_qkv[:, :, w * P:(w + 1) * P].rearrange("p k (d r) -> p k r d", r=GH)
        return dst, g_bank[w % 3][:].rearrange("p (k r d) -> p k r d", k=KT, r=GH)
    dst = w_qkv[:, :, w * P:(w + 1) * P] if w < 12 else w_o[:, :, (w - 12) * P:(w - 11) * P]
    return dst, g_bank[w % 3][:].rearrange("p (k o) -> p k o", k=KT)


def rotary_tables():
    import numpy as np
    half = HD // 2
    p = np.arange(half, dtype=np.float32)
    theta = np.power(np.float32(10000.0), -np.power(np.float32(2.0), p) / np.float32(HD)).astype(np.float32)
    angle = np.arange(1, T + 1, dtype=np.float32)[:, None] * theta
    freq = (np.arange(P) // GH) % half
    sign = np.where(np.arange(P) < P // 2, 1.0, -1.0).astype(np.float32)[:, None]
    return np.cos(angle).T[freq].copy(), np.sin(angle).T[freq] * sign


def backwards(rows):
    return view(rows, P - 1, [[P, KT], [-1, P]])


class Head:

    def __init__(self, k, parity):
        self.k, self.parity = k, parity
        self.n = k * 2 + parity


def heads_at(n):
    return [Head(h // 2, h % 2) if 0 <= h < CH else None for h in (n + 1, n, n - 1)]


def conv_schedule(eng, body):
    for n in (-1, 0, 1, 2, 3):
        body(*heads_at(n))
    with eng.Fori(2, 15) as i:
        body(Head(i, 1), Head(i, 0), Head(i - 1, 1))
        body(Head(i + 1, 0), Head(i, 1), Head(i, 0))
    for n in (30, 31, 32):
        body(*heads_at(n))


def split_product(pe, out, lhs, rhs, first, last):
    pe.matmul(out, lhs[0], rhs[0], start=first, stop=False)
    pe.matmul(out, lhs[0], rhs[1], start=False, stop=False)
    return pe.matmul(out, lhs[1], rhs[0], start=False, stop=last)


def convolution(nc, x_mid, ctx_in, taps_d, gate_w, logits, x_out, zT_d):
    with ExitStack() as ctx:
        def sb(name, shape, dt=F32):
            return ctx.enter_context(nc.sbuf_tensor(name, shape, dt))

        def sem(name):
            return ctx.enter_context(nc.semaphore(name))

        ident = sb("conv_ident", [P, P])
        gate_rows = sb("gate_rows", [CI, C])
        gateT_hi, gateT_lo = sb("gateT_hi", [P, KT, CI], F32R), sb("gateT_lo", [P, KT, CI], F32R)
        ctx_rows, mid_rows, res_rows = sb("ctx_rows", [P, C]), sb("mid_rows", [P, C]), sb("res_rows", [P, C])
        q_rows = sb("q_rows", [P, C])
        out_rows, z_rows = sb("out_rows", [P, C]), sb("z_rows", [P, C])
        taps_hi, taps_lo = ([sb(f"taps_{w}{i}", [P, C], F32R) for i in range(2)] for w in ("hi", "lo"))
        kT = sb("kT", [P, KT, KX])
        qT = [sb(f"qT{i}", [P, KT, KX]) for i in range(2)]
        pairs = sb("pairs", [P, KT, PAIR])
        kv_hi, kv_lo = ([sb(f"kv_{w}{i}", [P, KT, PAIR], F32R) for i in range(2)] for w in ("hi", "lo"))
        terms = [sb(f"terms{i}", [P, KT, TERM]) for i in range(2)]
        acc = sb("acc", [P, KT, P])
        zT_hi, zT_lo = sb("zT_hi", [P, KT, P], F32R), sb("zT_lo", [P, KT, P], F32R)
        stats, mean_var = sb("conv_stats", [P, 2, 6]), sb("conv_mean_var", [P, 2, 2])
        var_eps, rstd, newt = sb("conv_var_eps", [P, 2]), sb("conv_rstd", [P, 2]), sb("conv_newt", [P, 2])

        psum = [ctx.enter_context(nc.psum_tensor(f"conv_bank{i}", [P, 512], F32)) for i in range(8)]
        y_bank = (psum[0:2], psum[2:4])
        kT_bank, qT_bank, out_bank, z_bank = psum[4:8]
        logit_bank = kT_bank

        names = ("zeroed", "terms_zeroed", "const_built", "gate_loaded", "gate_turned", "gate_split", "ctx_loaded", "mid_loaded", "res_loaded",
                 "ctx_turned", "kT_out", "mid_normed", "mid_turned", "qT_out", "pairs_done", "kv_hi_done", "kv_lo_done",
                 "conv_done", "terms_done", "half_summed", "acc_done", "acc_turned", "out_done", "out_normed",
                 "z_turned", "z_hi_done", "z_lo_done", "logits_done", "logits_out", "out_stored", "z_stored",
                 "dve_passed", "pool_passed")
        S = {nm: sem("conv_" + nm) for nm in names}
        taps_loaded = [sem(f"conv_taps_loaded{i}") for i in range(2)]
        stats_chain = [sem(f"conv_stats_chain{i}") for i in range(2)]
        guess_done = [sem(f"conv_guess_done{i}") for i in range(2)]
        newton_done = [sem(f"conv_newton_done{i}") for i in range(2)]
        mid_v = x_mid.rearrange("s b c -> (s b) c")

        block = ctx.enter_context(nc.Block())

        @block.sync
        def _(sp):
            sp.dma_start(gate_rows[:], gate_w).then_inc(S["gate_loaded"], 16)

            def body(h0, h1, h2):
                if h0:
                    h = sp.snap(h0.n)
                    ge(sp, S["ctx_turned"], h0.n)
                    src = ctx_in[:, bass.ds(h * CI, CI), :].rearrange("b i c -> i b c")
                    sp.dma_start(ctx_rows[:], src).then_inc(S["ctx_loaded"], 16)
                    ge(sp, S["mid_normed"], h0.n)
                    sp.dma_start(mid_rows[:], mid_v[bass.ds(h * P, P), :]).then_inc(S["mid_loaded"], 16)
                    ge(sp, S["conv_done"], h0.n * 4 - 4)
                    for w, dst in ((0, taps_hi), (1, taps_lo)):
                        band = taps_d[w, h, :]
                        band = bass.AP(tensor=band.tensor, offset=band.offset, ap=[[1, P], [1, C]])
                        sp.dma_start(dst[h0.parity][:].bitcast(F32), band).then_inc(taps_loaded[h0.parity], 16)
                if h2:
                    h = sp.snap(h2.n)
                    ge(sp, S["out_done"], h2.n)
                    sp.dma_start(res_rows[:], mid_v[bass.ds(h * P, P), :]).then_inc(S["res_loaded"], 16)
                    sp.wait_ge(S["out_done"], h2.n + 1)
                    sp.dma_start(x_out[h], out_rows[:]).then_inc(S["out_stored"], 16)
                    sp.wait_ge(S["z_lo_done"], h2.n + 1)
                    sp.dma_start(zT_d[0, h], zT_hi[:].bitcast(F32)).then_inc(S["z_stored"], 16)
                    sp.dma_start(zT_d[1, h], zT_lo[:].bitcast(F32)).then_inc(S["z_stored"], 16)

            conv_schedule(sp, body)
            sp.wait_ge(S["out_stored"], 16 * CH)
            sp.wait_ge(S["z_stored"], 32 * CH)

        @block.gpsimd
        def _(pool):
            pool.memset(ident[:], 0.0).then_inc(S["zeroed"], 1)
            pool.wait_ge(S["zeroed"], 1)
            pool.affine_select(out=ident[:], in_=ident[:], compare_op=ALU.not_equal, fill=1.0, base=0,
                               pattern=[[-1, P]], channel_multiplier=1).then_inc(S["const_built"], 1)

            def newton(h, w):
                pool.wait_ge(guess_done[w], h.n + 1)
                newton_rsqrt(pool, newton_done[w], S["pool_passed"], h.n * NEWTON,
                             rstd[:, w:w + 1], var_eps[:, w:w + 1], newt[:, w:w + 1])

            def body(h0, h1, h2):
                if h0:
                    newton(h0, 0)
                    pool.wait_ge(S["kT_out"], h0.n * 2 + 2)
                    ge(pool, S["kv_lo_done"], h0.n)
                    k, p = kT[:], pairs[:]
                    row = [KX, KT]
                    pool.tensor_tensor(view(p, 0, [[PAIR, KT], [P, 2], [1, P]]), view(k, 0, [row, [0, 2], [1, P]]),
                                       view(k, 0, [row, [B, 2], [1, P]]), ALU.mult).then_inc(S["pairs_done"], 1)
                    pool.tensor_tensor(view(p, 320, [[PAIR, KT], [P, 2], [1, P]]), view(k, 0, [row, [0, 2], [1, P]]),
                                       view(k, 2 * B, [row, [B, 2], [1, P]]), ALU.mult).then_inc(S["pairs_done"], 1)
                    pool.tensor_tensor(view(p, 256, [[PAIR, KT], [1, 64]]), view(k, 0, [row, [1, 64]]),
                                       view(k, 64, [row, [1, 64]]), ALU.mult).then_inc(S["pairs_done"], 1)
                if h2:
                    newton(h2, 1)
                if h1:
                    pool.wait_ge(S["terms_done"], h1.n * 4 + 4)
                    t = terms[h1.parity]
                    for j, (a, b) in enumerate(((5, 6), (7, 8), (5, 7))):
                        if j == 2:
                            pool.wait_ge(S["half_summed"], h1.n * 3 + 2)
                        pool.tensor_tensor(t[:, :, a * P:(a + 1) * P], t[:, :, a * P:(a + 1) * P], t[:, :, b * P:(b + 1) * P],
                                           ALU.add).then_inc(S["half_summed"], 1)

            conv_schedule(pool, body)

        @block.scalar
        def _(act):
            def body(h0, h1, h2):
                if h0:
                    act.wait_ge(S["ctx_turned"], h0.n + 1)
                    ge(act, S["pairs_done"], h0.n * 3)
                    src = kT_bank[:].rearrange("p (k t) -> p k t", k=KT)
                    act.activation(kT[:, :, 0:P], src, ACT.Copy).then_inc(S["kT_out"], 1)
                    act.activation(kT[:, :, P:KX], src[:, :, 0:64], ACT.Copy).then_inc(S["kT_out"], 1)
                    act.wait_ge(S["pairs_done"], h0.n * 3 + 3)
                    ge(act, S["conv_done"], h0.n * 4 - 4)
                    act.activation(kv_hi[h0.parity][:], pairs[:], ACT.Copy).then_inc(S["kv_hi_done"], 1)
                    act.wait_ge(S["mid_turned"], h0.n + 1)
                    ge(act, S["terms_done"], h0.n * 4 - 4)
                    src = qT_bank[:].rearrange("p (k t) -> p k t", k=KT)
                    q = qT[h0.parity]
                    act.activation(q[:, :, 0:P], src, ACT.Copy).then_inc(S["qT_out"], 1)
                    act.activation(q[:, :, P:KX], src[:, :, 0:64], ACT.Copy).then_inc(S["qT_out"], 1)
                if h2:
                    act.wait_ge(S["z_turned"], h2.n + 1)
                    ge(act, S["z_stored"], h2.n * 32)
                    ge(act, S["logits_done"], h2.n)
                    act.activation(zT_hi[:], z_bank[:].rearrange("p (k t) -> p k t", k=KT), ACT.Copy).then_inc(S["z_hi_done"], 1)
                    act.wait_ge(S["logits_done"], h2.n + 1)
                    at = h2.n if isinstance(h2.n, int) else act.snap(h2.n)
                    act.activation(logits[:, bass.ds(at * CI, CI)], logit_bank[:, 0:CI], ACT.Copy).then_inc(S["logits_out"], 1)

            conv_schedule(act, body)

        @block.vector
        def _(dve):
            dve.memset(terms[0][:], 0.0).then_inc(S["terms_zeroed"], 1)
            dve.memset(terms[1][:], 0.0).then_inc(S["terms_zeroed"], 1)
            dve.wait_ge(S["gate_turned"], 1)
            src = kT_bank[:, 0:KT * CI].rearrange("p (k e) -> p k e", k=KT)
            dve.tensor_copy(gateT_hi[:], src).then_inc(S["gate_split"], 1)
            dve.wait_ge(S["gate_split"], 1)
            dve.tensor_tensor(gateT_lo[:], src, gateT_hi[:].bitcast(F32), ALU.subtract).then_inc(S["gate_split"], 1)
            dve.wait_ge(S["terms_zeroed"], 2)

            def norm_stats(h, w, rows):
                chain = stats_chain[w]
                dve.bn_stats(stats[:, w, :], rows).then_inc(chain, 1)
                wait_apart(dve, chain, h.n * 4 + 1, S["dve_passed"])
                dve.bn_aggr(mean_var[:, w, :], stats[:, w, :]).then_inc(chain, 1)
                dve.wait_ge(chain, h.n * 4 + 2)
                dve.tensor_scalar(var_eps[:, w:w + 1], mean_var[:, w, 1:2], EPS, None, ALU.add).then_inc(chain, 1)
                dve.wait_ge(chain, h.n * 4 + 3)
                dve.tensor_scalar(newt[:, w:w + 1].bitcast(I32), var_eps[:, w:w + 1].bitcast(I32), 1, None,
                                  ALU.logical_shift_right).then_inc(chain, 1)
                dve.wait_ge(chain, h.n * 4 + 4)
                dve.tensor_scalar(rstd[:, w:w + 1].bitcast(I32), newt[:, w:w + 1].bitcast(I32), -1.0, MAGIC,
                                  ALU.mult, ALU.add).then_inc(guess_done[w], 1)

            def norm_apply(h, w, out, rows, done):
                dve.wait_ge(newton_done[w], h.n * NEWTON + NEWTON)
                dve.tensor_scalar(out, rows, mean_var[:, w, 0:1], rstd[:, w:w + 1], ALU.subtract, ALU.mult).then_inc(done, 1)

            def products(h, lb):
                ya, yb = y_bank[lb % 2]
                q, t = qT[h.parity][:, lb, :], terms[h.parity][:, lb, :]
                a, b = ya[:], yb[:]
                if lb == 0:
                    dve.wait_ge(S["qT_out"], h.n * 2 + 2)
                    ge(dve, S["acc_done"], h.n - 1)
                dve.wait_ge(S["conv_done"], h.n * 4 + (lb + 1))
                two = [[P, 2], [1, P]]
                for out, y, m in (
                    (view(t, 0, [[P + B, 2], [1, P]]), view(a, 0, two), view(q, 0, [[0, 2], [1, P]])),
                    (view(t, 2 * (P + B), [[P + B, 2], [1, P]]), view(b, 0, two), view(q, 0, [[0, 2], [1, P]])),
                    (view(t, 5 * P, [[1, P]]), view(a, P, [[1, P]]), view(q, B, [[1, P]])),
                    (view(t, 6 * P, two), view(b, 0, two), view(q, 2 * B, [[B, 2], [1, P]])),
                    (view(t, 4 * P + 64, [[4 * P - 64, 2], [1, 64]]), view(a, 2 * P, [[0, 2], [1, 64]]), view(q, 0, [[64, 2], [1, 64]])),
                ):
                    ins = dve.tensor_tensor(out, y, m, ALU.mult)
                ins.then_inc(S["terms_done"], 1)

            def body(h0, h1, h2):
                if h0:
                    dve.wait_ge(S["mid_loaded"], h0.n * 16 + 16)
                    norm_stats(h0, 0, mid_rows[:])
                if h2:
                    dve.wait_ge(S["half_summed"], h2.n * 3 + 3)
                    ge(dve, S["acc_turned"], h2.n)
                    rows = view(terms[h2.parity][:], 0, [[TERM, KT], [1, P], [P, 6]])
                    dve.tensor_reduce(acc[:], rows, AX.X, ALU.add).then_inc(S["acc_done"], 1)
                if h1:
                    products(h1, 0)
                if h0:
                    ge(dve, S["mid_turned"], h0.n)
                    norm_apply(h0, 0, backwards(q_rows[:]), mid_rows[:].rearrange("p (k c) -> p k c", k=KT), S["mid_normed"])
                if h1:
                    products(h1, 1)
                if h2:
                    dve.wait_ge(S["acc_turned"], h2.n + 1)
                    dve.wait_ge(S["res_loaded"], h2.n * 16 + 16)
                    ge(dve, S["out_stored"], h2.n * 16)
                    out, res = (t[:].rearrange("p (k c) -> p k c", k=KT) for t in (out_rows, res_rows))
                    dve.tensor_tensor(out, backwards(out_bank[:]), res, ALU.add).then_inc(S["out_done"], 1)
                    dve.wait_ge(S["out_done"], h2.n + 1)
                    norm_stats(h2, 1, out_rows[:])
                if h1:
                    products(h1, 2)
                if h2:
                    ge(dve, S["z_turned"], h2.n)
                    norm_apply(h2, 1, z_rows[:], out_rows[:], S["out_normed"])
                if h1:
                    products(h1, 3)
                if h0:
                    dve.wait_ge(S["kv_hi_done"], h0.n + 1)
                    dve.tensor_tensor(kv_lo[h0.parity][:], pairs[:], kv_hi[h0.parity][:].bitcast(F32),
                                      ALU.subtract).then_inc(S["kv_lo_done"], 1)
                if h2:
                    dve.wait_ge(S["z_hi_done"], h2.n + 1)
                    dve.tensor_tensor(zT_lo[:], z_bank[:].rearrange("p (k t) -> p k t", k=KT), zT_hi[:].bitcast(F32),
                                      ALU.subtract).then_inc(S["z_lo_done"], 1)

            conv_schedule(dve, body)

        @block.tensor
        def _(pe):
            pe.wait_ge(S["gate_loaded"], 16)
            pe.wait_ge(S["const_built"], 1)
            for k in range(KT):
                ins = pe.transpose(kT_bank[:, k * CI:(k + 1) * CI], gate_rows[:, k * P:(k + 1) * P], ident[0:CI, 0:CI])
            ins.then_inc(S["gate_turned"], 1)
            pe.wait_ge(S["gate_split"], 2)

            def turn(bank, rows, done):
                for k in range(KT):
                    ins = pe.transpose(bank[:, k * P:(k + 1) * P], rows[:, k * P:(k + 1) * P], ident[:])
                ins.then_inc(done, 1)

            def convolve(h, lb):
                if lb == 0:
                    pe.wait_ge(S["kv_lo_done"], h.n + 1)
                    pe.wait_ge(taps_loaded[h.parity], h.k * 32 + 32)
                ge(pe, S["terms_done"], h.n * 4 + (lb - 1))
                for mb in range(lb + 1):
                    r = slice(C - (lb - mb + 1) * P, C - (lb - mb) * P)
                    hi, lo = taps_hi[h.parity][:, r], taps_lo[h.parity][:, r]
                    for bank, (c0, c1) in zip(y_bank[lb % 2], HALVES):
                        ins = split_product(pe, bank[:, 0:c1 - c0], (hi, lo),
                                            (kv_hi[h.parity][:, mb, c0:c1], kv_lo[h.parity][:, mb, c0:c1]),
                                            mb == 0, mb == lb)
                ins.then_inc(S["conv_done"], 1)

            def body(h0, h1, h2):
                if h0:
                    pe.wait_ge(S["ctx_loaded"], h0.n * 16 + 16)
                    ge(pe, S["kT_out"], h0.n * 2)
                    if h2:
                        ge(pe, S["logits_out"], h2.n)
                    turn(kT_bank, ctx_rows, S["ctx_turned"])
                if h1:
                    convolve(h1, 0)
                    convolve(h1, 1)
                if h2:
                    pe.wait_ge(S["acc_done"], h2.n + 1)
                    ge(pe, S["out_done"], h2.n)
                    for k in range(KT):
                        ins = pe.transpose(out_bank[:, k * P:(k + 1) * P], acc[:, k, :], ident[:])
                    ins.then_inc(S["acc_turned"], 1)
                if h1:
                    convolve(h1, 2)
                if h0:
                    pe.wait_ge(S["mid_normed"], h0.n + 1)
                    ge(pe, S["qT_out"], h0.n * 2)
                    turn(qT_bank, q_rows, S["mid_turned"])
                if h1:
                    convolve(h1, 3)
                if h2:
                    pe.wait_ge(S["out_normed"], h2.n + 1)
                    ge(pe, S["z_lo_done"], h2.n)
                    turn(z_bank, z_rows, S["z_turned"])
                    if h0:
                        pe.wait_ge(S["kT_out"], h0.n * 2 + 2)
                    ge(pe, S["logits_out"], h2.n)
                    pe.wait_ge(S["z_lo_done"], h2.n + 1)
                    for k in range(KT):
                        ins = split_product(pe, logit_bank[:, 0:CI], (zT_hi[:, k, :], zT_lo[:, k, :]),
                                            (gateT_hi[:, k, :], gateT_lo[:, k, :]), k == 0, k == KT - 1)
                    ins.then_inc(S["logits_done"], 1)

            conv_schedule(pe, body)


E = 8
F = 2048
FT = F // P
BLOCKS = B * T // 512
TB = 4


def experts(nc, logits, x_d, zT_d, w1, b1, w2, b2, out):
    with ExitStack() as ctx:
        def sb(name, shape, dt=F32):
            return ctx.enter_context(nc.sbuf_tensor(name, shape, dt))

        def sem(name):
            return ctx.enter_context(nc.semaphore("moe_" + name))

        w1_hi, w1_lo = sb("w1_hi", [P, FT, KT, P], F32R), sb("w1_lo", [P, FT, KT, P], F32R)
        w2_hi, w2_lo = sb("w2_hi", [P, FT, C], F32R), sb("w2_lo", [P, FT, C], F32R)
        w1_stage, w2_stage = sb("w1_stage", [P, 2, KT, P]), sb("w2_stage", [P, 2, C])
        z_hi, z_lo = ([sb(f"z_{w}{i}", [P, TB, KT, P], F32R) for i in range(2)] for w in ("hi", "lo"))
        hid = sb("hid", [P, 2, 512])
        h_hi, h_lo = sb("h_hi", [P, 2, 512], F32R), sb("h_lo", [P, 2, 512], F32R)
        x_rows = [sb(f"x_rows{i}", [P, TB, C]) for i in range(2)]
        b1_rows, b1_cols, b2_rows = sb("b1_rows", [FT, 2, P]), sb("b1_cols", [P, 2, FT]), sb("b2_rows", [P, 2, C])
        ident, ones, numbers = sb("moe_ident", [FT, FT]), sb("ones", [P, P]), sb("numbers", [P, E])
        tile_sum, total, top = sb("tile_sum", [P, E]), sb("total", [P, E]), sb("top", [P, E])
        chosen, chosen_f = sb("chosen", [P, E], U32), sb("chosen_f", [P, 2])
        is_chosen, picked = sb("is_chosen", [P, 2, E]), sb("picked", [P, CH, E])
        own, share, inv = sb("own", [P, 2, CH]), sb("share", [P, 2, CH]), sb("moe_inv", [P, CH])
        share_now = sb("share_now", [P, TB])

        psum = [ctx.enter_context(nc.psum_tensor(f"moe_bank{i}", [P, 512], F32)) for i in range(8)]
        h_bank, y_bank = psum[0:4], psum[4:8]

        ones_built = sem("ones_built")
        const_built, routed, total_done, exp_done = sem("const_built"), sem("routed"), sem("total_done"), sem("exp_done")
        b1_loaded, b2_loaded, b1_turned, b1_out = sem("b1_loaded"), sem("b2_loaded"), sem("b1_turned"), sem("b1_out")
        w_staged = [sem(f"w_staged{i}") for i in range(2)]
        w_high, w_ready = sem("w_high"), sem("w_ready")
        z_loaded = [sem(f"z_loaded{i}") for i in range(2)]
        x_loaded = [sem(f"x_loaded{i}") for i in range(2)]
        x_stored = [sem(f"x_stored{i}") for i in range(2)]
        h_done, h_bank_free = sem("h_done"), sem("h_bank_free")
        gelu_done, h_high, h_low = sem("gelu_done"), sem("h_high"), sem("h_low")
        y_part = sem("y_part")
        y_done, y_out = sem("y_done"), sem("y_out")
        share_out, x_biased = sem("share_out"), sem("x_biased")

        block = ctx.enter_context(nc.Block())

        def rounds(eng, body):
            for e in range(2):
                with eng.Fori(e * 4, e * 4 + 4) as k:
                    for parity in range(2):
                        body(e, k, parity)

        @block.sync
        def _(sp):
            def load(e, k, parity):
                it = k * 2 + parity
                at = it if isinstance(it, int) else sp.snap(it)
                blk = (at - e * BLOCKS) * TB
                blk = blk if isinstance(blk, int) else sp.snap(blk)
                ge(sp, h_done, it * FT - FT)
                for w, dst in ((0, z_hi), (1, z_lo)):
                    src = zT_d[w, bass.ds(blk, TB)].rearrange("t p k c -> p t (k c)")
                    sp.dma_start(dst[parity][:].rearrange("p t k c -> p t (k c)").bitcast(F32), src).then_inc(z_loaded[parity], 16)
                ge(sp, x_stored[parity], k * 16 if e == 0 else k * 16 * TB + (64 - 4 * 16 * TB))
                sp.dma_start(x_rows[parity][:], x_d[bass.ds(blk, TB)].rearrange("t p c -> p t c")).then_inc(x_loaded[parity], 16)

            def store(e, it, parity):
                at = it if isinstance(it, int) else sp.snap(it)
                if e == 0:
                    blk = at * TB
                    blk = blk if isinstance(blk, int) else sp.snap(blk)
                    sp.wait_ge(y_out, it * TB + (TB + 4))
                    sp.dma_start(x_d[bass.ds(blk, TB)].rearrange("t p c -> p t c"), x_rows[parity][:]).then_inc(x_stored[parity], 16)
                    return
                for t in range(TB):
                    pos = ((at - BLOCKS) * TB + t) * CI
                    pos = pos if isinstance(pos, int) else sp.snap(pos)
                    sp.wait_ge(y_out, it * TB + (t + 1 + 4))
                    dst = out[:, bass.ds(pos, CI), :].rearrange("b i c -> i b c")
                    sp.dma_start(dst, x_rows[parity][:, t, :]).then_inc(x_stored[parity], 16)

            def pair(e, k, e_before):
                load(e, k, 0)
                if e_before is not None:
                    store(e_before, k * 2 - 1, 1)
                load(e, k, 1)
                store(e, k * 2, 0)

            sp.wait_ge(routed, 4)
            for n in range(2):
                e = sp.value_load(chosen[0:1, n:n + 1], min_val=0, max_val=E - 1)
                sp.dma_start(b1_rows[:, n, :], b1[e, :].rearrange("(j p) -> j p", p=P)).then_inc(b1_loaded, 16)
                sp.dma_start(b2_rows[:, n, :], b2[e, :].partition_broadcast(P)).then_inc(b2_loaded, 16)
            pair(0, 0, None)
            with sp.Fori(1, 4) as k:
                pair(0, k, 0)
            pair(1, 4, 0)
            with sp.Fori(5, 8) as k:
                pair(1, k, 1)
            store(1, 2 * BLOCKS - 1, 1)
            for parity in range(2):
                sp.wait_ge(x_stored[parity], 4 * 16 + 4 * 16 * TB)

        @block.gpsimd
        def _(pool):
            pool.memset(ident[:], 0.0).then_inc(const_built, 1)
            pool.wait_ge(const_built, 1)
            pool.affine_select(out=ident[:], in_=ident[:], compare_op=ALU.not_equal, fill=1.0, base=0,
                               pattern=[[-1, FT]], channel_multiplier=1).then_inc(const_built, 1)
            pool.wait_ge(routed, 4)
            expert = [pool.value_load(chosen[0:1, n:n + 1], min_val=0, max_val=E - 1) for n in range(2)]

            def stage(n):
                e, j = expert[n // FT], n % FT
                if n >= 2:
                    pool.wait_ge(w_ready, n - 1)
                src = w1[e, :, j * P:(j + 1) * P].rearrange("(k p) f -> p k f", p=P)
                pool.dma_start(w1_stage[:, n % 2], src).then_inc(w_staged[n % 2], 16)
                pool.dma_start(w2_stage[:, n % 2, :], w2[e, j * P:(j + 1) * P, :]).then_inc(w_staged[n % 2], 16)

            stage(0)
            stage(1)
            for n in range(2 * FT):
                j = n % FT
                pool.wait_ge(w_staged[n % 2], 32 * (n // 2 + 1))
                if n >= FT:
                    pool.wait_ge(y_part, FT * (BLOCKS - 1) + j + 1 + 2)
                pool.tensor_copy(w1_hi[:, j], w1_stage[:, n % 2]).then_inc(w_high, 1)
                pool.tensor_copy(w2_hi[:, j], w2_stage[:, n % 2]).then_inc(w_high, 1)
                pool.wait_ge(w_high, 3 * n + 2)
                pool.tensor_tensor(w1_lo[:, j], w1_stage[:, n % 2], w1_hi[:, j].bitcast(F32), ALU.subtract).then_inc(w_high, 1)
                pool.wait_ge(w_high, 3 * n + 3)
                pool.tensor_tensor(w2_lo[:, j], w2_stage[:, n % 2], w2_hi[:, j].bitcast(F32), ALU.subtract).then_inc(w_ready, 1)
                if n + 2 < 2 * FT:
                    stage(n + 2)

        @block.scalar
        def _(act):
            act.sem_inc(h_bank_free, 4)
            act.wait_ge(routed, ROUTED_EXP)
            act.activation(own[:], own[:], ACT.Exp).then_inc(exp_done, 1)
            act.wait_ge(b1_out, 1)

            def body(e, k, parity):
                it = k * 2 + parity
                for j in range(FT):
                    act.wait_ge(h_done, it * FT + (j + 1))
                    act.wait_ge(h_low, it * FT + (j + 1))
                    act.activation(hid[:, j % 2, :], h_bank[j % 4][:], ACT.Gelu_apprx_tanh,
                                   bias=b1_cols[:, e, j:j + 1]).then_inc(h_bank_free, 1)
                    act.wait_ge(h_bank_free, it * FT + (j + 1 + 4))
                    act.wait_ge(y_part, it * FT + (j + 1))
                    act.activation(h_hi[:, j % 2, :], hid[:, j % 2, :], ACT.Copy).then_inc(h_high, 1)

            rounds(act, body)

        @block.vector
        def _(dve):
            dve.sem_inc(h_low, 2)
            dve.sem_inc(y_out, 4)
            for n in range(E):
                dve.memset(numbers[:, n:n + 1], float(n)).then_inc(ones_built, 1)
            dve.memset(ones[:], 1.0).then_inc(ones_built, 1)
            dve.tensor_reduce(tile_sum[:], view(logits[:], 0, [[1, E], [E, CH]]), AX.X, ALU.add).then_inc(routed, 1)
            dve.wait_ge(total_done, 1)
            dve.tensor_copy(total[:], h_bank[0][:, 0:E]).then_inc(routed, 1)
            dve.wait_ge(routed, 2)
            dve.max(top[:], total[:]).then_inc(routed, 1)
            dve.wait_ge(routed, 3)
            dve.max_index(chosen[:], top[:], total[:]).then_inc(routed, 1)
            dve.wait_ge(routed, 4)
            dve.tensor_copy(chosen_f[:], chosen[:, 0:2]).then_inc(routed, 1)
            dve.wait_ge(routed, 5)
            dve.wait_ge(ones_built, E + 1)
            for n in range(2):
                dve.tensor_scalar(is_chosen[:, n, :], numbers[:], chosen_f[:, n:n + 1], None, ALU.is_equal).then_inc(routed, 1)
            for n in range(2):
                dve.wait_ge(routed, 7 + 2 * n)
                dve.tensor_tensor(picked[:], logits[:].rearrange("p (t e) -> p t e", e=E),
                                  view(is_chosen[:], n * E, [[0, CH], [1, E]]), ALU.mult).then_inc(routed, 1)
                dve.wait_ge(routed, 8 + 2 * n)
                dve.tensor_reduce(own[:, n, :], picked[:], AX.X, ALU.add).then_inc(routed, 1)
            dve.wait_ge(routed, 11)
            dve.tensor_tensor(inv[:], own[:, 0, :], own[:, 1, :], ALU.max).then_inc(routed, 1)
            dve.wait_ge(routed, 12)
            dve.tensor_tensor(own[:], own[:], view(inv[:], 0, [[0, 2], [1, CH]]), ALU.subtract).then_inc(routed, 1)
            dve.wait_ge(exp_done, 1)
            dve.tensor_tensor(inv[:], own[:, 0, :], own[:, 1, :], ALU.add).then_inc(routed, 1)
            dve.wait_ge(routed, 14)
            dve.reciprocal(inv[:], inv[:]).then_inc(routed, 1)
            dve.wait_ge(routed, 15)
            dve.tensor_tensor(share[:], own[:], view(inv[:], 0, [[0, 2], [1, CH]]), ALU.mult).then_inc(routed, 1)
            dve.wait_ge(b1_turned, 1)
            dve.tensor_copy(b1_cols[:], h_bank[1][:, 0:2 * FT].rearrange("p (n j) -> p n j", n=2)).then_inc(b1_out, 1)
            dve.wait_ge(routed, 16)
            dve.wait_ge(b2_loaded, 32)

            def body(e, k, parity):
                it = k * 2 + parity
                for j in range(FT):
                    dve.wait_ge(h_high, it * FT + (j + 1))
                    dve.wait_ge(y_part, it * FT + (j + 1))
                    dve.tensor_tensor(h_lo[:, j % 2, :], hid[:, j % 2, :], h_hi[:, j % 2, :].bitcast(F32),
                                      ALU.subtract).then_inc(h_low, 1)
                    if j == 3:
                        at = dve.snap(it * TB)
                        dve.tensor_copy(share_now[:], share[:].rearrange("p n t -> p (n t)")[:, bass.ds(at, TB)]).then_inc(share_out, 1)
                    if j == 4:
                        dve.wait_ge(x_loaded[parity], k * 16 + 16)
                        dve.wait_ge(share_out, it + 1)
                        for t in range(TB):
                            dve.scalar_tensor_tensor(out=x_rows[parity][:, t, :], in0=b2_rows[:, e, :], scalar=share_now[:, t:t + 1],
                                                     in1=x_rows[parity][:, t, :], op0=ALU.mult, op1=ALU.add).then_inc(x_biased, 1)
                for t in range(TB):
                    if t < TB - 1:
                        dve.wait_ge(y_done, it * (TB - 1) + (t + 1))
                    else:
                        dve.wait_ge(y_part, it * FT + (FT + 2))
                    dve.wait_ge(x_biased, it * TB + (t + 1))
                    dve.scalar_tensor_tensor(out=x_rows[parity][:, t, :], in0=y_bank[t][:], scalar=share_now[:, t:t + 1],
                                             in1=x_rows[parity][:, t, :], op0=ALU.mult, op1=ALU.add).then_inc(y_out, 1)

            rounds(dve, body)

        @block.tensor
        def _(pe):
            pe.sem_inc(y_part, 2)
            pe.wait_ge(const_built, 2)
            pe.wait_ge(ones_built, E + 1)
            pe.wait_ge(routed, 1)
            pe.matmul(h_bank[0][:, 0:E], ones[:], tile_sum[:], start=True, stop=True).then_inc(total_done, 1)
            pe.wait_ge(b1_loaded, 32)
            for n in range(2):
                ins = pe.transpose(h_bank[1][:, n * FT:(n + 1) * FT], b1_rows[:, n, :], ident[:])
            ins.then_inc(b1_turned, 1)
            pe.wait_ge(b1_out, 1)
            pe.wait_ge(routed, 2)

            with pe.Fori(0, 2) as e, pe.Fori(0, 4) as b:
                for parity in range(2):
                    it = pe.snap(e * 8 + b * 2 + parity)

                    def hidden(j):
                        if parity == 0:
                            pe.wait_ge(w_ready, e * FT + (j + 1))
                        pe.wait_ge(h_bank_free, it * FT + (j + 1))
                        for k in range(KT):
                            ins = split_product(pe, h_bank[j % 4][:], (w1_hi[:, j, k, :], w1_lo[:, j, k, :]),
                                                (z_hi[parity][:, :, k, :], z_lo[parity][:, :, k, :]), k == 0, k == KT - 1)
                        ins.then_inc(h_done, 1)

                    def output(j):
                        pe.wait_ge(h_low, it * FT + (j + 1 + 2))
                        for t in range(TB):
                            if j == 0:
                                pe.wait_ge(y_out, it * TB + (t + 1))
                            rows = slice(t * P, (t + 1) * P)
                            ins = split_product(pe, y_bank[t][:], (h_hi[:, j % 2, rows], h_lo[:, j % 2, rows]),
                                                (w2_hi[:, j, :], w2_lo[:, j, :]), j == 0, j == FT - 1)
                            if j == FT - 1 and t < TB - 1:
                                ins.then_inc(y_done, 1)
                        ins.then_inc(y_part, 1)

                    pe.wait_ge(z_loaded[parity], (e * 4 + b) * 32 + 32)
                    hidden(0)
                    for j in range(FT):
                        if j + 1 < FT:
                            hidden(j + 1)
                        output(j)


ROUTED_EXP = 13


_INS = {"x": "x", "ctx": "ctx_2048", "wqkv": "L0_attn_Wqkv", "bqkv": "L0_attn_bqkv", "wo": "L0_attn_Wo", "bo": "L0_attn_bo",
        "taps": "L0_xattn_ssm_kernel", "D": "L0_xattn_D", "gate": "L0_ffn_gate_w", "w1": "L0_ffn_w1", "b1": "L0_ffn_b1",
        "w2": "L0_ffn_w2", "b2": "L0_ffn_b2"}


def decoder_layer(nc, a, out):
    x_mid = nc.dram_tensor("x_mid", (T, B, C), F32, kind="Internal").ap()
    taps_d = nc.dram_tensor("taps_d", (2, CH, TAPW), F32, kind="Internal").ap()
    x_d = nc.dram_tensor("x_d", (CH, P, C), F32, kind="Internal").ap()
    zT_d = nc.dram_tensor("zT_d", (2, CH, P, KT, P), F32, kind="Internal").ap()
    attention(nc, a["x"], a["wqkv"], a["bqkv"], a["wo"], a["bo"], a["cos"], a["sin"], a["taps"], a["D"], x_mid, taps_d)
    with nc.sbuf_tensor("logits", [P, CH * CI], F32) as logits:
        convolution(nc, x_mid, a["ctx"], taps_d, a["gate"], logits, x_d, zT_d)
        experts(nc, logits, x_d, zT_d, a["w1"], a["b1"], a["w2"], a["b2"], out)


def kernel(**inputs):
    import numpy as np
    import concourse.bacc as bacc
    from concourse.bass_utils import run_bass_kernel_spmd as run

    nc = bacc.Bacc("TRN2", target_bir_lowering=False, num_devices=1)
    cos_t, sin_t = rotary_tables()
    given = {short: np.asarray(inputs[name]) for short, name in _INS.items()}
    given.update(cos=cos_t, sin=sin_t)
    arrays, args = {}, {}
    for name, value in given.items():
        arrays[f"in_{name}"] = np.ascontiguousarray(value)
        args[name] = nc.dram_tensor(f"in_{name}", arrays[f"in_{name}"].shape, F32, kind="ExternalInput").ap()
    out = nc.dram_tensor("out_0", (B, T, C), F32, kind="ExternalOutput").ap()
    decoder_layer(nc, args, out)
    return run(nc, [arrays], core_ids=[0]).results[0]["out_0"]
```

```python
from contextlib import ExitStack

import concourse.bass as bass
from concourse import mybir

F32 = mybir.dt.float32
F32R = mybir.dt.float32r
BF16 = mybir.dt.bfloat16
I32 = mybir.dt.int32
U32 = mybir.dt.uint32
ALU = mybir.AluOpType
ACT = mybir.ActivationFunctionType
AX = mybir.AxisListType

P = 128
B, T, C = 16, 256, 512
KT = C // P
NT = T // P
NHEAD, HD = 16, 32
GH = P // HD
SCALE = float(HD) ** -0.5
EPS = 1e-5
MAGIC = float(0x5F3759DF)
MASKED = -1.0e30


def view(ap, offset, dims):
    return bass.AP(tensor=ap.tensor, offset=ap.offset + offset, ap=[list(ap.ap[0])] + [list(d) for d in dims])


def ge(eng, sem, count):
    if isinstance(count, int) and count <= 0:
        return
    eng.wait_ge(sem, count)


def wait_apart(eng, sem, count, passed):
    eng.wait_ge(sem, count)
    if not isinstance(count, int):
        eng.sem_inc(passed, 1)


def newton_rsqrt(pool, sem, passed, base, y, v, a):
    n = 0
    for _ in range(3):
        for op in range(4):
            if op == 0:
                ins = pool.tensor_tensor(a, y, y, ALU.mult)
            elif op == 1:
                ins = pool.tensor_tensor(a, a, v, ALU.mult)
            elif op == 2:
                ins = pool.tensor_scalar(a, a, -0.5, 1.5, ALU.mult, ALU.add)
            else:
                ins = pool.tensor_tensor(y, y, a, ALU.mult)
            n += 1
            ins.then_inc(sem, 1)
            if n < NEWTON:
                wait_apart(pool, sem, base + n, passed)


NEWTON = 12


CH, CI = 32, 8
TAPW = C + P
KX = CI * B + 64
PAIR = 576
HALVES = ((0, 320), (320, 576))
TERM = 9 * P
CONST_LOADS = 3 + 3 * KT


class Batch:

    def __init__(self, k, parity):
        self.k, self.parity = k, parity
        self.n = k * 2 + parity


def batches(n):
    return [Batch(b // 2, b % 2) if 0 <= b < B else None for b in (n + 1, n, n - 1, n - 2)]


def schedule(eng, body):
    for n in (0, 1, 2, 3):
        body(*batches(n))
    with eng.Fori(1, 6) as i:
        body(Batch(i + 1, 1), Batch(i + 1, 0), Batch(i, 1), Batch(i, 0))
        body(Batch(i + 2, 0), Batch(i + 1, 1), Batch(i + 1, 0), Batch(i, 1))
    for n in (14, 15, 16, 17):
        body(*batches(n))


def attention(nc, x, Wqkv, bqkv, Wo, bo, cos_t, sin_t, ssm_kernel, ssm_D, x_mid, taps_d):
    with ExitStack() as ctx:
        def sb(name, shape, dt=F32):
            return ctx.enter_context(nc.sbuf_tensor(name, shape, dt))

        def sem(name):
            return ctx.enter_context(nc.semaphore(name))

        w_stage = sb("w_stage", [P, 4, C])
        y_rows, x_res = w_stage[:, 0:NT, :], w_stage[:, NT:2 * NT, :]
        wT_hi, wT_lo = sb("wT_hi", [P, KT, 3 * C], F32R), sb("wT_lo", [P, KT, 3 * C], F32R)
        woT_hi, woT_lo = sb("woT_hi", [P, KT, C], F32R), sb("woT_lo", [P, KT, C], F32R)
        bias_qk, bias_v, bo_rows = sb("bias_qk", [P, 8]), sb("bias_v", [P, KT]), sb("bo_rows", [P, C])
        cos_s, sin_s = sb("cos_s", [P, T]), sb("sin_s", [P, T])
        ident, ident_b = sb("ident", [P, P]), sb("ident_b", [P, P], BF16)
        mask_b = sb("mask_b", [P, P], BF16)
        x_in = sb("x_in", [P, NT, C])
        stats, mean_var = sb("stats", [P, NT, 6]), sb("mean_var", [P, NT, 2])
        var_eps, rstd, newt = sb("var_eps", [P, NT]), sb("rstd", [P, NT]), sb("newt", [P, NT])
        xT_hi, xT_lo = sb("xT_hi", [P, KT, T], F32R), sb("xT_lo", [P, KT, T], F32R)
        q_rot, q_sin = sb("q_rot", [P, 2, 2, T]), sb("q_sin", [P, 2, 2, T])
        r_hi, r_lo = sb("r_hi", [P, 2, 2 * T], F32R), sb("r_lo", [P, 2, 2 * T], F32R)
        q_stack = [sb(f"q_stack{i}", [P, NHEAD, T], F32R) for i in range(2)]
        k_stack = [sb(f"k_stack{i}", [P, NHEAD, T], F32R) for i in range(2)]
        v_split = [sb(f"v_split{i}", [P, NT, NHEAD, 2, HD], F32R) for i in range(2)]
        row_max, neg_max = sb("row_max", [P, 2, 4]), sb("neg_max", [P, 12, 4])
        row_sum, inv_sum = sb("row_sum", [P, NT, NHEAD]), sb("inv_sum", [P, NT, NHEAD])
        probs = sb("probs", [P, 2, 512])
        p_hi, p_lo = sb("p_hi", [P, 2, 512], F32R), sb("p_lo", [P, 2, 512], F32R)
        y_cross, y_sum = sb("y_cross", [P, NT, GH, HD]), sb("y_sum", [P, NT, GH, HD])
        yT_hi, yT_lo = sb("yT_hi", [P, KT, T], F32R), sb("yT_lo", [P, KT, T], F32R)

        psum = [ctx.enter_context(nc.psum_tensor(f"attn_bank{i}", [P, 512], F32)) for i in range(8)]
        g_bank, s_bank, t_bank, y_bank = psum[0:3], psum[3:5], psum[5:7], psum[7]

        w_loaded = [sem(f"w_loaded{i}") for i in range(4)]
        const_loaded, x_loaded, res_loaded = sem("const_loaded"), sem("x_loaded"), sem("res_loaded")
        taps_zeroed, taps_loaded, taps_built, taps_stored = (sem(nm) for nm in ("taps_zeroed", "taps_loaded", "taps_built", "taps_stored"))
        stacked = [[sem(f"stacked{p_}_{i}") for i in range(4)] for p_ in range(2)]
        x_mid_stored = sem("x_mid_stored")
        zeroed, const_built = sem("zeroed"), sem("const_built")
        w_turned, w_hi_done, w_lo_done = sem("w_turned"), sem("w_hi_done"), sem("w_lo_done")
        stats_chain, guess_done, newton_done, xn_done = sem("stats_chain"), sem("guess_done"), sem("newton_done"), sem("xn_done")
        dve_passed, pool_passed = sem("dve_passed"), sem("pool_passed")
        xt_done, xt_hi_done, xt_lo_done = sem("xt_done"), sem("xt_hi_done"), sem("xt_lo_done")
        qk_done, qk_out = sem("qk_done"), sem("qk_out")
        cos_done, sin_done, rot_done, r_hi_done, r_lo_done = (sem(nm) for nm in ("cos_done", "sin_done", "rot_done", "r_hi_done", "r_lo_done"))
        v_done, v_hi_done, v_lo_done = sem("v_done"), sem("v_hi_done"), sem("v_lo_done")
        yt_done, yt_hi_done, yt_lo_done = sem("yt_done"), sem("yt_hi_done"), sem("yt_lo_done")
        wo_done, res_biased, x_mid_done = sem("wo_done"), sem("res_biased"), sem("x_mid_done")
        scores_done, max_done, neg_done, exp_done = sem("scores_done"), sem("max_done"), sem("neg_done"), sem("exp_done")
        pt_done, p_hi_done, p_lo_done, pv_done = sem("pt_done"), sem("p_hi_done"), sem("p_lo_done"), sem("pv_done")
        cross_out, inv_done, ysum_done, y_done = sem("cross_out"), sem("inv_done"), sem("ysum_done"), sem("y_done")

        def unit(u):
            g, kind = divmod(u, 3)
            heads = range(4) if kind == 0 else range(2 * kind - 2, 2 * kind)
            return g, int(kind > 0), list(heads), P if kind == 0 else T

        def place(g, r):
            return r * 4 + g

        taps = q_rot[0:CH, :, :, :].rearrange("p a b c -> p (a b c)")[:, 0:C]
        taps_backwards = view(taps, C - 1, [[-1, C]])
        taps_D = q_sin[0:CH, 0, 0, 0:1]
        taps_hi = r_hi[0:CH].rearrange("p a b -> p (a b)")[:, 0:TAPW]
        taps_lo = r_lo[0:CH].rearrange("p a b -> p (a b)")[:, 0:TAPW]

        QK_TILES = ((0, 1), (4, 5), (2, 3), (6, 7))
        AFTER_QK = (4, 6, 8, 9)
        ROTATED = (6, 8, 10, 11)
        xm = x_mid

        block = ctx.enter_context(nc.Block())

        @block.sync
        def _(sp):
            sp.dma_start(x_in[:], x[0].rearrange("(t p) c -> p t c", p=P)).then_inc(x_loaded, 16)
            for w in range(16):
                if w >= 4:
                    sp.wait_ge(w_turned, w - 3)
                src = Wqkv[w * P:(w + 1) * P, :] if w < 12 else Wo[(w - 12) * P:(w - 11) * P, :]
                sp.dma_start(w_stage[:, w % 4, :], src).then_inc(w_loaded[w % 4], 16)
                if w == 3:
                    sp.dma_start(taps_D, ssm_D.rearrange("(h o) -> h o", o=1)).then_inc(taps_loaded, 16)
                    sp.dma_start(taps, ssm_kernel).then_inc(taps_loaded, 16)
            sp.wait_ge(taps_built, 3)
            sp.wait_ge(taps_zeroed, 2)
            sp.dma_start(taps_d[0], taps_hi.bitcast(F32)).then_inc(taps_stored, 16)
            sp.dma_start(taps_d[1], taps_lo.bitcast(F32)).then_inc(taps_stored, 16)
            sp.dma_start(cos_s[:], cos_t).then_inc(const_loaded, 16)
            sp.dma_start(sin_s[:], sin_t).then_inc(const_loaded, 16)
            sp.dma_start(bo_rows[:], bo.partition_broadcast(P)).then_inc(const_loaded, 16)
            for k in range(KT):
                src = bqkv[2 * C + k * P:2 * C + (k + 1) * P].rearrange("(p o) -> p o", o=1)
                sp.dma_start(bias_v[:, k:k + 1], src).then_inc(const_loaded, 16)
            for d in range(2 * KT):
                src = bqkv[d * P:(d + 1) * P].rearrange("(r d o) -> d r o", r=GH, o=1)
                sp.dma_start(bias_qk[:, d:d + 1], src, allow_slow_non_contiguous=True).then_inc(const_loaded, 16)

            def body(b0, b1, b2, b3):
                if b3:
                    row3 = sp.snap(b3.n)
                    ge(sp, x_mid_stored, b3.n * 32)
                    sp.dma_start(x_res, x[row3].rearrange("(t p) c -> p t c", p=P)).then_inc(res_loaded, 16)
                if b0:
                    row = sp.snap(b0.n)
                    sp.wait_ge(xt_done, b0.n * 2)
                    sp.dma_start(x_in[:], x[row].rearrange("(t p) c -> p t c", p=P)).then_inc(x_loaded, 16)
                if b1:
                    ge(sp, scores_done, b1.n * 12 - 12)
                    for i in range(4):
                        stack, low, high = (q_stack, 64, (0, 32)) if i % 2 == 0 else (k_stack, 32, (0, 64))
                        g0 = 2 * (i // 2)
                        sp.wait_ge(r_hi_done, b1.n * 4 + (i + 1))
                        sp.wait_ge(r_lo_done, b1.n * 4 + (i + 1))
                        for at, src in ((high[0], r_hi), (high[1], r_hi), (low, r_lo)):
                            dst = stack[b1.parity][at:at + HD].rearrange("d (r g) t -> d r g t", r=GH)[:, :, g0:g0 + 2, :]
                            sp.dma_start(dst.bitcast(F32), src[:, i % 2, :].bitcast(F32)).then_inc(stacked[b1.parity][i], 16)
                if b3:
                    for t in range(NT):
                        sp.wait_ge(x_mid_done, b3.n * 2 + (t + 1))
                        sp.dma_start(xm[t * P:(t + 1) * P, row3, :], x_res[:, t, :]).then_inc(x_mid_stored, 16)

            schedule(sp, body)
            sp.wait_ge(x_mid_stored, 32 * B)

        @block.gpsimd
        def _(pool):
            pool.memset(taps_hi[:, C:TAPW].bitcast(F32), 0.0).then_inc(taps_zeroed, 1)
            pool.memset(taps_lo[:, C:TAPW].bitcast(F32), 0.0).then_inc(taps_zeroed, 1)
            pool.memset(ident[:], 0.0).then_inc(zeroed, 1)
            pool.memset(mask_b[:], 0.0).then_inc(zeroed, 1)
            pool.wait_ge(zeroed, 2)
            pool.affine_select(out=ident[:], in_=ident[:], compare_op=ALU.not_equal, fill=1.0, base=0,
                               pattern=[[-1, P]], channel_multiplier=1).then_inc(zeroed, 1)
            pool.affine_select(out=mask_b[:], in_=mask_b[:], compare_op=ALU.is_ge, fill=MASKED, base=0,
                               pattern=[[-1, P]], channel_multiplier=1).then_inc(const_built, 1)
            pool.wait_ge(zeroed, 3)
            pool.tensor_copy(ident_b[:], ident[:]).then_inc(const_built, 1)

            def newton(b):
                pool.wait_ge(guess_done, b.n + 1)
                newton_rsqrt(pool, newton_done, pool_passed, b.n * NEWTON, rstd[:], var_eps[:], newt[:])

            newton(Batch(0, 0))
            pool.wait_ge(taps_loaded, 32)
            pool.tensor_tensor(taps[:, 0:1], taps[:, 0:1], taps_D, ALU.add).then_inc(taps_built, 1)
            pool.wait_ge(taps_built, 1)
            pool.tensor_copy(taps_hi[:, 0:C], taps_backwards).then_inc(taps_built, 1)
            pool.wait_ge(taps_built, 2)
            pool.tensor_tensor(taps_lo[:, 0:C], taps_backwards, taps_hi[:, 0:C].bitcast(F32), ALU.subtract).then_inc(taps_built, 1)
            pool.wait_ge(const_loaded, 16 * CONST_LOADS)

            def scale_y(b, g):
                pool.wait_ge(ysum_done, b.n * 4 + (g + 1))
                if g == 0:
                    ge(pool, yt_done, b.n * 2)
                out = y_rows.rearrange("p t (h d) -> p t h d", d=HD)[:, :, 4 * g:4 * g + 4, :]
                inv = view(inv_sum[:], 4 * g, [[NHEAD, NT], [1, GH], [0, HD]])
                pool.tensor_tensor(out, y_sum[:], inv, ALU.mult).then_inc(y_done, 1)

            def body(b0, b1, b2, b3):
                for s in range(12):
                    if s == 3 and b3:
                        pool.wait_ge(res_loaded, b3.n * 16 + 16)
                        bo_both = view(bo_rows[:], 0, [[0, NT], [1, C]])
                        pool.tensor_tensor(x_res, x_res, bo_both, ALU.add).then_inc(res_biased, 1)
                    if s == 2 and b3:
                        scale_y(b3, 3)
                    if s in (5, 8, 11) and b2:
                        scale_y(b2, (s - 5) // 3)
                    if s == 4 and b0:
                        newton(b0)
                    if s in AFTER_QK and b1:
                        i = AFTER_QK.index(s)
                        pool.wait_ge(qk_out, b1.n * 4 + (i + 1))
                        pool.wait_ge(sin_done, b1.n * 4 + (i + 1))
                        cos2 = view(cos_s[:], 0, [[0, 2], [1, T]])
                        pool.tensor_tensor(q_rot[:, i % 2], q_rot[:, i % 2], cos2, ALU.mult).then_inc(cos_done, 1)
                        pool.wait_ge(cos_done, b1.n * 4 + (i + 1))
                        pool.tensor_tensor(q_rot[:, i % 2], q_rot[:, i % 2], q_sin[:, i % 2], ALU.add).then_inc(rot_done, 1)

            schedule(pool, body)

        @block.scalar
        def _(act):
            for w in range(16):
                act.wait_ge(w_turned, w + 1)
                dst, src = weight_dst(wT_hi, woT_hi, g_bank, w)
                act.activation(dst, src, ACT.Copy).then_inc(w_hi_done, 1)
            act.wait_ge(const_loaded, 16 * CONST_LOADS)
            act.wait_ge(taps_stored, 32)

            def exps(b, u):
                g, qt, heads, nk = unit(u)
                act.wait_ge(neg_done, b.n * 12 + (u + 1))
                ge(act, pt_done, b.n * 12 + (u - 1))
                if u % 3 == 0:
                    ge(act, inv_done, b.n * 4 + (g - 3))
                for j, r in enumerate(heads):
                    cols = slice(j * nk, (j + 1) * nk)
                    ins = act.activation(probs[:, u % 2, cols], s_bank[u % 2][:, cols], ACT.Exp,
                                         bias=neg_max[:, u, j:j + 1], scale=SCALE,
                                         accum_out=row_sum[:, qt, 4 * g + r:4 * g + r + 1])
                ins.then_inc(exp_done, 1)

            def p_high(b, u):
                act.wait_ge(pt_done, b.n * 12 + (u + 1))
                ge(act, pv_done, b.n * 12 + (u - 1))
                act.activation(p_hi[:, u % 2, :], t_bank[u % 2][:], ACT.Copy).then_inc(p_hi_done, 1)

            def cross(b, g):
                act.wait_ge(pv_done, b.n * 12 + (3 * g + 3))
                ge(act, ysum_done, b.n * 4 + g)
                src = y_bank[:].rearrange("p (t h w d) -> p t h w d", t=NT, h=GH, w=2)[:, :, :, 1, :]
                act.activation(y_cross[:], src, ACT.Copy).then_inc(cross_out, 1)

            def body(b0, b1, b2, b3):
                for s in range(12):
                    bank = g_bank[(s - 1) % 3]
                    if s in ROTATED and b1:
                        i = ROTATED.index(s)
                        act.wait_ge(rot_done, b1.n * 4 + (i + 1))
                        if i < 2:
                            ge(act, stacked[1 - b1.parity][i + 2], (b1.k + b1.parity) * 48)
                        else:
                            act.wait_ge(stacked[b1.parity][i - 2], b1.k * 48 + 48)
                        act.activation(r_hi[:, i % 2, :], q_rot[:, i % 2].rearrange("p m t -> p (m t)"),
                                       ACT.Copy).then_inc(r_hi_done, 1)
                    if s in (1, 2) and b1:
                        t = s - 1
                        act.wait_ge(xt_done, b1.n * 2 + (t + 1))
                        ge(act, v_done, b1.n * 2)
                        act.activation(xT_hi[:, :, t * P:(t + 1) * P], bank[:].rearrange("p (k t) -> p k t", k=KT),
                                       ACT.Copy).then_inc(xt_hi_done, 1)
                    if s in AFTER_QK and b1:
                        i = AFTER_QK.index(s)
                        act.wait_ge(qk_done, b1.n * 4 + (i + 1))
                        ge(act, r_lo_done, b1.n * 4 + (i - 1))
                        for m, tile in enumerate(QK_TILES[i]):
                            ins = act.activation(q_rot[:, i % 2, m, :], bank[:, m * T:(m + 1) * T], ACT.Identity,
                                                 bias=bias_qk[:, tile:tile + 1])
                        ins.then_inc(qk_out, 1)
                    if s in (5, 7) and b3:
                        t = (s - 5) // 2
                        act.wait_ge(yt_done, b3.n * 2 + (t + 1))
                        ge(act, wo_done, b3.n * 2)
                        for k in range(KT):
                            ins = act.activation(yT_hi[:, k, t * P:(t + 1) * P], bank[:, k * P:(k + 1) * P],
                                                 ACT.Identity, bias=bias_v[:, k:k + 1])
                        ins.then_inc(yt_hi_done, 1)
                    if s in (3, 10) and b1:
                        t = (3, 10).index(s)
                        act.wait_ge(v_done, b1.n * 2 + (t + 1))
                        if t == 0:
                            ge(act, pv_done, b1.n * 12 - 12)
                        act.activation(v_split[b1.parity][:, t, :, 0, :], bank[:].rearrange("p (h d) -> p h d", d=HD),
                                       ACT.Copy).then_inc(v_hi_done, 1)
                    if s == 2 and b3:
                        cross(b3, 3)
                    if s in (5, 8, 11) and b2:
                        cross(b2, (s - 5) // 3)
                    if s == 0 and b3:
                        p_high(b3, 11)
                    if s >= 1 and b2:
                        p_high(b2, s - 1)
                    if b2:
                        exps(b2, s)

            schedule(act, body)

        @block.vector
        def _(dve):
            def norm_stats(b):
                dve.wait_ge(x_loaded, b.n * 16 + 16)
                for t in range(NT):
                    dve.bn_stats(stats[:, t, :], x_in[:, t, :]).then_inc(stats_chain, 1)
                for t in range(NT):
                    wait_apart(dve, stats_chain, b.n * 6 + (t + 1), dve_passed)
                    dve.bn_aggr(mean_var[:, t, :], stats[:, t, :]).then_inc(stats_chain, 1)
                dve.wait_ge(stats_chain, b.n * 6 + 4)
                dve.tensor_scalar(var_eps[:], mean_var[:, :, 1], EPS, None, ALU.add).then_inc(stats_chain, 1)
                dve.wait_ge(stats_chain, b.n * 6 + 5)
                dve.tensor_scalar(newt[:].bitcast(I32), var_eps[:].bitcast(I32), 1, None,
                                  ALU.logical_shift_right).then_inc(stats_chain, 1)
                dve.wait_ge(stats_chain, b.n * 6 + 6)
                dve.tensor_scalar(rstd[:].bitcast(I32), newt[:].bitcast(I32), -1.0, MAGIC,
                                  ALU.mult, ALU.add).then_inc(guess_done, 1)

            def norm_apply(b):
                dve.wait_ge(newton_done, b.n * NEWTON + NEWTON)
                for t in range(NT):
                    dve.tensor_scalar(x_in[:, t, :], x_in[:, t, :], mean_var[:, t, 0:1], rstd[:, t:t + 1],
                                      ALU.subtract, ALU.mult).then_inc(xn_done, 1)

            norm_stats(Batch(0, 0))
            for w in range(16):
                dve.wait_ge(w_hi_done, w + 1)
                hi, src = weight_dst(wT_hi, woT_hi, g_bank, w)
                lo, _ = weight_dst(wT_lo, woT_lo, g_bank, w)
                dve.tensor_tensor(lo, src, hi.bitcast(F32), ALU.subtract).then_inc(w_lo_done, 1)
                if w == 2:
                    norm_apply(Batch(0, 0))
            dve.wait_ge(const_loaded, 16 * CONST_LOADS)
            dve.wait_ge(taps_stored, 32)

            def maxima(b, u):
                g, qt, heads, nk = unit(u)
                nh = len(heads)
                dve.wait_ge(scores_done, b.n * 12 + (u + 1))
                dve.tensor_reduce(row_max[:, u % 2, 0:nh], s_bank[u % 2][:].rearrange("p (h k) -> p h k", h=nh),
                                  AX.X, ALU.max).then_inc(max_done, 1)
                dve.wait_ge(max_done, b.n * 12 + (u + 1))
                dve.tensor_scalar(neg_max[:, u, 0:nh], row_max[:, u % 2, 0:nh], -SCALE, None, ALU.mult).then_inc(neg_done, 1)

            def p_low(b, u):
                dve.wait_ge(p_hi_done, b.n * 12 + (u + 1))
                ge(dve, pv_done, b.n * 12 + (u - 1))
                dve.tensor_tensor(p_lo[:, u % 2, :], t_bank[u % 2][:], p_hi[:, u % 2, :].bitcast(F32),
                                  ALU.subtract).then_inc(p_lo_done, 1)

            def combine(b, g):
                if g == 0:
                    ge(dve, y_done, b.n * 4)
                dve.wait_ge(pv_done, b.n * 12 + (3 * g + 3))
                dve.reciprocal(inv_sum[:, :, 4 * g:4 * g + 4], row_sum[:, :, 4 * g:4 * g + 4]).then_inc(inv_done, 1)
                dve.wait_ge(cross_out, b.n * 4 + (g + 1))
                ge(dve, y_done, b.n * 4 + g)
                src = y_bank[:].rearrange("p (t h w d) -> p t h w d", t=NT, h=GH, w=2)[:, :, :, 0, :]
                dve.tensor_tensor(y_sum[:], src, y_cross[:], ALU.add).then_inc(ysum_done, 1)

            def body(b0, b1, b2, b3):
                for s in range(12):
                    if b2:
                        maxima(b2, s)
                    if s == 0 and b3:
                        p_low(b3, 11)
                    if s >= 1 and b2:
                        p_low(b2, s - 1)
                    if s == 2 and b3:
                        combine(b3, 3)
                    if s in (5, 8, 11) and b2:
                        combine(b2, (s - 5) // 3)
                    bank = g_bank[(s - 1) % 3]
                    if s in ROTATED and b1:
                        i = ROTATED.index(s)
                        dve.wait_ge(r_hi_done, b1.n * 4 + (i + 1))
                        dve.tensor_tensor(r_lo[:, i % 2, :], q_rot[:, i % 2].rearrange("p m t -> p (m t)"),
                                          r_hi[:, i % 2, :].bitcast(F32), ALU.subtract).then_inc(r_lo_done, 1)
                    if s in (1, 2) and b1:
                        dve.wait_ge(xt_hi_done, b1.n * 2 + s)
                        cols = slice((s - 1) * P, s * P)
                        dve.tensor_tensor(xT_lo[:, :, cols], bank[:].rearrange("p (k t) -> p k t", k=KT),
                                          xT_hi[:, :, cols].bitcast(F32), ALU.subtract).then_inc(xt_lo_done, 1)
                    if s in AFTER_QK and b1:
                        i = AFTER_QK.index(s)
                        dve.wait_ge(qk_out, b1.n * 4 + (i + 1))
                        ge(dve, rot_done, b1.n * 4 + (i - 1))
                        for half in (0, 64):
                            other = 64 - half
                            sin2 = view(sin_s[other:other + 64], 0, [[0, 2], [1, T]])
                            ins = dve.tensor_tensor(q_sin[half:half + 64, i % 2], q_rot[other:other + 64, i % 2], sin2,
                                                    ALU.mult)
                        ins.then_inc(sin_done, 1)
                    if s in (5, 7) and b3:
                        t = (s - 5) // 2
                        dve.wait_ge(yt_hi_done, b3.n * 2 + (t + 1))
                        for k in range(KT):
                            cols = slice(t * P, (t + 1) * P)
                            ins = dve.scalar_tensor_tensor(out=yT_lo[:, k, cols], in0=bank[:, k * P:(k + 1) * P],
                                                           scalar=bias_v[:, k:k + 1], in1=yT_hi[:, k, cols].bitcast(F32),
                                                           op0=ALU.add, op1=ALU.subtract)
                        ins.then_inc(yt_lo_done, 1)
                    if s in (3, 10) and b1:
                        t = (3, 10).index(s)
                        dve.wait_ge(v_hi_done, b1.n * 2 + (t + 1))
                        vs = v_split[b1.parity]
                        dve.tensor_tensor(vs[:, t, :, 1, :], bank[:].rearrange("p (h d) -> p h d", d=HD),
                                          vs[:, t, :, 0, :].bitcast(F32), ALU.subtract).then_inc(v_lo_done, 1)
                    if s == 3 and b0:
                        norm_stats(b0)
                    if s == 7 and b0:
                        norm_apply(b0)
                    if s == 11 and b3:
                        for t in range(NT):
                            dve.wait_ge(wo_done, b3.n * 2 + (t + 1))
                            dve.wait_ge(res_biased, b3.n + 1)
                            dve.tensor_tensor(x_res[:, t, :], g_bank[(10 + t) % 3][:], x_res[:, t, :],
                                              ALU.add).then_inc(x_mid_done, 1)

            schedule(dve, body)

        @block.tensor
        def _(pe):
            def split_product(out, lhs, rhs, first, last):
                pe.matmul(out, lhs[0], rhs[0], start=first, stop=False)
                pe.matmul(out, lhs[0], rhs[1], start=False, stop=False)
                return pe.matmul(out, lhs[1], rhs[0], start=False, stop=last)

            pe.wait_ge(zeroed, 3)
            for w in range(16):
                pe.wait_ge(w_loaded[w % 4], 16 * (w // 4 + 1))
                if w >= 3:
                    pe.wait_ge(w_lo_done, w - 2)
                for k in range(KT):
                    ins = pe.transpose(g_bank[w % 3][:, k * P:(k + 1) * P], w_stage[:, w % 4, k * P:(k + 1) * P], ident[:])
                ins.then_inc(w_turned, 1)
            pe.wait_ge(w_lo_done, 16)
            pe.wait_ge(const_built, 2)

            def scores(b, u):
                g, qt, heads, nk = unit(u)
                ge(pe, exp_done, b.n * 12 + (u - 1))
                if u % 6 == 0:
                    for i in (u // 3, u // 3 + 1):
                        pe.wait_ge(stacked[b.parity][i], b.k * 48 + 48)
                for j, r in enumerate(heads):
                    h = place(g, r)
                    out = s_bank[u % 2]
                    pe.matmul(out[:, j * nk:(j + 1) * nk], q_stack[b.parity][0:96, h, qt * P:(qt + 1) * P],
                              k_stack[b.parity][0:96, h, 0:nk], start=True, stop=False)
                    ins = pe.matmul(out[:, (j + 1) * nk - P:(j + 1) * nk], ident_b[:], mask_b[:], start=False, stop=True)
                ins.then_inc(scores_done, 1)

            def turn_probs(b, u):
                pe.wait_ge(exp_done, b.n * 12 + (u + 1))
                ge(pe, p_lo_done, b.n * 12 + (u - 1))
                for k in range(4):
                    ins = pe.transpose(t_bank[u % 2][:, k * P:(k + 1) * P], probs[:, u % 2, k * P:(k + 1) * P], ident[:])
                ins.then_inc(pt_done, 1)

            def values(b, u):
                g, qt, heads, nk = unit(u)
                pe.wait_ge(p_lo_done, b.n * 12 + (u + 1))
                if u == 0:
                    pe.wait_ge(v_lo_done, b.n * 2 + 2)
                if u % 3 == 0:
                    ge(pe, ysum_done, b.n * 4 + g)
                v = v_split[b.parity]
                nb = nk // P
                for j, r in enumerate(heads):
                    col = (qt * GH + r) * 2 * HD
                    for k in range(nb):
                        blk = slice((j * nb + k) * P, (j * nb + k + 1) * P)
                        pe.matmul(y_bank[:, col:col + 2 * HD], p_hi[:, u % 2, blk],
                                  v[:, k, 4 * g + r].rearrange("p w d -> p (w d)"), start=(k == 0), stop=False)
                    for k in range(nb):
                        blk = slice((j * nb + k) * P, (j * nb + k + 1) * P)
                        ins = pe.matmul(y_bank[:, col:col + HD], p_lo[:, u % 2, blk], v[:, k, 4 * g + r, 0, :],
                                        start=False, stop=(k == nb - 1))
                ins.then_inc(pv_done, 1)

            def turn_x(b, t):
                pe.wait_ge(xn_done, b.n * 2 + (t + 1))
                for k in range(KT):
                    ins = pe.transpose(g_bank[t][:, k * P:(k + 1) * P], x_in[:, t, k * P:(k + 1) * P], ident[:])
                ins.then_inc(xt_done, 1)

            def project_qk(b, i, bank):
                for m, tile in enumerate(QK_TILES[i]):
                    for k in range(KT):
                        cols = slice(tile * P, (tile + 1) * P)
                        ins = split_product(bank[:, m * T:(m + 1) * T], (wT_hi[:, k, cols], wT_lo[:, k, cols]),
                                            (xT_hi[:, k, :], xT_lo[:, k, :]), k == 0, k == KT - 1)
                ins.then_inc(qk_done, 1)

            def project_rows(lhs, rhs, cols, rcols, bank, done):
                for k in range(KT):
                    ins = split_product(bank[:], (lhs[0][:, k, cols], lhs[1][:, k, cols]),
                                        (rhs[0][:, k, rcols], rhs[1][:, k, rcols]), k == 0, k == KT - 1)
                ins.then_inc(done, 1)

            def general(s, b1, b3):
                bank = g_bank[s % 3]
                if s == 0 and b1:
                    ge(pe, v_lo_done, b1.n * 2)
                    turn_x(b1, 0)
                if s == 1 and b1:
                    ge(pe, qk_out, b1.n * 4)
                    if b3:
                        ge(pe, x_mid_done, b3.n * 2 - 1)
                    turn_x(b1, 1)
                if s in (2, 9) and b1:
                    t = (2, 9).index(s)
                    if b3:
                        ge(pe, x_mid_done, b3.n * 2)
                    if b3 and t:
                        pe.wait_ge(yt_lo_done, b3.n * 2 + 2)
                    pe.wait_ge(xt_lo_done, b1.n * 2 + (t + 1))
                    project_rows((xT_hi, xT_lo), (wT_hi, wT_lo), slice(t * P, (t + 1) * P), slice(2 * C, 3 * C), bank, v_done)
                if s in (3, 5, 7, 8) and b1:
                    i = (3, 5, 7, 8).index(s)
                    pe.wait_ge(xt_lo_done, b1.n * 2 + 2)
                    if i == 1:
                        pe.wait_ge(v_lo_done, b1.n * 2 + 1)
                    if i == 2 and b3:
                        pe.wait_ge(yt_lo_done, b3.n * 2 + 1)
                    if i == 3:
                        pe.wait_ge(qk_out, b1.n * 4 + 2)
                    project_qk(b1, i, bank)
                if s in (4, 6) and b3:
                    t = (4, 6).index(s)
                    if b1 and t == 0:
                        pe.wait_ge(xt_lo_done, b1.n * 2 + 2)
                    if b1 and t == 1:
                        pe.wait_ge(qk_out, b1.n * 4 + 1)
                    if not b1:
                        pe.wait_ge(x_mid_done, b3.n * 2)
                        pe.wait_ge(v_lo_done, 2 * B)
                        pe.wait_ge(yt_lo_done, b3.n * 2)
                    pe.wait_ge(y_done, b3.n * 4 + 4)
                    for k in range(KT):
                        ins = pe.transpose(bank[:, k * P:(k + 1) * P], y_rows[:, t, k * P:(k + 1) * P], ident[:])
                    ins.then_inc(yt_done, 1)
                if s in (10, 11) and b3:
                    t = s - 10
                    pe.wait_ge(yt_lo_done, b3.n * 2 + (t + 1))
                    if b1:
                        pe.wait_ge(qk_out, b1.n * 4 + (t + 3))
                    else:
                        pe.wait_ge(x_mid_done, b3.n * 2)
                    project_rows((yT_hi, yT_lo), (woT_hi, woT_lo), slice(t * P, (t + 1) * P), slice(0, C), bank, wo_done)

            def body(b0, b1, b2, b3):
                for s in range(12):
                    if b2:
                        scores(b2, s)
                    if s == 0 and b3:
                        turn_probs(b3, 11)
                    if s >= 1 and b2:
                        turn_probs(b2, s - 1)
                    general(s, b1, b3)
                    if s <= 1 and b3:
                        values(b3, s + 10)
                    if s >= 2 and b2:
                        values(b2, s - 2)

            schedule(pe, body)


def weight_dst(w_qkv, w_o, g_bank, w):
    if w < 8:
        dst = w_qkv[:, :, w * P:(w + 1) * P].rearrange("p k (d r) -> p k r d", r=GH)
        return dst, g_bank[w % 3][:].rearrange("p (k r d) -> p k r d", k=KT, r=GH)
    dst = w_qkv[:, :, w * P:(w + 1) * P] if w < 12 else w_o[:, :, (w - 12) * P:(w - 11) * P]
    return dst, g_bank[w % 3][:].rearrange("p (k o) -> p k o", k=KT)


def rotary_tables():
    import numpy as np
    half = HD // 2
    p = np.arange(half, dtype=np.float32)
    theta = np.power(np.float32(10000.0), -np.power(np.float32(2.0), p) / np.float32(HD)).astype(np.float32)
    angle = np.arange(1, T + 1, dtype=np.float32)[:, None] * theta
    freq = (np.arange(P) // GH) % half
    sign = np.where(np.arange(P) < P // 2, 1.0, -1.0).astype(np.float32)[:, None]
    return np.cos(angle).T[freq].copy(), np.sin(angle).T[freq] * sign


def backwards(rows):
    return view(rows, P - 1, [[P, KT], [-1, P]])


class Head:

    def __init__(self, k, parity):
        self.k, self.parity = k, parity
        self.n = k * 2 + parity


class Step:

    def __init__(self, k, parity):
        self.k, self.parity = k, parity
        self.n = k * 2 + parity

    def head(self, d):
        if isinstance(self.n, int) and not 0 <= self.n + d < CH:
            return None
        return Head(self.k + (self.parity + d) // 2, (self.parity + d) % 2)


def conv_schedule(body):
    def run(eng):
        for n in range(-3, 4):
            body(Step(n // 2, n % 2))
        with eng.Fori(2, 14) as i:
            body(Step(i, 0))
            body(Step(i, 1))
        for n in range(28, 35):
            body(Step(n // 2, n % 2))
    return run


def split_product(pe, out, lhs, rhs, first, last):
    pe.matmul(out, lhs[0], rhs[0], start=first, stop=False)
    pe.matmul(out, lhs[0], rhs[1], start=False, stop=False)
    return pe.matmul(out, lhs[1], rhs[0], start=False, stop=last)


def convolution(nc, x_mid, ctx_in, taps_d, gate_w, logits, x_out, zT_d):
    with ExitStack() as ctx:
        def sb(name, shape, dt=F32):
            return ctx.enter_context(nc.sbuf_tensor(name, shape, dt))

        def sem(name):
            return ctx.enter_context(nc.semaphore(name))

        ident = sb("conv_ident", [P, P])
        gate_rows = sb("gate_rows", [CI, C])
        gateT_hi, gateT_lo = sb("gateT_hi", [P, KT, CI], F32R), sb("gateT_lo", [P, KT, CI], F32R)
        ctx_rows, mid_rows, res_rows = sb("ctx_rows", [P, C]), sb("mid_rows", [P, C]), sb("res_rows", [P, C])
        q_rows = sb("q_rows", [P, C])
        out_rows, z_rows = sb("out_rows", [P, C]), sb("z_rows", [P, C])
        taps_hi, taps_lo = ([sb(f"taps_{w}{i}", [P, C], F32R) for i in range(2)] for w in ("hi", "lo"))
        kT = sb("kT", [P, KT, KX])
        qT = [sb(f"qT{i}", [P, KT, KX]) for i in range(2)]
        pairs = sb("pairs", [P, KT, PAIR])
        kv_hi, kv_lo = ([sb(f"kv_{w}{i}", [P, KT, PAIR], F32R) for i in range(2)] for w in ("hi", "lo"))
        terms = [sb(f"terms{i}", [P, KT, TERM]) for i in range(2)]
        acc = sb("acc", [P, KT, P])
        zT_hi, zT_lo = sb("zT_hi", [P, KT, P], F32R), sb("zT_lo", [P, KT, P], F32R)
        stats, mean_var = sb("conv_stats", [P, 2, 6]), sb("conv_mean_var", [P, 2, 2])
        var_eps, rstd, newt = sb("conv_var_eps", [P, 2]), sb("conv_rstd", [P, 2]), sb("conv_newt", [P, 2])
        minus_mean, shift = sb("minus_mean", [P, 2]), sb("shift", [P, 2])

        psum = [ctx.enter_context(nc.psum_tensor(f"conv_bank{i}", [P, 512], F32)) for i in range(8)]
        y_bank = (psum[0:2], psum[2:4])
        kT_bank, qT_bank, out_bank, z_bank = psum[4:8]
        logit_bank = z_bank

        names = ("zeroed", "terms_zeroed", "const_built", "gate_loaded", "gate_turned", "gate_split", "ctx_loaded", "mid_loaded", "res_loaded",
                 "ctx_turned", "kT_out", "mid_normed", "mid_turned", "qT_out", "pairs_done", "kv_hi_done", "kv_lo_done",
                 "conv_done", "terms_done", "half_summed", "acc_done", "acc_turned", "out_done", "out_normed",
                 "z_turned", "z_hi_done", "z_lo_done", "logits_done", "logits_out", "out_stored", "z_stored",
                 "norm_cleared", "stats0_chain", "stats1_chain", "guess_chain", "guess_done", "newton_done", "shift_done",
                 "dve_passed", "pool_passed")
        S = {nm: sem("conv_" + nm) for nm in names}
        taps_loaded = [sem(f"conv_taps_loaded{i}") for i in range(2)]
        stats_chain = [S["stats0_chain"], S["stats1_chain"]]
        mid_v = x_mid.rearrange("s b c -> (s b) c")

        block = ctx.enter_context(nc.Block())

        @block.sync
        def _(sp):
            sp.dma_start(gate_rows[:], gate_w).then_inc(S["gate_loaded"], 16)

            def body(step):
                early, front, split, tail, out = (step.head(d) for d in (3, 2, 1, -1, -2))
                if tail:
                    h = sp.snap(tail.n)
                    ge(sp, S["out_done"], tail.n)
                    sp.dma_start(res_rows[:], mid_v[bass.ds(h * P, P), :]).then_inc(S["res_loaded"], 16)
                if split:
                    h = sp.snap(split.n)
                    ge(sp, S["conv_done"], split.n * 4 - 4)
                    for w, dst in ((0, taps_hi), (1, taps_lo)):
                        band = taps_d[w, h, :]
                        band = bass.AP(tensor=band.tensor, offset=band.offset, ap=[[1, P], [1, C]])
                        sp.dma_start(dst[split.parity][:].bitcast(F32), band).then_inc(taps_loaded[split.parity], 16)
                if early:
                    h = sp.snap(early.n)
                    ge(sp, S["ctx_turned"], early.n)
                    src = ctx_in[:, bass.ds(h * CI, CI), :].rearrange("b i c -> i b c")
                    sp.dma_start(ctx_rows[:], src).then_inc(S["ctx_loaded"], 16)
                if front:
                    h = sp.snap(front.n)
                    ge(sp, S["mid_normed"], front.n)
                    sp.dma_start(mid_rows[:], mid_v[bass.ds(h * P, P), :]).then_inc(S["mid_loaded"], 16)
                if tail:
                    h = sp.snap(tail.n)
                    sp.wait_ge(S["out_done"], tail.n + 1)
                    sp.dma_start(x_out[h], out_rows[:]).then_inc(S["out_stored"], 16)
                if out:
                    h = sp.snap(out.n)
                    sp.wait_ge(S["z_lo_done"], out.n + 1)
                    sp.dma_start(zT_d[0, h], zT_hi[:].bitcast(F32)).then_inc(S["z_stored"], 16)
                    sp.dma_start(zT_d[1, h], zT_lo[:].bitcast(F32)).then_inc(S["z_stored"], 16)

            conv_schedule(body)(sp)
            sp.wait_ge(S["out_stored"], 16 * CH)
            sp.wait_ge(S["z_stored"], 32 * CH)

        @block.gpsimd
        def _(pool):
            pool.memset(ident[:], 0.0).then_inc(S["zeroed"], 1)
            pool.wait_ge(S["zeroed"], 1)
            pool.affine_select(out=ident[:], in_=ident[:], compare_op=ALU.not_equal, fill=1.0, base=0,
                               pattern=[[-1, P]], channel_multiplier=1).then_inc(S["const_built"], 1)

            def body(step):
                front, tail = step.head(2), step.head(-1)
                if tail:
                    pool.wait_ge(S["terms_done"], tail.n * 4 + 4)
                    t = terms[tail.parity]
                    for j, (a, b) in enumerate(((5, 6), (7, 8), (5, 7))):
                        if j == 2:
                            pool.wait_ge(S["half_summed"], tail.n * 3 + 2)
                        pool.tensor_tensor(t[:, :, a * P:(a + 1) * P], t[:, :, a * P:(a + 1) * P], t[:, :, b * P:(b + 1) * P],
                                           ALU.add).then_inc(S["half_summed"], 1)
                if step.head(1) or step.head(-2):
                    j = step.n + 1
                    pool.wait_ge(S["guess_done"], j + 1)
                    newton_rsqrt(pool, S["newton_done"], S["pool_passed"], j * NEWTON, rstd[:], var_eps[:], newt[:])
                    pool.wait_ge(S["newton_done"], j * NEWTON + NEWTON)
                    pool.tensor_tensor(shift[:], minus_mean[:], rstd[:], ALU.mult).then_inc(S["shift_done"], 1)
                if front:
                    pool.wait_ge(S["kT_out"], front.n * 2 + 2)
                    ge(pool, S["kv_lo_done"], front.n)
                    k, p = kT[:], pairs[:]
                    row = [KX, KT]
                    pool.tensor_tensor(view(p, 0, [[PAIR, KT], [P, 2], [1, P]]), view(k, 0, [row, [0, 2], [1, P]]),
                                       view(k, 0, [row, [B, 2], [1, P]]), ALU.mult).then_inc(S["pairs_done"], 1)
                    pool.tensor_tensor(view(p, 320, [[PAIR, KT], [P, 2], [1, P]]), view(k, 0, [row, [0, 2], [1, P]]),
                                       view(k, 2 * B, [row, [B, 2], [1, P]]), ALU.mult).then_inc(S["pairs_done"], 1)
                    pool.tensor_tensor(view(p, 256, [[PAIR, KT], [1, 64]]), view(k, 0, [row, [1, 64]]),
                                       view(k, 64, [row, [1, 64]]), ALU.mult).then_inc(S["pairs_done"], 1)

            conv_schedule(body)(pool)

        @block.scalar
        def _(act):
            def norm_apply(step, w, out, rows, done):
                act.wait_ge(S["shift_done"], step.n + 2)
                act.activation(out, rows, ACT.Identity, bias=shift[:, w:w + 1], scale=rstd[:, w:w + 1]).then_inc(done, 1)

            def body(step):
                front, split, out, last = (step.head(d) for d in (2, 1, -2, -3))
                if split:
                    act.wait_ge(S["pairs_done"], split.n * 3 + 3)
                    ge(act, S["conv_done"], split.n * 4 - 4)
                    act.activation(kv_hi[split.parity][:], pairs[:], ACT.Copy).then_inc(S["kv_hi_done"], 1)
                if last:
                    at = last.n if isinstance(last.n, int) else act.snap(last.n)
                    act.wait_ge(S["logits_done"], last.n + 1)
                    act.activation(logits[:, bass.ds(at * CI, CI)], logit_bank[:, 0:CI], ACT.Copy).then_inc(S["logits_out"], 1)
                if front:
                    act.wait_ge(S["ctx_turned"], front.n + 1)
                    ge(act, S["pairs_done"], front.n * 3)
                    src = kT_bank[:].rearrange("p (k t) -> p k t", k=KT)
                    act.activation(kT[:, :, 0:P], src, ACT.Copy).then_inc(S["kT_out"], 1)
                    act.activation(kT[:, :, P:KX], src[:, :, 0:64], ACT.Copy).then_inc(S["kT_out"], 1)
                if out:
                    ge(act, S["z_turned"], out.n)
                    norm_apply(step, 1, z_rows[:], out_rows[:], S["out_normed"])
                if split:
                    ge(act, S["mid_turned"], split.n)
                    norm_apply(step, 0, backwards(q_rows[:]), mid_rows[:].rearrange("p (k c) -> p k c", k=KT), S["mid_normed"])
                if out:
                    act.wait_ge(S["z_turned"], out.n + 1)
                    ge(act, S["z_stored"], out.n * 32)
                    ge(act, S["logits_done"], out.n)
                    act.activation(zT_hi[:], z_bank[:].rearrange("p (k t) -> p k t", k=KT), ACT.Copy).then_inc(S["z_hi_done"], 1)
                if split:
                    act.wait_ge(S["mid_turned"], split.n + 1)
                    ge(act, S["terms_done"], split.n * 4 - 4)
                    src = qT_bank[:].rearrange("p (k t) -> p k t", k=KT)
                    q = qT[split.parity]
                    act.activation(q[:, :, 0:P], src, ACT.Copy).then_inc(S["qT_out"], 1)
                    act.activation(q[:, :, P:KX], src[:, :, 0:64], ACT.Copy).then_inc(S["qT_out"], 1)

            conv_schedule(body)(act)

        @block.vector
        def _(dve):
            dve.memset(terms[0][:], 0.0).then_inc(S["terms_zeroed"], 1)
            dve.memset(terms[1][:], 0.0).then_inc(S["terms_zeroed"], 1)
            dve.wait_ge(S["gate_turned"], 1)
            src = kT_bank[:, 0:KT * CI].rearrange("p (k e) -> p k e", k=KT)
            dve.tensor_copy(gateT_hi[:], src).then_inc(S["gate_split"], 1)
            dve.wait_ge(S["gate_split"], 1)
            dve.tensor_tensor(gateT_lo[:], src, gateT_hi[:].bitcast(F32), ALU.subtract).then_inc(S["gate_split"], 1)
            dve.memset(mean_var[:], 0.0).then_inc(S["norm_cleared"], 1)
            dve.wait_ge(S["norm_cleared"], 1)
            dve.wait_ge(S["terms_zeroed"], 2)

            def norm_stats(h, w, rows):
                dve.bn_stats(stats[:, w, :], rows).then_inc(stats_chain[w], 1)

            def norm_mean_var(h, w):
                wait_apart(dve, stats_chain[w], h.n * 2 + 1, S["dve_passed"])
                dve.bn_aggr(mean_var[:, w, :], stats[:, w, :]).then_inc(stats_chain[w], 1)

            def guess(step, n):
                chain, base = S["guess_chain"], step.n * 3 + 6
                front, split, tail, out = (step.head(d) for d in (2, 1, -1, -2))
                if n == 0:
                    if split:
                        dve.wait_ge(S["mid_normed"], split.n + 1)
                    if out:
                        dve.wait_ge(S["out_normed"], out.n + 1)
                    if front:
                        dve.wait_ge(stats_chain[0], front.n * 2 + 2)
                    if tail:
                        dve.wait_ge(stats_chain[1], tail.n * 2 + 2)
                    dve.tensor_scalar(var_eps[:], mean_var[:, :, 1], EPS, None, ALU.add).then_inc(chain, 1)
                    dve.tensor_scalar(minus_mean[:], mean_var[:, :, 0], -1.0, None, ALU.mult).then_inc(chain, 1)
                elif n == 1:
                    dve.wait_ge(chain, base + 2)
                    dve.tensor_scalar(newt[:].bitcast(I32), var_eps[:].bitcast(I32), 1, None,
                                      ALU.logical_shift_right).then_inc(chain, 1)
                else:
                    dve.wait_ge(chain, base + 3)
                    dve.tensor_scalar(rstd[:].bitcast(I32), newt[:].bitcast(I32), -1.0, MAGIC,
                                      ALU.mult, ALU.add).then_inc(S["guess_done"], 1)

            def products(h, lb):
                ya, yb = y_bank[lb % 2]
                q, t = qT[h.parity][:, lb, :], terms[h.parity][:, lb, :]
                a, b = ya[:], yb[:]
                if lb == 0:
                    dve.wait_ge(S["qT_out"], h.n * 2 + 2)
                    ge(dve, S["acc_done"], h.n - 1)
                dve.wait_ge(S["conv_done"], h.n * 4 + (lb + 1))
                two = [[P, 2], [1, P]]
                for out, y, m in (
                    (view(t, 0, [[P + B, 2], [1, P]]), view(a, 0, two), view(q, 0, [[0, 2], [1, P]])),
                    (view(t, 2 * (P + B), [[P + B, 2], [1, P]]), view(b, 0, two), view(q, 0, [[0, 2], [1, P]])),
                    (view(t, 5 * P, [[1, P]]), view(a, P, [[1, P]]), view(q, B, [[1, P]])),
                    (view(t, 6 * P, two), view(b, 0, two), view(q, 2 * B, [[B, 2], [1, P]])),
                    (view(t, 4 * P + 64, [[4 * P - 64, 2], [1, 64]]), view(a, 2 * P, [[0, 2], [1, 64]]), view(q, 0, [[64, 2], [1, 64]])),
                ):
                    ins = dve.tensor_tensor(out, y, m, ALU.mult)
                ins.then_inc(S["terms_done"], 1)

            def body(step):
                front, split, conv, tail, out = (step.head(d) for d in (2, 1, 0, -1, -2))
                if conv:
                    products(conv, 0)
                if split:
                    dve.wait_ge(S["kv_hi_done"], split.n + 1)
                    dve.tensor_tensor(kv_lo[split.parity][:], pairs[:], kv_hi[split.parity][:].bitcast(F32),
                                      ALU.subtract).then_inc(S["kv_lo_done"], 1)
                if conv:
                    products(conv, 1)
                if tail:
                    dve.wait_ge(S["half_summed"], tail.n * 3 + 3)
                    ge(dve, S["acc_turned"], tail.n)
                    rows = view(terms[tail.parity][:], 0, [[TERM, KT], [1, P], [P, 6]])
                    dve.tensor_reduce(acc[:], rows, AX.X, ALU.add).then_inc(S["acc_done"], 1)
                if conv:
                    products(conv, 2)
                if tail:
                    dve.wait_ge(S["acc_turned"], tail.n + 1)
                    dve.wait_ge(S["res_loaded"], tail.n * 16 + 16)
                    ge(dve, S["out_stored"], tail.n * 16)
                    ge(dve, S["out_normed"], tail.n)
                    rows, res = (t[:].rearrange("p (k c) -> p k c", k=KT) for t in (out_rows, res_rows))
                    dve.tensor_tensor(rows, backwards(out_bank[:]), res, ALU.add).then_inc(S["out_done"], 1)
                if front:
                    dve.wait_ge(S["mid_loaded"], front.n * 16 + 16)
                    norm_stats(front, 0, mid_rows[:])
                if tail:
                    dve.wait_ge(S["out_done"], tail.n + 1)
                    norm_stats(tail, 1, out_rows[:])
                if front:
                    norm_mean_var(front, 0)
                if out:
                    dve.wait_ge(S["z_hi_done"], out.n + 1)
                    dve.tensor_tensor(zT_lo[:], z_bank[:].rearrange("p (k t) -> p k t", k=KT), zT_hi[:].bitcast(F32),
                                      ALU.subtract).then_inc(S["z_lo_done"], 1)
                if tail:
                    norm_mean_var(tail, 1)
                if front or tail:
                    guess(step, 0)
                if conv:
                    products(conv, 3)
                if front or tail:
                    guess(step, 1)
                    guess(step, 2)

            conv_schedule(body)(dve)

        @block.tensor
        def _(pe):
            pe.wait_ge(S["gate_loaded"], 16)
            pe.wait_ge(S["const_built"], 1)
            for k in range(KT):
                ins = pe.transpose(kT_bank[:, k * CI:(k + 1) * CI], gate_rows[:, k * P:(k + 1) * P], ident[0:CI, 0:CI])
            ins.then_inc(S["gate_turned"], 1)
            pe.wait_ge(S["gate_split"], 2)

            def turn(bank, rows, done):
                for k in range(KT):
                    ins = pe.transpose(bank[:, k * P:(k + 1) * P], rows[:, k * P:(k + 1) * P], ident[:])
                ins.then_inc(done, 1)

            def convolve(h, lb):
                if lb == 0:
                    pe.wait_ge(S["kv_lo_done"], h.n + 1)
                    pe.wait_ge(taps_loaded[h.parity], h.k * 32 + 32)
                ge(pe, S["terms_done"], h.n * 4 + (lb - 1))
                for mb in range(lb + 1):
                    r = slice(C - (lb - mb + 1) * P, C - (lb - mb) * P)
                    hi, lo = taps_hi[h.parity][:, r], taps_lo[h.parity][:, r]
                    for bank, (c0, c1) in zip(y_bank[lb % 2], HALVES):
                        ins = split_product(pe, bank[:, 0:c1 - c0], (hi, lo),
                                            (kv_hi[h.parity][:, mb, c0:c1], kv_lo[h.parity][:, mb, c0:c1]),
                                            mb == 0, mb == lb)
                ins.then_inc(S["conv_done"], 1)

            def body(step):
                front, split, conv, tail, out, last = (step.head(d) for d in (2, 1, 0, -1, -2, -3))
                if conv:
                    convolve(conv, 0)
                    convolve(conv, 1)
                if last:
                    pe.wait_ge(S["z_lo_done"], last.n + 1)
                    for k in range(KT):
                        ins = split_product(pe, logit_bank[:, 0:CI], (zT_hi[:, k, :], zT_lo[:, k, :]),
                                            (gateT_hi[:, k, :], gateT_lo[:, k, :]), k == 0, k == KT - 1)
                    ins.then_inc(S["logits_done"], 1)
                if front:
                    pe.wait_ge(S["ctx_loaded"], front.n * 16 + 16)
                    ge(pe, S["kT_out"], front.n * 2)
                    turn(kT_bank, ctx_rows, S["ctx_turned"])
                if conv:
                    convolve(conv, 2)
                    convolve(conv, 3)
                if out:
                    pe.wait_ge(S["out_normed"], out.n + 1)
                    ge(pe, S["logits_out"], out.n)
                    turn(z_bank, z_rows, S["z_turned"])
                if split:
                    pe.wait_ge(S["mid_normed"], split.n + 1)
                    ge(pe, S["qT_out"], split.n * 2)
                    turn(qT_bank, q_rows, S["mid_turned"])
                if tail:
                    pe.wait_ge(S["acc_done"], tail.n + 1)
                    ge(pe, S["out_done"], tail.n)
                    for k in range(KT):
                        ins = pe.transpose(out_bank[:, k * P:(k + 1) * P], acc[:, k, :], ident[:])
                    ins.then_inc(S["acc_turned"], 1)

            conv_schedule(body)(pe)


E = 8
F = 2048
FT = F // P
BLOCKS = B * T // 512
TB = 4


def experts(nc, logits, x_d, zT_d, w1, b1, w2, b2, out):
    with ExitStack() as ctx:
        def sb(name, shape, dt=F32):
            return ctx.enter_context(nc.sbuf_tensor(name, shape, dt))

        def sem(name):
            return ctx.enter_context(nc.semaphore("moe_" + name))

        w1_hi, w1_lo = sb("w1_hi", [P, FT, KT, P], F32R), sb("w1_lo", [P, FT, KT, P], F32R)
        w2_hi, w2_lo = sb("w2_hi", [P, FT, C], F32R), sb("w2_lo", [P, FT, C], F32R)
        w1_stage, w2_stage = sb("w1_stage", [P, 2, KT, P]), sb("w2_stage", [P, 2, C])
        z_hi, z_lo = ([sb(f"z_{w}{i}", [P, TB, KT, P], F32R) for i in range(2)] for w in ("hi", "lo"))
        hid = sb("hid", [P, 2, 512])
        h_hi, h_lo = sb("h_hi", [P, 2, 512], F32R), sb("h_lo", [P, 2, 512], F32R)
        x_rows = [sb(f"x_rows{i}", [P, TB, C]) for i in range(2)]
        b1_rows, b1_cols, b2_rows = sb("b1_rows", [FT, 2, P]), sb("b1_cols", [P, 2, FT]), sb("b2_rows", [P, 2, C])
        ident, ones, numbers = sb("moe_ident", [FT, FT]), sb("ones", [P, P]), sb("numbers", [P, E])
        tile_sum, total, top = sb("tile_sum", [P, E]), sb("total", [P, E]), sb("top", [P, E])
        chosen, chosen_f = sb("chosen", [P, E], U32), sb("chosen_f", [P, 2])
        is_chosen, picked = sb("is_chosen", [P, 2, E]), sb("picked", [P, CH, E])
        own, share, inv = sb("own", [P, 2, CH]), sb("share", [P, 2, CH]), sb("moe_inv", [P, CH])
        share_now = sb("share_now", [P, TB])

        psum = [ctx.enter_context(nc.psum_tensor(f"moe_bank{i}", [P, 512], F32)) for i in range(8)]
        h_bank, y_bank = psum[0:4], psum[4:8]

        ones_built = sem("ones_built")
        const_built, routed, total_done, exp_done = sem("const_built"), sem("routed"), sem("total_done"), sem("exp_done")
        b1_loaded, b2_loaded, b1_turned, b1_out = sem("b1_loaded"), sem("b2_loaded"), sem("b1_turned"), sem("b1_out")
        w_staged = [sem(f"w_staged{i}") for i in range(2)]
        w_high, w_ready = sem("w_high"), sem("w_ready")
        z_loaded = [sem(f"z_loaded{i}") for i in range(2)]
        x_loaded = [sem(f"x_loaded{i}") for i in range(2)]
        x_stored = [sem(f"x_stored{i}") for i in range(2)]
        h_done, h_bank_free = sem("h_done"), sem("h_bank_free")
        gelu_done, h_high, h_low = sem("gelu_done"), sem("h_high"), sem("h_low")
        y_part = sem("y_part")
        y_done, y_out = sem("y_done"), sem("y_out")
        share_out, x_biased = sem("share_out"), sem("x_biased")

        block = ctx.enter_context(nc.Block())

        def rounds(eng, body):
            for e in range(2):
                with eng.Fori(e * 4, e * 4 + 4) as k:
                    for parity in range(2):
                        body(e, k, parity)

        @block.sync
        def _(sp):
            def load(e, k, parity):
                it = k * 2 + parity
                at = it if isinstance(it, int) else sp.snap(it)
                blk = (at - e * BLOCKS) * TB
                blk = blk if isinstance(blk, int) else sp.snap(blk)
                ge(sp, h_done, it * FT - FT)
                for w, dst in ((0, z_hi), (1, z_lo)):
                    src = zT_d[w, bass.ds(blk, TB)].rearrange("t p k c -> p t (k c)")
                    sp.dma_start(dst[parity][:].rearrange("p t k c -> p t (k c)").bitcast(F32), src).then_inc(z_loaded[parity], 16)
                ge(sp, x_stored[parity], k * 16 if e == 0 else k * 16 * TB + (64 - 4 * 16 * TB))
                sp.dma_start(x_rows[parity][:], x_d[bass.ds(blk, TB)].rearrange("t p c -> p t c")).then_inc(x_loaded[parity], 16)

            def store(e, it, parity):
                at = it if isinstance(it, int) else sp.snap(it)
                if e == 0:
                    blk = at * TB
                    blk = blk if isinstance(blk, int) else sp.snap(blk)
                    sp.wait_ge(y_out, it * TB + (TB + 4))
                    sp.dma_start(x_d[bass.ds(blk, TB)].rearrange("t p c -> p t c"), x_rows[parity][:]).then_inc(x_stored[parity], 16)
                    return
                for t in range(TB):
                    pos = ((at - BLOCKS) * TB + t) * CI
                    pos = pos if isinstance(pos, int) else sp.snap(pos)
                    sp.wait_ge(y_out, it * TB + (t + 1 + 4))
                    dst = out[:, bass.ds(pos, CI), :].rearrange("b i c -> i b c")
                    sp.dma_start(dst, x_rows[parity][:, t, :]).then_inc(x_stored[parity], 16)

            def pair(e, k, e_before):
                load(e, k, 0)
                if e_before is not None:
                    store(e_before, k * 2 - 1, 1)
                load(e, k, 1)
                store(e, k * 2, 0)

            sp.wait_ge(routed, 4)
            for n in range(2):
                e = sp.value_load(chosen[0:1, n:n + 1], min_val=0, max_val=E - 1)
                sp.dma_start(b1_rows[:, n, :], b1[e, :].rearrange("(j p) -> j p", p=P)).then_inc(b1_loaded, 16)
                sp.dma_start(b2_rows[:, n, :], b2[e, :].partition_broadcast(P)).then_inc(b2_loaded, 16)
            pair(0, 0, None)
            with sp.Fori(1, 4) as k:
                pair(0, k, 0)
            pair(1, 4, 0)
            with sp.Fori(5, 8) as k:
                pair(1, k, 1)
            store(1, 2 * BLOCKS - 1, 1)
            for parity in range(2):
                sp.wait_ge(x_stored[parity], 4 * 16 + 4 * 16 * TB)

        @block.gpsimd
        def _(pool):
            pool.memset(ident[:], 0.0).then_inc(const_built, 1)
            pool.wait_ge(const_built, 1)
            pool.affine_select(out=ident[:], in_=ident[:], compare_op=ALU.not_equal, fill=1.0, base=0,
                               pattern=[[-1, FT]], channel_multiplier=1).then_inc(const_built, 1)
            pool.wait_ge(routed, 4)
            expert = [pool.value_load(chosen[0:1, n:n + 1], min_val=0, max_val=E - 1) for n in range(2)]

            def stage(n):
                e, j = expert[n // FT], n % FT
                if n >= 2:
                    pool.wait_ge(w_ready, n - 1)
                src = w1[e, :, j * P:(j + 1) * P].rearrange("(k p) f -> p k f", p=P)
                pool.dma_start(w1_stage[:, n % 2], src).then_inc(w_staged[n % 2], 16)
                pool.dma_start(w2_stage[:, n % 2, :], w2[e, j * P:(j + 1) * P, :]).then_inc(w_staged[n % 2], 16)

            stage(0)
            stage(1)
            for n in range(2 * FT):
                j = n % FT
                pool.wait_ge(w_staged[n % 2], 32 * (n // 2 + 1))
                if n >= FT:
                    pool.wait_ge(y_part, FT * (BLOCKS - 1) + j + 1 + 2)
                pool.tensor_copy(w1_hi[:, j], w1_stage[:, n % 2]).then_inc(w_high, 1)
                pool.tensor_copy(w2_hi[:, j], w2_stage[:, n % 2]).then_inc(w_high, 1)
                pool.wait_ge(w_high, 3 * n + 2)
                pool.tensor_tensor(w1_lo[:, j], w1_stage[:, n % 2], w1_hi[:, j].bitcast(F32), ALU.subtract).then_inc(w_high, 1)
                pool.wait_ge(w_high, 3 * n + 3)
                pool.tensor_tensor(w2_lo[:, j], w2_stage[:, n % 2], w2_hi[:, j].bitcast(F32), ALU.subtract).then_inc(w_ready, 1)
                if n + 2 < 2 * FT:
                    stage(n + 2)

        @block.scalar
        def _(act):
            act.sem_inc(h_bank_free, 4)
            act.wait_ge(routed, ROUTED_EXP)
            act.activation(own[:], own[:], ACT.Exp).then_inc(exp_done, 1)
            act.wait_ge(b1_out, 1)

            def body(e, k, parity):
                it = k * 2 + parity
                for j in range(FT):
                    act.wait_ge(h_done, it * FT + (j + 1))
                    act.wait_ge(h_low, it * FT + (j + 1))
                    act.activation(hid[:, j % 2, :], h_bank[j % 4][:], ACT.Gelu_apprx_tanh,
                                   bias=b1_cols[:, e, j:j + 1]).then_inc(h_bank_free, 1)
                    act.wait_ge(h_bank_free, it * FT + (j + 1 + 4))
                    act.wait_ge(y_part, it * FT + (j + 1))
                    act.activation(h_hi[:, j % 2, :], hid[:, j % 2, :], ACT.Copy).then_inc(h_high, 1)

            rounds(act, body)

        @block.vector
        def _(dve):
            dve.sem_inc(h_low, 2)
            dve.sem_inc(y_out, 4)
            for n in range(E):
                dve.memset(numbers[:, n:n + 1], float(n)).then_inc(ones_built, 1)
            dve.memset(ones[:], 1.0).then_inc(ones_built, 1)
            dve.tensor_reduce(tile_sum[:], view(logits[:], 0, [[1, E], [E, CH]]), AX.X, ALU.add).then_inc(routed, 1)
            dve.wait_ge(total_done, 1)
            dve.tensor_copy(total[:], h_bank[0][:, 0:E]).then_inc(routed, 1)
            dve.wait_ge(routed, 2)
            dve.max(top[:], total[:]).then_inc(routed, 1)
            dve.wait_ge(routed, 3)
            dve.max_index(chosen[:], top[:], total[:]).then_inc(routed, 1)
            dve.wait_ge(routed, 4)
            dve.tensor_copy(chosen_f[:], chosen[:, 0:2]).then_inc(routed, 1)
            dve.wait_ge(routed, 5)
            dve.wait_ge(ones_built, E + 1)
            for n in range(2):
                dve.tensor_scalar(is_chosen[:, n, :], numbers[:], chosen_f[:, n:n + 1], None, ALU.is_equal).then_inc(routed, 1)
            for n in range(2):
                dve.wait_ge(routed, 7 + 2 * n)
                dve.tensor_tensor(picked[:], logits[:].rearrange("p (t e) -> p t e", e=E),
                                  view(is_chosen[:], n * E, [[0, CH], [1, E]]), ALU.mult).then_inc(routed, 1)
                dve.wait_ge(routed, 8 + 2 * n)
                dve.tensor_reduce(own[:, n, :], picked[:], AX.X, ALU.add).then_inc(routed, 1)
            dve.wait_ge(routed, 11)
            dve.tensor_tensor(inv[:], own[:, 0, :], own[:, 1, :], ALU.max).then_inc(routed, 1)
            dve.wait_ge(routed, 12)
            dve.tensor_tensor(own[:], own[:], view(inv[:], 0, [[0, 2], [1, CH]]), ALU.subtract).then_inc(routed, 1)
            dve.wait_ge(exp_done, 1)
            dve.tensor_tensor(inv[:], own[:, 0, :], own[:, 1, :], ALU.add).then_inc(routed, 1)
            dve.wait_ge(routed, 14)
            dve.reciprocal(inv[:], inv[:]).then_inc(routed, 1)
            dve.wait_ge(routed, 15)
            dve.tensor_tensor(share[:], own[:], view(inv[:], 0, [[0, 2], [1, CH]]), ALU.mult).then_inc(routed, 1)
            dve.wait_ge(b1_turned, 1)
            dve.tensor_copy(b1_cols[:], h_bank[1][:, 0:2 * FT].rearrange("p (n j) -> p n j", n=2)).then_inc(b1_out, 1)
            dve.wait_ge(routed, 16)
            dve.wait_ge(b2_loaded, 32)

            def body(e, k, parity):
                it = k * 2 + parity
                for j in range(FT):
                    dve.wait_ge(h_high, it * FT + (j + 1))
                    dve.wait_ge(y_part, it * FT + (j + 1))
                    dve.tensor_tensor(h_lo[:, j % 2, :], hid[:, j % 2, :], h_hi[:, j % 2, :].bitcast(F32),
                                      ALU.subtract).then_inc(h_low, 1)
                    if j == 3:
                        at = dve.snap(it * TB)
                        dve.tensor_copy(share_now[:], share[:].rearrange("p n t -> p (n t)")[:, bass.ds(at, TB)]).then_inc(share_out, 1)
                    if j == 4:
                        dve.wait_ge(x_loaded[parity], k * 16 + 16)
                        dve.wait_ge(share_out, it + 1)
                        for t in range(TB):
                            dve.scalar_tensor_tensor(out=x_rows[parity][:, t, :], in0=b2_rows[:, e, :], scalar=share_now[:, t:t + 1],
                                                     in1=x_rows[parity][:, t, :], op0=ALU.mult, op1=ALU.add).then_inc(x_biased, 1)
                for t in range(TB):
                    if t < TB - 1:
                        dve.wait_ge(y_done, it * (TB - 1) + (t + 1))
                    else:
                        dve.wait_ge(y_part, it * FT + (FT + 2))
                    dve.wait_ge(x_biased, it * TB + (t + 1))
                    dve.scalar_tensor_tensor(out=x_rows[parity][:, t, :], in0=y_bank[t][:], scalar=share_now[:, t:t + 1],
                                             in1=x_rows[parity][:, t, :], op0=ALU.mult, op1=ALU.add).then_inc(y_out, 1)

            rounds(dve, body)

        @block.tensor
        def _(pe):
            pe.sem_inc(y_part, 2)
            pe.wait_ge(const_built, 2)
            pe.wait_ge(ones_built, E + 1)
            pe.wait_ge(routed, 1)
            pe.matmul(h_bank[0][:, 0:E], ones[:], tile_sum[:], start=True, stop=True).then_inc(total_done, 1)
            pe.wait_ge(b1_loaded, 32)
            for n in range(2):
                ins = pe.transpose(h_bank[1][:, n * FT:(n + 1) * FT], b1_rows[:, n, :], ident[:])
            ins.then_inc(b1_turned, 1)
            pe.wait_ge(b1_out, 1)
            pe.wait_ge(routed, 2)

            with pe.Fori(0, 2) as e, pe.Fori(0, 4) as b:
                for parity in range(2):
                    it = pe.snap(e * 8 + b * 2 + parity)

                    def hidden(j):
                        if parity == 0:
                            pe.wait_ge(w_ready, e * FT + (j + 1))
                        pe.wait_ge(h_bank_free, it * FT + (j + 1))
                        for k in range(KT):
                            ins = split_product(pe, h_bank[j % 4][:], (w1_hi[:, j, k, :], w1_lo[:, j, k, :]),
                                                (z_hi[parity][:, :, k, :], z_lo[parity][:, :, k, :]), k == 0, k == KT - 1)
                        ins.then_inc(h_done, 1)

                    def output(j):
                        pe.wait_ge(h_low, it * FT + (j + 1 + 2))
                        for t in range(TB):
                            if j == 0:
                                pe.wait_ge(y_out, it * TB + (t + 1))
                            rows = slice(t * P, (t + 1) * P)
                            ins = split_product(pe, y_bank[t][:], (h_hi[:, j % 2, rows], h_lo[:, j % 2, rows]),
                                                (w2_hi[:, j, :], w2_lo[:, j, :]), j == 0, j == FT - 1)
                            if j == FT - 1 and t < TB - 1:
                                ins.then_inc(y_done, 1)
                        ins.then_inc(y_part, 1)

                    pe.wait_ge(z_loaded[parity], (e * 4 + b) * 32 + 32)
                    hidden(0)
                    for j in range(FT):
                        if j + 1 < FT:
                            hidden(j + 1)
                        output(j)


ROUTED_EXP = 13


_INS = {"x": "x", "ctx": "ctx_2048", "wqkv": "L0_attn_Wqkv", "bqkv": "L0_attn_bqkv", "wo": "L0_attn_Wo", "bo": "L0_attn_bo",
        "taps": "L0_xattn_ssm_kernel", "D": "L0_xattn_D", "gate": "L0_ffn_gate_w", "w1": "L0_ffn_w1", "b1": "L0_ffn_b1",
        "w2": "L0_ffn_w2", "b2": "L0_ffn_b2"}


def decoder_layer(nc, a, out):
    x_mid = nc.dram_tensor("x_mid", (T, B, C), F32, kind="Internal").ap()
    taps_d = nc.dram_tensor("taps_d", (2, CH, TAPW), F32, kind="Internal").ap()
    x_d = nc.dram_tensor("x_d", (CH, P, C), F32, kind="Internal").ap()
    zT_d = nc.dram_tensor("zT_d", (2, CH, P, KT, P), F32, kind="Internal").ap()
    attention(nc, a["x"], a["wqkv"], a["bqkv"], a["wo"], a["bo"], a["cos"], a["sin"], a["taps"], a["D"], x_mid, taps_d)
    with nc.sbuf_tensor("logits", [P, CH * CI], F32) as logits:
        convolution(nc, x_mid, a["ctx"], taps_d, a["gate"], logits, x_d, zT_d)
        experts(nc, logits, x_d, zT_d, a["w1"], a["b1"], a["w2"], a["b2"], out)


def kernel(**inputs):
    import numpy as np
    import concourse.bacc as bacc
    from concourse.bass_utils import run_bass_kernel_spmd as run

    nc = bacc.Bacc("TRN2", target_bir_lowering=False, num_devices=1)
    cos_t, sin_t = rotary_tables()
    given = {short: np.asarray(inputs[name]) for short, name in _INS.items()}
    given.update(cos=cos_t, sin=sin_t)
    arrays, args = {}, {}
    for name, value in given.items():
        arrays[f"in_{name}"] = np.ascontiguousarray(value)
        args[name] = nc.dram_tensor(f"in_{name}", arrays[f"in_{name}"].shape, F32, kind="ExternalInput").ap()
    out = nc.dram_tensor("out_0", (B, T, C), F32, kind="ExternalOutput").ap()
    decoder_layer(nc, args, out)
    return run(nc, [arrays], core_ids=[0]).results[0]["out_0"]
```

```python
from contextlib import ExitStack

import concourse.bass as bass
from concourse import mybir

F32 = mybir.dt.float32
F32R = mybir.dt.float32r
BF16 = mybir.dt.bfloat16
I32 = mybir.dt.int32
U32 = mybir.dt.uint32
ALU = mybir.AluOpType
ACT = mybir.ActivationFunctionType
AX = mybir.AxisListType

P = 128
B, T, C = 16, 256, 512
KT = C // P
NT = T // P
NHEAD, HD = 16, 32
GH = P // HD
SCALE = float(HD) ** -0.5
EPS = 1e-5
MAGIC = float(0x5F3759DF)
NEWTON, ACT_NEWTON = 12, 15
MASKED = -1.0e30


def view(ap, offset, dims):
    return bass.AP(tensor=ap.tensor, offset=ap.offset + offset, ap=[list(ap.ap[0])] + [list(d) for d in dims])


def ge(eng, sem, count):
    if isinstance(count, int) and count <= 0:
        return
    eng.wait_ge(sem, count)


def wait_apart(eng, sem, count, passed):
    eng.wait_ge(sem, count)
    if not isinstance(count, int):
        eng.sem_inc(passed, 1)


def newton_rsqrt(pool, sem, passed, base, y, v, a):
    n = 0
    for _ in range(3):
        for op in range(4):
            if op == 0:
                ins = pool.tensor_tensor(a, y, y, ALU.mult)
            elif op == 1:
                ins = pool.tensor_tensor(a, a, v, ALU.mult)
            elif op == 2:
                ins = pool.tensor_scalar(a, a, -0.5, 1.5, ALU.mult, ALU.add)
            else:
                ins = pool.tensor_tensor(y, y, a, ALU.mult)
            n += 1
            ins.then_inc(sem, 1)
            if n < NEWTON:
                wait_apart(pool, sem, base + n, passed)


CH, CI = 32, 8
TAPW = C + P
KX = CI * B + 64
PAIR = 576
HALVES = ((0, 320), (320, 576))
POOL_LOW = 2
TERM = 9 * P
CONST_LOADS = 3 + 3 * KT


class Batch:

    def __init__(self, k, parity):
        self.k, self.parity = k, parity
        self.n = k * 2 + parity


def batches(n):
    return [Batch(b // 2, b % 2) if 0 <= b < B else None for b in (n + 1, n, n - 1, n - 2)]


def schedule(eng, body):
    for n in (0, 1, 2, 3):
        body(*batches(n))
    with eng.Fori(1, 6) as i:
        body(Batch(i + 1, 1), Batch(i + 1, 0), Batch(i, 1), Batch(i, 0))
        body(Batch(i + 2, 0), Batch(i + 1, 1), Batch(i + 1, 0), Batch(i, 1))
    for n in (14, 15, 16, 17):
        body(*batches(n))


def attention(nc, x, Wqkv, bqkv, Wo, bo, cos_t, sin_t, ssm_kernel, ssm_D, x_mid, taps_d):
    with ExitStack() as ctx:
        def sb(name, shape, dt=F32):
            return ctx.enter_context(nc.sbuf_tensor(name, shape, dt))

        def sem(name):
            return ctx.enter_context(nc.semaphore(name))

        w_stage = sb("w_stage", [P, 4, C])
        y_rows, x_res = w_stage[:, 0:NT, :], w_stage[:, NT:2 * NT, :]
        wT_hi, wT_lo = sb("wT_hi", [P, KT, 3 * C], F32R), sb("wT_lo", [P, KT, 3 * C], F32R)
        woT_hi, woT_lo = sb("woT_hi", [P, KT, C], F32R), sb("woT_lo", [P, KT, C], F32R)
        bias_qk, bias_v, bo_rows = sb("bias_qk", [P, 8]), sb("bias_v", [P, KT]), sb("bo_rows", [P, C])
        cos_s, sin_s = sb("cos_s", [P, T]), sb("sin_s", [P, T])
        ident, ident_b = sb("ident", [P, P]), sb("ident_b", [P, P], BF16)
        mask_b = sb("mask_b", [P, P], BF16)
        x_in = sb("x_in", [P, NT, C])
        stats, mean_var = sb("stats", [P, NT, 6]), sb("mean_var", [P, NT, 2])
        var_eps, rstd, newt = sb("var_eps", [P, NT]), sb("rstd", [P, NT]), sb("newt", [P, NT])
        xT_hi, xT_lo = sb("xT_hi", [P, KT, T], F32R), sb("xT_lo", [P, KT, T], F32R)
        q_rot, q_sin = sb("q_rot", [P, 2, 2, T]), sb("q_sin", [P, 2, 2, T])
        r_hi, r_lo = sb("r_hi", [P, 2, 2 * T], F32R), sb("r_lo", [P, 2, 2 * T], F32R)
        q_stack = [sb(f"q_stack{i}", [P, NHEAD, T], F32R) for i in range(2)]
        k_stack = [sb(f"k_stack{i}", [P, NHEAD, T], F32R) for i in range(2)]
        v_split = [sb(f"v_split{i}", [P, NT, NHEAD, 2, HD], F32R) for i in range(2)]
        row_max, neg_max = sb("row_max", [P, 2, 4]), sb("neg_max", [P, 12, 4])
        row_sum, inv_sum = sb("row_sum", [P, NT, NHEAD]), sb("inv_sum", [P, NT, NHEAD])
        probs = sb("probs", [P, 2, 512])
        p_hi, p_lo = sb("p_hi", [P, 2, 512], F32R), sb("p_lo", [P, 2, 512], F32R)
        y_cross, y_sum = sb("y_cross", [P, NT, GH, HD]), sb("y_sum", [P, NT, GH, HD])
        yT_hi, yT_lo = sb("yT_hi", [P, KT, T], F32R), sb("yT_lo", [P, KT, T], F32R)

        psum = [ctx.enter_context(nc.psum_tensor(f"attn_bank{i}", [P, 512], F32)) for i in range(8)]
        g_bank, s_bank, t_bank, y_bank = psum[0:3], psum[3:5], psum[5:7], psum[7]

        w_loaded = [sem(f"w_loaded{i}") for i in range(4)]
        const_loaded, x_loaded, res_loaded = sem("const_loaded"), sem("x_loaded"), sem("res_loaded")
        taps_zeroed, taps_loaded, taps_built, taps_stored = (sem(nm) for nm in ("taps_zeroed", "taps_loaded", "taps_built", "taps_stored"))
        stacked = [[sem(f"stacked{p_}_{i}") for i in range(4)] for p_ in range(2)]
        x_mid_stored = sem("x_mid_stored")
        zeroed, const_built = sem("zeroed"), sem("const_built")
        w_turned, w_hi_done, w_lo_done = sem("w_turned"), sem("w_hi_done"), sem("w_lo_done")
        stats_chain, guess_done, newton_done, xn_done = sem("stats_chain"), sem("guess_done"), sem("newton_done"), sem("xn_done")
        dve_passed, pool_passed = sem("dve_passed"), sem("pool_passed")
        xt_done, xt_hi_done, xt_lo_done = sem("xt_done"), sem("xt_hi_done"), sem("xt_lo_done")
        qk_done, qk_out = sem("qk_done"), sem("qk_out")
        cos_done, sin_done, rot_done, r_hi_done, r_lo_done = (sem(nm) for nm in ("cos_done", "sin_done", "rot_done", "r_hi_done", "r_lo_done"))
        v_done, v_hi_done, v_lo_done = sem("v_done"), sem("v_hi_done"), sem("v_lo_done")
        yt_done, yt_hi_done, yt_lo_done = sem("yt_done"), sem("yt_hi_done"), sem("yt_lo_done")
        wo_done, res_biased, x_mid_done = sem("wo_done"), sem("res_biased"), sem("x_mid_done")
        scores_done, max_done, neg_done, exp_done = sem("scores_done"), sem("max_done"), sem("neg_done"), sem("exp_done")
        pt_done, p_hi_done, p_lo_done, pv_done = sem("pt_done"), sem("p_hi_done"), sem("p_lo_done"), sem("pv_done")
        cross_out, inv_done, ysum_done, y_done = sem("cross_out"), sem("inv_done"), sem("ysum_done"), sem("y_done")

        def unit(u):
            g, kind = divmod(u, 3)
            heads = range(4) if kind == 0 else range(2 * kind - 2, 2 * kind)
            return g, int(kind > 0), list(heads), P if kind == 0 else T

        def place(g, r):
            return r * 4 + g

        taps = q_rot[0:CH, :, :, :].rearrange("p a b c -> p (a b c)")[:, 0:C]
        taps_backwards = view(taps, C - 1, [[-1, C]])
        taps_D = q_sin[0:CH, 0, 0, 0:1]
        taps_hi = r_hi[0:CH].rearrange("p a b -> p (a b)")[:, 0:TAPW]
        taps_lo = r_lo[0:CH].rearrange("p a b -> p (a b)")[:, 0:TAPW]

        QK_TILES = ((0, 1), (4, 5), (2, 3), (6, 7))
        AFTER_QK = (4, 6, 8, 9)
        ROTATED = (6, 8, 10, 11)
        xm = x_mid

        block = ctx.enter_context(nc.Block())

        @block.sync
        def _(sp):
            sp.dma_start(x_in[:], x[0].rearrange("(t p) c -> p t c", p=P)).then_inc(x_loaded, 16)
            for w in range(16):
                if w >= 4:
                    sp.wait_ge(w_turned, w - 3)
                src = Wqkv[w * P:(w + 1) * P, :] if w < 12 else Wo[(w - 12) * P:(w - 11) * P, :]
                sp.dma_start(w_stage[:, w % 4, :], src).then_inc(w_loaded[w % 4], 16)
                if w == 3:
                    sp.dma_start(taps_D, ssm_D.rearrange("(h o) -> h o", o=1)).then_inc(taps_loaded, 16)
                    sp.dma_start(taps, ssm_kernel).then_inc(taps_loaded, 16)
            sp.wait_ge(taps_built, 3)
            sp.wait_ge(taps_zeroed, 2)
            sp.dma_start(taps_d[0], taps_hi.bitcast(F32)).then_inc(taps_stored, 16)
            sp.dma_start(taps_d[1], taps_lo.bitcast(F32)).then_inc(taps_stored, 16)

            def body(b0, b1, b2, b3):
                if b3:
                    row3 = sp.snap(b3.n)
                    ge(sp, x_mid_stored, b3.n * 32)
                    sp.dma_start(x_res, x[row3].rearrange("(t p) c -> p t c", p=P)).then_inc(res_loaded, 16)
                if b0:
                    row = sp.snap(b0.n)
                    sp.wait_ge(xt_done, b0.n * 2)
                    sp.dma_start(x_in[:], x[row].rearrange("(t p) c -> p t c", p=P)).then_inc(x_loaded, 16)
                if b1:
                    ge(sp, scores_done, b1.n * 12 - 12)
                    for i in range(4):
                        stack, low, high = (q_stack, 64, (0, 32)) if i % 2 == 0 else (k_stack, 32, (0, 64))
                        g0 = 2 * (i // 2)
                        sp.wait_ge(r_hi_done, b1.n * 4 + (i + 1))
                        sp.wait_ge(r_lo_done, b1.n * 4 + (i + 1))
                        for at, src in ((high[0], r_hi), (high[1], r_hi), (low, r_lo)):
                            dst = stack[b1.parity][at:at + HD].rearrange("d (r g) t -> d r g t", r=GH)[:, :, g0:g0 + 2, :]
                            sp.dma_start(dst.bitcast(F32), src[:, i % 2, :].bitcast(F32)).then_inc(stacked[b1.parity][i], 16)
                if b3:
                    for t in range(NT):
                        sp.wait_ge(x_mid_done, b3.n * 2 + (t + 1))
                        sp.dma_start(xm[t * P:(t + 1) * P, row3, :], x_res[:, t, :]).then_inc(x_mid_stored, 16)

            schedule(sp, body)
            sp.wait_ge(x_mid_stored, 32 * B)

        @block.gpsimd
        def _(pool):
            pool.memset(taps_hi[:, C:TAPW].bitcast(F32), 0.0).then_inc(taps_zeroed, 1)
            pool.memset(taps_lo[:, C:TAPW].bitcast(F32), 0.0).then_inc(taps_zeroed, 1)
            pool.memset(ident[:], 0.0).then_inc(zeroed, 1)
            pool.memset(mask_b[:], 0.0).then_inc(zeroed, 1)
            pool.wait_ge(zeroed, 2)
            pool.affine_select(out=ident[:], in_=ident[:], compare_op=ALU.not_equal, fill=1.0, base=0,
                               pattern=[[-1, P]], channel_multiplier=1).then_inc(zeroed, 1)
            pool.affine_select(out=mask_b[:], in_=mask_b[:], compare_op=ALU.is_ge, fill=MASKED, base=0,
                               pattern=[[-1, P]], channel_multiplier=1).then_inc(const_built, 1)
            pool.wait_ge(zeroed, 3)
            pool.tensor_copy(ident_b[:], ident[:]).then_inc(const_built, 1)

            def newton(b):
                pool.wait_ge(guess_done, b.n + 1)
                newton_rsqrt(pool, newton_done, pool_passed, b.n * NEWTON, rstd[:], var_eps[:], newt[:])

            newton(Batch(0, 0))
            pool.wait_ge(taps_loaded, 32)
            pool.tensor_tensor(taps[:, 0:1], taps[:, 0:1], taps_D, ALU.add).then_inc(taps_built, 1)
            pool.wait_ge(taps_built, 1)
            pool.tensor_copy(taps_hi[:, 0:C], taps_backwards).then_inc(taps_built, 1)
            pool.wait_ge(taps_built, 2)
            pool.tensor_tensor(taps_lo[:, 0:C], taps_backwards, taps_hi[:, 0:C].bitcast(F32), ALU.subtract).then_inc(taps_built, 1)
            pool.wait_ge(const_loaded, 16 * CONST_LOADS)

            def scale_y(b, g):
                pool.wait_ge(ysum_done, b.n * 4 + (g + 1))
                if g == 0:
                    ge(pool, yt_done, b.n * 2)
                out = y_rows.rearrange("p t (h d) -> p t h d", d=HD)[:, :, 4 * g:4 * g + 4, :]
                inv = view(inv_sum[:], 4 * g, [[NHEAD, NT], [1, GH], [0, HD]])
                pool.tensor_tensor(out, y_sum[:], inv, ALU.mult).then_inc(y_done, 1)

            def body(b0, b1, b2, b3):
                for s in range(12):
                    if s == 3 and b3:
                        pool.wait_ge(res_loaded, b3.n * 16 + 16)
                        bo_both = view(bo_rows[:], 0, [[0, NT], [1, C]])
                        pool.tensor_tensor(x_res, x_res, bo_both, ALU.add).then_inc(res_biased, 1)
                    if s == 2 and b3:
                        scale_y(b3, 3)
                    if s in (5, 8, 11) and b2:
                        scale_y(b2, (s - 5) // 3)
                    if s in AFTER_QK and b1:
                        i = AFTER_QK.index(s)
                        pool.wait_ge(qk_out, b1.n * 4 + (i + 1))
                        pool.wait_ge(sin_done, b1.n * 4 + (i + 1))
                        cos2 = view(cos_s[:], 0, [[0, 2], [1, T]])
                        pool.tensor_tensor(q_rot[:, i % 2], q_rot[:, i % 2], cos2, ALU.mult).then_inc(cos_done, 1)
                        pool.wait_ge(cos_done, b1.n * 4 + (i + 1))
                        pool.tensor_tensor(q_rot[:, i % 2], q_rot[:, i % 2], q_sin[:, i % 2], ALU.add).then_inc(rot_done, 1)
                    if s == 4 and b0:
                        newton(b0)

            schedule(pool, body)

        @block.scalar
        def _(act):
            for d in range(2 * KT):
                src = bqkv[d * P:(d + 1) * P].rearrange("(r d o) -> d r o", r=GH, o=1)
                act.dma_start(bias_qk[:, d:d + 1], src, allow_slow_non_contiguous=True).then_inc(const_loaded, 16)
            for k in range(KT):
                src = bqkv[2 * C + k * P:2 * C + (k + 1) * P].rearrange("(p o) -> p o", o=1)
                act.dma_start(bias_v[:, k:k + 1], src).then_inc(const_loaded, 16)
            act.dma_start(cos_s[:], cos_t).then_inc(const_loaded, 16)
            act.dma_start(sin_s[:], sin_t).then_inc(const_loaded, 16)
            act.dma_start(bo_rows[:], bo.partition_broadcast(P)).then_inc(const_loaded, 16)
            for w in range(16):
                act.wait_ge(w_turned, w + 1)
                dst, src = weight_dst(wT_hi, woT_hi, psum, w)
                act.activation(dst, src, ACT.Copy).then_inc(w_hi_done, 1)
            act.wait_ge(const_loaded, 16 * CONST_LOADS)
            act.wait_ge(taps_stored, 32)

            def exps(b, u):
                g, qt, heads, nk = unit(u)
                act.wait_ge(neg_done, b.n * 12 + (u + 1))
                ge(act, pt_done, b.n * 12 + (u - 1))
                if u % 3 == 0:
                    ge(act, inv_done, b.n * 4 + (g - 3))
                for j, r in enumerate(heads):
                    cols = slice(j * nk, (j + 1) * nk)
                    ins = act.activation(probs[:, u % 2, cols], s_bank[u % 2][:, cols], ACT.Exp,
                                         bias=neg_max[:, u, j:j + 1], scale=SCALE,
                                         accum_out=row_sum[:, qt, 4 * g + r:4 * g + r + 1])
                ins.then_inc(exp_done, 1)

            def p_high(b, u):
                act.wait_ge(pt_done, b.n * 12 + (u + 1))
                ge(act, pv_done, b.n * 12 + (u - 1))
                act.activation(p_hi[:, u % 2, :], t_bank[u % 2][:], ACT.Copy).then_inc(p_hi_done, 1)

            def cross(b, g):
                act.wait_ge(pv_done, b.n * 12 + (3 * g + 3))
                ge(act, ysum_done, b.n * 4 + g)
                src = y_bank[:].rearrange("p (t h w d) -> p t h w d", t=NT, h=GH, w=2)[:, :, :, 1, :]
                act.activation(y_cross[:], src, ACT.Copy).then_inc(cross_out, 1)

            def body(b0, b1, b2, b3):
                for s in range(12):
                    bank = g_bank[(s - 1) % 3]
                    if s in ROTATED and b1:
                        i = ROTATED.index(s)
                        act.wait_ge(rot_done, b1.n * 4 + (i + 1))
                        if i < 2:
                            ge(act, stacked[1 - b1.parity][i + 2], (b1.k + b1.parity) * 48)
                        else:
                            act.wait_ge(stacked[b1.parity][i - 2], b1.k * 48 + 48)
                        act.activation(r_hi[:, i % 2, :], q_rot[:, i % 2].rearrange("p m t -> p (m t)"),
                                       ACT.Copy).then_inc(r_hi_done, 1)
                    if s in (1, 2) and b1:
                        t = s - 1
                        act.wait_ge(xt_done, b1.n * 2 + (t + 1))
                        ge(act, v_done, b1.n * 2)
                        act.activation(xT_hi[:, :, t * P:(t + 1) * P], bank[:].rearrange("p (k t) -> p k t", k=KT),
                                       ACT.Copy).then_inc(xt_hi_done, 1)
                    if s in AFTER_QK and b1:
                        i = AFTER_QK.index(s)
                        act.wait_ge(qk_done, b1.n * 4 + (i + 1))
                        ge(act, r_lo_done, b1.n * 4 + (i - 1))
                        for m, tile in enumerate(QK_TILES[i]):
                            ins = act.activation(q_rot[:, i % 2, m, :], bank[:, m * T:(m + 1) * T], ACT.Identity,
                                                 bias=bias_qk[:, tile:tile + 1])
                        ins.then_inc(qk_out, 1)
                    if s in (5, 7) and b3:
                        t = (s - 5) // 2
                        act.wait_ge(yt_done, b3.n * 2 + (t + 1))
                        ge(act, wo_done, b3.n * 2)
                        for k in range(KT):
                            ins = act.activation(yT_hi[:, k, t * P:(t + 1) * P], bank[:, k * P:(k + 1) * P],
                                                 ACT.Identity, bias=bias_v[:, k:k + 1])
                        ins.then_inc(yt_hi_done, 1)
                    if s in (3, 10) and b1:
                        t = (3, 10).index(s)
                        act.wait_ge(v_done, b1.n * 2 + (t + 1))
                        if t == 0:
                            ge(act, pv_done, b1.n * 12 - 12)
                        act.activation(v_split[b1.parity][:, t, :, 0, :], bank[:].rearrange("p (h d) -> p h d", d=HD),
                                       ACT.Copy).then_inc(v_hi_done, 1)
                    if s == 2 and b3:
                        cross(b3, 3)
                    if s in (5, 8, 11) and b2:
                        cross(b2, (s - 5) // 3)
                    if s == 0 and b3:
                        p_high(b3, 11)
                    if s >= 1 and b2:
                        p_high(b2, s - 1)
                    if b2:
                        exps(b2, s)

            schedule(act, body)

        @block.vector
        def _(dve):
            def norm_stats(b):
                dve.wait_ge(x_loaded, b.n * 16 + 16)
                for t in range(NT):
                    dve.bn_stats(stats[:, t, :], x_in[:, t, :]).then_inc(stats_chain, 1)
                for t in range(NT):
                    wait_apart(dve, stats_chain, b.n * 6 + (t + 1), dve_passed)
                    dve.bn_aggr(mean_var[:, t, :], stats[:, t, :]).then_inc(stats_chain, 1)
                dve.wait_ge(stats_chain, b.n * 6 + 4)
                dve.tensor_scalar(var_eps[:], mean_var[:, :, 1], EPS, None, ALU.add).then_inc(stats_chain, 1)
                dve.wait_ge(stats_chain, b.n * 6 + 5)
                dve.tensor_scalar(newt[:].bitcast(I32), var_eps[:].bitcast(I32), 1, None,
                                  ALU.logical_shift_right).then_inc(stats_chain, 1)
                dve.wait_ge(stats_chain, b.n * 6 + 6)
                dve.tensor_scalar(rstd[:].bitcast(I32), newt[:].bitcast(I32), -1.0, MAGIC,
                                  ALU.mult, ALU.add).then_inc(guess_done, 1)

            def norm_apply(b):
                dve.wait_ge(newton_done, b.n * NEWTON + NEWTON)
                for t in range(NT):
                    dve.tensor_scalar(x_in[:, t, :], x_in[:, t, :], mean_var[:, t, 0:1], rstd[:, t:t + 1],
                                      ALU.subtract, ALU.mult).then_inc(xn_done, 1)

            norm_stats(Batch(0, 0))
            for w in range(16):
                dve.wait_ge(w_hi_done, w + 1)
                hi, src = weight_dst(wT_hi, woT_hi, psum, w)
                lo, _ = weight_dst(wT_lo, woT_lo, psum, w)
                dve.tensor_tensor(lo, src, hi.bitcast(F32), ALU.subtract).then_inc(w_lo_done, 1)
                if w == 2:
                    norm_apply(Batch(0, 0))
            dve.wait_ge(const_loaded, 16 * CONST_LOADS)
            dve.wait_ge(taps_stored, 32)

            def maxima(b, u):
                g, qt, heads, nk = unit(u)
                nh = len(heads)
                dve.wait_ge(scores_done, b.n * 12 + (u + 1))
                dve.tensor_reduce(row_max[:, u % 2, 0:nh], s_bank[u % 2][:].rearrange("p (h k) -> p h k", h=nh),
                                  AX.X, ALU.max).then_inc(max_done, 1)
                dve.wait_ge(max_done, b.n * 12 + (u + 1))
                dve.tensor_scalar(neg_max[:, u, 0:nh], row_max[:, u % 2, 0:nh], -SCALE, None, ALU.mult).then_inc(neg_done, 1)

            def p_low(b, u):
                dve.wait_ge(p_hi_done, b.n * 12 + (u + 1))
                ge(dve, pv_done, b.n * 12 + (u - 1))
                dve.tensor_tensor(p_lo[:, u % 2, :], t_bank[u % 2][:], p_hi[:, u % 2, :].bitcast(F32),
                                  ALU.subtract).then_inc(p_lo_done, 1)

            def combine(b, g):
                if g == 0:
                    ge(dve, y_done, b.n * 4)
                dve.wait_ge(pv_done, b.n * 12 + (3 * g + 3))
                dve.reciprocal(inv_sum[:, :, 4 * g:4 * g + 4], row_sum[:, :, 4 * g:4 * g + 4]).then_inc(inv_done, 1)
                dve.wait_ge(cross_out, b.n * 4 + (g + 1))
                ge(dve, y_done, b.n * 4 + g)
                src = y_bank[:].rearrange("p (t h w d) -> p t h w d", t=NT, h=GH, w=2)[:, :, :, 0, :]
                dve.tensor_tensor(y_sum[:], src, y_cross[:], ALU.add).then_inc(ysum_done, 1)

            def body(b0, b1, b2, b3):
                for s in range(12):
                    if b2:
                        maxima(b2, s)
                    if s == 2 and b3:
                        combine(b3, 3)
                    if s in (5, 8, 11) and b2:
                        combine(b2, (s - 5) // 3)
                    if s == 0 and b3:
                        p_low(b3, 11)
                    if s >= 1 and b2:
                        p_low(b2, s - 1)
                    bank = g_bank[(s - 1) % 3]
                    if s in ROTATED and b1:
                        i = ROTATED.index(s)
                        dve.wait_ge(r_hi_done, b1.n * 4 + (i + 1))
                        dve.tensor_tensor(r_lo[:, i % 2, :], q_rot[:, i % 2].rearrange("p m t -> p (m t)"),
                                          r_hi[:, i % 2, :].bitcast(F32), ALU.subtract).then_inc(r_lo_done, 1)
                    if s in (1, 2) and b1:
                        dve.wait_ge(xt_hi_done, b1.n * 2 + s)
                        cols = slice((s - 1) * P, s * P)
                        dve.tensor_tensor(xT_lo[:, :, cols], bank[:].rearrange("p (k t) -> p k t", k=KT),
                                          xT_hi[:, :, cols].bitcast(F32), ALU.subtract).then_inc(xt_lo_done, 1)
                    if s in AFTER_QK and b1:
                        i = AFTER_QK.index(s)
                        dve.wait_ge(qk_out, b1.n * 4 + (i + 1))
                        ge(dve, rot_done, b1.n * 4 + (i - 1))
                        for half in (0, 64):
                            other = 64 - half
                            sin2 = view(sin_s[other:other + 64], 0, [[0, 2], [1, T]])
                            ins = dve.tensor_tensor(q_sin[half:half + 64, i % 2], q_rot[other:other + 64, i % 2], sin2,
                                                    ALU.mult)
                        ins.then_inc(sin_done, 1)
                    if s in (5, 7) and b3:
                        t = (s - 5) // 2
                        dve.wait_ge(yt_hi_done, b3.n * 2 + (t + 1))
                        for k in range(KT):
                            cols = slice(t * P, (t + 1) * P)
                            ins = dve.scalar_tensor_tensor(out=yT_lo[:, k, cols], in0=bank[:, k * P:(k + 1) * P],
                                                           scalar=bias_v[:, k:k + 1], in1=yT_hi[:, k, cols].bitcast(F32),
                                                           op0=ALU.add, op1=ALU.subtract)
                        ins.then_inc(yt_lo_done, 1)
                    if s in (3, 10) and b1:
                        t = (3, 10).index(s)
                        dve.wait_ge(v_hi_done, b1.n * 2 + (t + 1))
                        vs = v_split[b1.parity]
                        dve.tensor_tensor(vs[:, t, :, 1, :], bank[:].rearrange("p (h d) -> p h d", d=HD),
                                          vs[:, t, :, 0, :].bitcast(F32), ALU.subtract).then_inc(v_lo_done, 1)
                    if s == 3 and b0:
                        norm_stats(b0)
                    if s == 7 and b0:
                        norm_apply(b0)
                    if s == 11 and b3:
                        for t in range(NT):
                            dve.wait_ge(wo_done, b3.n * 2 + (t + 1))
                            dve.wait_ge(res_biased, b3.n + 1)
                            dve.tensor_tensor(x_res[:, t, :], g_bank[(10 + t) % 3][:], x_res[:, t, :],
                                              ALU.add).then_inc(x_mid_done, 1)

            schedule(dve, body)

        @block.tensor
        def _(pe):
            def split_product(out, lhs, rhs, first, last):
                pe.matmul(out, lhs[0], rhs[0], start=first, stop=False)
                pe.matmul(out, lhs[0], rhs[1], start=False, stop=False)
                return pe.matmul(out, lhs[1], rhs[0], start=False, stop=last)

            pe.wait_ge(zeroed, 3)
            for w in range(16):
                pe.wait_ge(w_loaded[w % 4], 16 * (w // 4 + 1))
                if w >= 8:
                    pe.wait_ge(w_lo_done, w - 7)
                for k in range(KT):
                    ins = pe.transpose(psum[w % 8][:, k * P:(k + 1) * P], w_stage[:, w % 4, k * P:(k + 1) * P], ident[:])
                ins.then_inc(w_turned, 1)
            pe.wait_ge(w_lo_done, 10)
            pe.wait_ge(const_built, 2)

            def scores(b, u):
                g, qt, heads, nk = unit(u)
                ge(pe, exp_done, b.n * 12 + (u - 1))
                if u % 6 == 0:
                    for i in (u // 3, u // 3 + 1):
                        pe.wait_ge(stacked[b.parity][i], b.k * 48 + 48)
                out, nh, masked = s_bank[u % 2], len(heads), qt == 0
                if masked:
                    pe.matmul(out[:], ident_b[:], view(mask_b[:], 0, [[0, nh], [1, P]]), start=True, stop=False)
                for j, r in enumerate(heads):
                    ins = pe.matmul(out[:, j * nk:(j + 1) * nk], q_stack[b.parity][0:96, place(g, r), qt * P:(qt + 1) * P],
                                    k_stack[b.parity][0:96, place(g, r), 0:nk], start=not masked, stop=masked and j == nh - 1)
                    if not masked:
                        ins = pe.matmul(out[:, (j + 1) * nk - P:(j + 1) * nk], ident_b[:], mask_b[:], start=False, stop=True)
                ins.then_inc(scores_done, 1)

            def turn_probs(b, u):
                pe.wait_ge(exp_done, b.n * 12 + (u + 1))
                ge(pe, p_lo_done, b.n * 12 + (u - 1))
                for k in range(4):
                    ins = pe.transpose(t_bank[u % 2][:, k * P:(k + 1) * P], probs[:, u % 2, k * P:(k + 1) * P], ident[:])
                ins.then_inc(pt_done, 1)

            def values(b, u):
                g, qt, heads, nk = unit(u)
                pe.wait_ge(p_lo_done, b.n * 12 + (u + 1))
                if u == 0:
                    pe.wait_ge(v_lo_done, b.n * 2 + 2)
                if u % 3 == 0:
                    ge(pe, ysum_done, b.n * 4 + g)
                v = v_split[b.parity]
                nb = nk // P
                for j, r in enumerate(heads):
                    col = (qt * GH + r) * 2 * HD
                    for k in range(nb):
                        blk = slice((j * nb + k) * P, (j * nb + k + 1) * P)
                        pe.matmul(y_bank[:, col:col + 2 * HD], p_hi[:, u % 2, blk],
                                  v[:, k, 4 * g + r].rearrange("p w d -> p (w d)"), start=(k == 0), stop=False)
                    for k in range(nb):
                        blk = slice((j * nb + k) * P, (j * nb + k + 1) * P)
                        ins = pe.matmul(y_bank[:, col:col + HD], p_lo[:, u % 2, blk], v[:, k, 4 * g + r, 0, :],
                                        start=False, stop=(k == nb - 1))
                ins.then_inc(pv_done, 1)

            def turn_x(b, t):
                pe.wait_ge(xn_done, b.n * 2 + (t + 1))
                for k in range(KT):
                    ins = pe.transpose(g_bank[t][:, k * P:(k + 1) * P], x_in[:, t, k * P:(k + 1) * P], ident[:])
                ins.then_inc(xt_done, 1)

            def project_qk(b, i, bank):
                for m, tile in enumerate(QK_TILES[i]):
                    for k in range(KT):
                        cols = slice(tile * P, (tile + 1) * P)
                        ins = split_product(bank[:, m * T:(m + 1) * T], (wT_hi[:, k, cols], wT_lo[:, k, cols]),
                                            (xT_hi[:, k, :], xT_lo[:, k, :]), k == 0, k == KT - 1)
                ins.then_inc(qk_done, 1)

            def project_rows(lhs, rhs, cols, rcols, bank, done):
                for k in range(KT):
                    ins = split_product(bank[:], (lhs[0][:, k, cols], lhs[1][:, k, cols]),
                                        (rhs[0][:, k, rcols], rhs[1][:, k, rcols]), k == 0, k == KT - 1)
                ins.then_inc(done, 1)

            def general(s, b1, b3):
                bank = g_bank[s % 3]
                if s == 0 and b1:
                    ge(pe, v_lo_done, b1.n * 2)
                    turn_x(b1, 0)
                if s == 1 and b1:
                    ge(pe, qk_out, b1.n * 4)
                    if b3:
                        ge(pe, x_mid_done, b3.n * 2 - 1)
                    turn_x(b1, 1)
                if s in (2, 9) and b1:
                    t = (2, 9).index(s)
                    if b3:
                        ge(pe, x_mid_done, b3.n * 2)
                    if b3 and t:
                        pe.wait_ge(yt_lo_done, b3.n * 2 + 2)
                    pe.wait_ge(xt_lo_done, b1.n * 2 + (t + 1))
                    project_rows((xT_hi, xT_lo), (wT_hi, wT_lo), slice(t * P, (t + 1) * P), slice(2 * C, 3 * C), bank, v_done)
                if s in (3, 5, 7, 8) and b1:
                    i = (3, 5, 7, 8).index(s)
                    pe.wait_ge(xt_lo_done, b1.n * 2 + 2)
                    if i == 1:
                        pe.wait_ge(v_lo_done, b1.n * 2 + 1)
                    if i == 2 and b3:
                        pe.wait_ge(yt_lo_done, b3.n * 2 + 1)
                    if i == 3:
                        pe.wait_ge(qk_out, b1.n * 4 + 2)
                    project_qk(b1, i, bank)
                if s in (4, 6) and b3:
                    t = (4, 6).index(s)
                    if b1 and t == 0:
                        pe.wait_ge(xt_lo_done, b1.n * 2 + 2)
                    if b1 and t == 1:
                        pe.wait_ge(qk_out, b1.n * 4 + 1)
                    if not b1:
                        pe.wait_ge(x_mid_done, b3.n * 2)
                        pe.wait_ge(v_lo_done, 2 * B)
                        pe.wait_ge(yt_lo_done, b3.n * 2)
                    pe.wait_ge(y_done, b3.n * 4 + 4)
                    for k in range(KT):
                        ins = pe.transpose(bank[:, k * P:(k + 1) * P], y_rows[:, t, k * P:(k + 1) * P], ident[:])
                    ins.then_inc(yt_done, 1)
                if s in (10, 11) and b3:
                    t = s - 10
                    pe.wait_ge(yt_lo_done, b3.n * 2 + (t + 1))
                    if b1:
                        pe.wait_ge(qk_out, b1.n * 4 + (t + 3))
                    else:
                        pe.wait_ge(x_mid_done, b3.n * 2)
                    project_rows((yT_hi, yT_lo), (woT_hi, woT_lo), slice(t * P, (t + 1) * P), slice(0, C), bank, wo_done)

            def body(b0, b1, b2, b3):
                for s in range(12):
                    if b2:
                        scores(b2, s)
                    if s == 0 and b3:
                        turn_probs(b3, 11)
                    if s >= 1 and b2:
                        turn_probs(b2, s - 1)
                    general(s, b1, b3)
                    if s <= 1 and b3:
                        values(b3, s + 10)
                    if s >= 2 and b2:
                        values(b2, s - 2)

            schedule(pe, body)


def weight_dst(w_qkv, w_o, psum, w):
    if w < 8:
        dst = w_qkv[:, :, w * P:(w + 1) * P].rearrange("p k (d r) -> p k r d", r=GH)
        return dst, psum[w % 8][:].rearrange("p (k r d) -> p k r d", k=KT, r=GH)
    dst = w_qkv[:, :, w * P:(w + 1) * P] if w < 12 else w_o[:, :, (w - 12) * P:(w - 11) * P]
    return dst, psum[w % 8][:].rearrange("p (k o) -> p k o", k=KT)


def rotary_tables():
    import numpy as np
    half = HD // 2
    p = np.arange(half, dtype=np.float32)
    theta = np.power(np.float32(10000.0), -np.power(np.float32(2.0), p) / np.float32(HD)).astype(np.float32)
    angle = np.arange(1, T + 1, dtype=np.float32)[:, None] * theta
    freq = (np.arange(P) // GH) % half
    sign = np.where(np.arange(P) < P // 2, 1.0, -1.0).astype(np.float32)[:, None]
    return np.cos(angle).T[freq].copy(), np.sin(angle).T[freq] * sign


def backwards(rows):
    return view(rows, P - 1, [[P, KT], [-1, P]])


class Head:

    def __init__(self, k, parity):
        self.k, self.parity = k, parity
        self.n = k * 2 + parity


class Step:

    def __init__(self, k, parity):
        self.k, self.parity = k, parity
        self.n = k * 2 + parity

    def head(self, d):
        if isinstance(self.n, int) and not 0 <= self.n + d < CH:
            return None
        return Head(self.k + (self.parity + d) // 2, (self.parity + d) % 2)


def conv_schedule(body):
    def run(eng):
        for n in range(-3, 4):
            body(Step(n // 2, n % 2))
        with eng.Fori(2, 14) as i:
            body(Step(i, 0))
            body(Step(i, 1))
        for n in range(28, 35):
            body(Step(n // 2, n % 2))
    return run


def split_product(pe, out, lhs, rhs, first, last):
    pe.matmul(out, lhs[0], rhs[0], start=first, stop=False)
    pe.matmul(out, lhs[0], rhs[1], start=False, stop=False)
    return pe.matmul(out, lhs[1], rhs[0], start=False, stop=last)


def convolution(nc, x_mid, ctx_in, taps_d, gate_w, logits, x_out, zT_d):
    with ExitStack() as ctx:
        def sb(name, shape, dt=F32):
            return ctx.enter_context(nc.sbuf_tensor(name, shape, dt))

        def sem(name):
            return ctx.enter_context(nc.semaphore(name))

        ident = sb("conv_ident", [P, P])
        gate_rows = sb("gate_rows", [CI, C])
        gateT_hi, gateT_lo = sb("gateT_hi", [P, KT, CI], F32R), sb("gateT_lo", [P, KT, CI], F32R)
        ctx_rows, res_rows = sb("ctx_rows", [P, C]), sb("res_rows", [P, C])
        mid_rows = [sb(f"mid_rows{i}", [P, C]) for i in range(2)]
        q_rows = sb("q_rows", [P, C])
        out_rows, z_rows = sb("out_rows", [P, C]), sb("z_rows", [P, C])
        taps_hi, taps_lo = ([sb(f"taps_{w}{i}", [P, C], F32R) for i in range(2)] for w in ("hi", "lo"))
        kT = sb("kT", [P, KT, KX])
        qT = [sb(f"qT{i}", [P, KT, KX]) for i in range(2)]
        pairs = [sb(f"pairs{i}", [P, KT, PAIR]) for i in range(2)]
        kv_hi, kv_lo = ([sb(f"kv_{w}{i}", [P, KT, PAIR], F32R) for i in range(2)] for w in ("hi", "lo"))
        terms = [sb(f"terms{i}", [P, KT, TERM]) for i in range(2)]
        acc = sb("acc", [P, KT, P])
        zT_hi, zT_lo = sb("zT_hi", [P, KT, P], F32R), sb("zT_lo", [P, KT, P], F32R)
        stats, mean_var = sb("conv_stats", [P, 2, 6]), sb("conv_mean_var", [P, 2, 2])
        var_eps, rstd, newt = sb("conv_var_eps", [P, 2]), sb("conv_rstd", [P, 2]), sb("conv_newt", [P, 2])
        minus_mean, shift = sb("minus_mean", [P, 2]), sb("shift", [P, 2])
        half_var, three_halves = sb("half_var", [P, 2]), sb("three_halves", [P, 1])

        psum = [ctx.enter_context(nc.psum_tensor(f"conv_bank{i}", [P, 512], F32)) for i in range(8)]
        y_bank = (psum[0:2], psum[2:4])
        kT_bank, qT_bank, out_bank, z_bank = psum[4:8]
        logit_bank = z_bank

        names = ("zeroed", "terms_zeroed", "const_built", "gate_loaded", "gate_turned", "gate_split", "ctx_loaded", "res_loaded",
                 "ctx_turned", "kT_out", "mid_normed", "mid_turned", "qT_out", "pairs_done", "squares_done", "kv_hi_done", "kv_lo0_done", "kv_lo_done",
                 "conv_done", "terms_done", "half_summed", "acc_done", "acc_turned", "out_done", "out_normed",
                 "z_turned", "z_hi_done", "z_lo_done", "logits_done", "logits_out", "out_stored", "z_stored",
                 "norm_cleared", "stats0_chain", "stats1_chain", "guess_chain", "guess_done", "newton_done", "shift_done",
                 "dve_passed", "pool_passed")
        S = {nm: sem("conv_" + nm) for nm in names}
        taps_loaded = [sem(f"conv_taps_loaded{i}") for i in range(2)]
        mid_loaded = [sem(f"conv_mid_loaded{i}") for i in range(2)]
        stats_chain = [S["stats0_chain"], S["stats1_chain"]]
        mid_v = x_mid.rearrange("s b c -> (s b) c")

        block = ctx.enter_context(nc.Block())

        @block.sync
        def _(sp):
            sp.dma_start(gate_rows[:], gate_w).then_inc(S["gate_loaded"], 16)

            def body(step):
                early, front, split, tail, out = (step.head(d) for d in (3, 2, 1, -1, -2))
                if tail:
                    h = sp.snap(tail.n)
                    ge(sp, S["out_done"], tail.n)
                    sp.dma_start(res_rows[:], mid_v[bass.ds(h * P, P), :]).then_inc(S["res_loaded"], 16)
                if split:
                    h = sp.snap(split.n)
                    ge(sp, S["conv_done"], split.n * 4 - 4)
                    for w, dst in ((0, taps_hi), (1, taps_lo)):
                        band = taps_d[w, h, :]
                        band = bass.AP(tensor=band.tensor, offset=band.offset, ap=[[1, P], [1, C]])
                        sp.dma_start(dst[split.parity][:].bitcast(F32), band).then_inc(taps_loaded[split.parity], 16)
                if early:
                    h = sp.snap(early.n)
                    ge(sp, S["ctx_turned"], early.n)
                    src = ctx_in[:, bass.ds(h * CI, CI), :].rearrange("b i c -> i b c")
                    sp.dma_start(ctx_rows[:], src).then_inc(S["ctx_loaded"], 16)
                if front:
                    h = sp.snap(front.n)
                    ge(sp, S["mid_normed"], front.n - 1)
                    sp.dma_start(mid_rows[front.parity][:], mid_v[bass.ds(h * P, P), :]).then_inc(mid_loaded[front.parity], 16)
                if tail:
                    h = sp.snap(tail.n)
                    sp.wait_ge(S["out_done"], tail.n + 1)
                    sp.dma_start(x_out[h], out_rows[:]).then_inc(S["out_stored"], 16)
                if out:
                    h = sp.snap(out.n)
                    sp.wait_ge(S["z_lo_done"], out.n + 1)
                    sp.dma_start(zT_d[0, h], zT_hi[:].bitcast(F32)).then_inc(S["z_stored"], 16)
                    sp.dma_start(zT_d[1, h], zT_lo[:].bitcast(F32)).then_inc(S["z_stored"], 16)

            conv_schedule(body)(sp)
            sp.wait_ge(S["out_stored"], 16 * CH)
            sp.wait_ge(S["z_stored"], 32 * CH)

        @block.gpsimd
        def _(pool):
            pool.memset(ident[:], 0.0).then_inc(S["zeroed"], 1)
            pool.wait_ge(S["zeroed"], 1)
            pool.affine_select(out=ident[:], in_=ident[:], compare_op=ALU.not_equal, fill=1.0, base=0,
                               pattern=[[-1, P]], channel_multiplier=1).then_inc(S["const_built"], 1)

            def body(step):
                front, split, tail = (step.head(d) for d in (2, 1, -1))
                if tail:
                    pool.wait_ge(S["terms_done"], tail.n * 4 + 4)
                    t = terms[tail.parity]
                    for j, (a, b) in enumerate(((5, 4), (7, 6), (5, 8), (5, 7))):
                        if j >= 2:
                            pool.wait_ge(S["half_summed"], tail.n * 4 + j)
                        pool.tensor_tensor(t[:, :, a * P:(a + 1) * P], t[:, :, a * P:(a + 1) * P],
                                           t[:, :, b * P:(b + 1) * P], ALU.add).then_inc(S["half_summed"], 1)
                if split:
                    pool.wait_ge(S["kv_hi_done"], split.n + 1)
                    pool.tensor_tensor(kv_lo[split.parity][:, 0:POOL_LOW], pairs[split.parity][:, 0:POOL_LOW],
                                       kv_hi[split.parity][:, 0:POOL_LOW].bitcast(F32),
                                       ALU.subtract).then_inc(S["kv_lo0_done"], 1)
                if front:
                    pool.wait_ge(S["kT_out"], front.n * 2 + 2)
                    ge(pool, S["kv_lo0_done"], front.n - 1)
                    ge(pool, S["kv_lo_done"], front.n - 1)
                    k, p = kT[:], pairs[front.parity][:]
                    row = [KX, KT]
                    pool.tensor_tensor(view(p, P, [[PAIR, KT], [1, P]]), view(k, 0, [row, [1, P]]),
                                       view(k, B, [row, [1, P]]), ALU.mult).then_inc(S["pairs_done"], 1)
                    pool.tensor_tensor(view(p, 320, [[PAIR, KT], [P, 2], [1, P]]), view(k, 0, [row, [0, 2], [1, P]]),
                                       view(k, 2 * B, [row, [B, 2], [1, P]]), ALU.mult).then_inc(S["pairs_done"], 1)
                    pool.tensor_tensor(view(p, 256, [[PAIR, KT], [1, 64]]), view(k, 0, [row, [1, 64]]),
                                       view(k, 64, [row, [1, 64]]), ALU.mult).then_inc(S["pairs_done"], 1)

            conv_schedule(body)(pool)

        @block.scalar
        def _(act):
            def newton(step):
                done, base = S["newton_done"], (step.n + 1) * ACT_NEWTON
                act.wait_ge(S["guess_done"], step.n + 2)
                act.activation(newt[:], rstd[:], ACT.Square).then_inc(done, 1)
                for i in range(3):
                    act.wait_ge(done, base + 5 * i + 1)
                    for w in range(2):
                        act.activation(newt[:, w:w + 1], newt[:, w:w + 1], ACT.Identity, bias=three_halves[:],
                                       scale=half_var[:, w:w + 1]).then_inc(done, 1)
                    act.wait_ge(done, base + 5 * i + 3)
                    for w in range(2):
                        act.activation(rstd[:, w:w + 1], rstd[:, w:w + 1], ACT.Identity, scale=newt[:, w:w + 1]).then_inc(done, 1)
                    act.wait_ge(done, base + 5 * i + 5)
                    if i < 2:
                        act.activation(newt[:], rstd[:], ACT.Square).then_inc(done, 1)
                for w in range(2):
                    ins = act.activation(shift[:, w:w + 1], minus_mean[:, w:w + 1], ACT.Identity, scale=rstd[:, w:w + 1])
                ins.then_inc(S["shift_done"], 1)

            def norm_apply(step, w, out, rows, done):
                act.wait_ge(S["shift_done"], step.n + 2)
                act.activation(out, rows, ACT.Identity, bias=shift[:, w:w + 1], scale=rstd[:, w:w + 1]).then_inc(done, 1)

            def body(step):
                front, split, out, last = (step.head(d) for d in (2, 1, -2, -3))
                if split:
                    act.wait_ge(S["pairs_done"], split.n * 3 + 3)
                    act.wait_ge(S["squares_done"], split.n + 1)
                    ge(act, S["conv_done"], split.n * 4 - 4)
                    act.activation(kv_hi[split.parity][:], pairs[split.parity][:], ACT.Copy).then_inc(S["kv_hi_done"], 1)
                if front:
                    act.wait_ge(S["ctx_turned"], front.n + 1)
                    ge(act, S["pairs_done"], front.n * 3)
                    src = kT_bank[:].rearrange("p (k t) -> p k t", k=KT)
                    act.activation(kT[:, :, 0:P], src, ACT.Copy).then_inc(S["kT_out"], 1)
                    act.activation(kT[:, :, P:KX], src[:, :, 0:64], ACT.Copy).then_inc(S["kT_out"], 1)
                    ge(act, S["kv_lo0_done"], front.n - 1)
                    ge(act, S["kv_lo_done"], front.n - 1)
                    act.activation(pairs[front.parity][:, :, 0:P], src, ACT.Square).then_inc(S["squares_done"], 1)
                if split or out:
                    newton(step)
                if last:
                    at = last.n if isinstance(last.n, int) else act.snap(last.n)
                    act.wait_ge(S["logits_done"], last.n + 1)
                    act.activation(logits[:, bass.ds(at * CI, CI)], logit_bank[:, 0:CI], ACT.Copy).then_inc(S["logits_out"], 1)
                if out:
                    ge(act, S["z_turned"], out.n)
                    norm_apply(step, 1, z_rows[:], out_rows[:], S["out_normed"])
                if split:
                    ge(act, S["mid_turned"], split.n)
                    norm_apply(step, 0, backwards(q_rows[:]), mid_rows[split.parity][:].rearrange("p (k c) -> p k c", k=KT), S["mid_normed"])
                if out:
                    act.wait_ge(S["z_turned"], out.n + 1)
                    ge(act, S["z_stored"], out.n * 32)
                    ge(act, S["logits_done"], out.n)
                    act.activation(zT_hi[:], z_bank[:].rearrange("p (k t) -> p k t", k=KT), ACT.Copy).then_inc(S["z_hi_done"], 1)
                if split:
                    act.wait_ge(S["mid_turned"], split.n + 1)
                    ge(act, S["terms_done"], split.n * 4 - 4)
                    src = qT_bank[:].rearrange("p (k t) -> p k t", k=KT)
                    q = qT[split.parity]
                    act.activation(q[:, :, 0:P], src, ACT.Copy).then_inc(S["qT_out"], 1)
                    act.activation(q[:, :, P:KX], src[:, :, 0:64], ACT.Copy).then_inc(S["qT_out"], 1)

            conv_schedule(body)(act)

        @block.vector
        def _(dve):
            for t in terms:
                dve.memset(view(t[:], P, [[TERM, KT], [P + B, 4], [1, B]]), 0.0).then_inc(S["terms_zeroed"], 1)
                dve.memset(view(t[:], 8 * P + 64, [[TERM, KT], [1, 64]]), 0.0).then_inc(S["terms_zeroed"], 1)
            dve.wait_ge(S["gate_turned"], 1)
            src = z_bank[:, 0:KT * CI].rearrange("p (k e) -> p k e", k=KT)
            dve.tensor_copy(gateT_hi[:], src).then_inc(S["gate_split"], 1)
            dve.wait_ge(S["gate_split"], 1)
            dve.tensor_tensor(gateT_lo[:], src, gateT_hi[:].bitcast(F32), ALU.subtract).then_inc(S["gate_split"], 1)
            dve.memset(mean_var[:], 0.0).then_inc(S["norm_cleared"], 1)
            dve.memset(three_halves[:], 1.5).then_inc(S["norm_cleared"], 1)
            dve.wait_ge(S["norm_cleared"], 2)
            dve.wait_ge(S["terms_zeroed"], 4)

            def norm_stats(h, w, rows):
                dve.bn_stats(stats[:, w, :], rows).then_inc(stats_chain[w], 1)

            def norm_mean_var(h, w):
                wait_apart(dve, stats_chain[w], h.n * 2 + 1, S["dve_passed"])
                dve.bn_aggr(mean_var[:, w, :], stats[:, w, :]).then_inc(stats_chain[w], 1)

            def guess(step, n):
                chain, base = S["guess_chain"], step.n * 4 + 8
                front, split, tail, out = (step.head(d) for d in (2, 1, -1, -2))
                if n == 0:
                    if split:
                        dve.wait_ge(S["mid_normed"], split.n + 1)
                    if out:
                        dve.wait_ge(S["out_normed"], out.n + 1)
                    if front:
                        dve.wait_ge(stats_chain[0], front.n * 2 + 2)
                    if tail:
                        dve.wait_ge(stats_chain[1], tail.n * 2 + 2)
                    dve.tensor_scalar(var_eps[:], mean_var[:, :, 1], EPS, None, ALU.add).then_inc(chain, 1)
                    dve.tensor_scalar(minus_mean[:], mean_var[:, :, 0], -1.0, None, ALU.mult).then_inc(chain, 1)
                    dve.tensor_scalar(half_var[:], mean_var[:, :, 1], EPS, -0.5, ALU.add, ALU.mult).then_inc(chain, 1)
                elif n == 1:
                    dve.wait_ge(chain, base + 3)
                    dve.tensor_scalar(newt[:].bitcast(I32), var_eps[:].bitcast(I32), 1, None,
                                      ALU.logical_shift_right).then_inc(chain, 1)
                else:
                    dve.wait_ge(chain, base + 4)
                    dve.tensor_scalar(rstd[:].bitcast(I32), newt[:].bitcast(I32), -1.0, MAGIC,
                                      ALU.mult, ALU.add).then_inc(S["guess_done"], 1)

            def products(h, lb):
                ya, yb = y_bank[lb % 2]
                q, t = qT[h.parity][:, lb, :], terms[h.parity][:, lb, :]
                a, b = ya[:], yb[:]
                if lb == 0:
                    dve.wait_ge(S["qT_out"], h.n * 2 + 2)
                    ge(dve, S["acc_turned"], h.n - 1)
                dve.wait_ge(S["conv_done"], h.n * 4 + (lb + 1))
                two = [[P, 2], [1, P]]
                for out, y, m in (
                    (view(t, 0, [[P + B, 2], [1, P]]), view(a, 0, two), view(q, 0, [[0, 2], [1, P]])),
                    (view(t, 2 * (P + B), [[P + B, 2], [1, P]]), view(b, 0, two), view(q, 0, [[0, 2], [1, P]])),
                    (view(t, 5 * P, [[1, P]]), view(a, P, [[1, P]]), view(q, B, [[1, P]])),
                    (view(t, 6 * P, two), view(b, 0, two), view(q, 2 * B, [[B, 2], [1, P]])),
                    (view(t, 4 * P + 64, [[4 * P - 64, 2], [1, 64]]), view(a, 2 * P, [[0, 2], [1, 64]]), view(q, 0, [[64, 2], [1, 64]])),
                ):
                    ins = dve.tensor_tensor(out, y, m, ALU.mult)
                ins.then_inc(S["terms_done"], 1)

            def body(step):
                front, split, conv, tail, out = (step.head(d) for d in (2, 1, 0, -1, -2))
                if conv:
                    products(conv, 1)
                if tail:
                    dve.wait_ge(S["terms_done"], tail.n * 4 + 4)
                    ge(dve, S["acc_turned"], tail.n)
                    rows = view(terms[tail.parity][:], 0, [[TERM, KT], [1, P], [P, 4]])
                    dve.tensor_reduce(acc[:], rows, AX.X, ALU.add).then_inc(S["acc_done"], 1)
                if conv:
                    products(conv, 2)
                if split:
                    dve.wait_ge(S["kv_hi_done"], split.n + 1)
                    dve.tensor_tensor(kv_lo[split.parity][:, POOL_LOW:KT], pairs[split.parity][:, POOL_LOW:KT],
                                      kv_hi[split.parity][:, POOL_LOW:KT].bitcast(F32),
                                      ALU.subtract).then_inc(S["kv_lo_done"], 1)
                if conv:
                    products(conv, 3)
                if front:
                    dve.wait_ge(mid_loaded[front.parity], front.k * 16 + 16)
                    norm_stats(front, 0, mid_rows[front.parity][:])
                if tail:
                    dve.wait_ge(S["acc_turned"], tail.n + 1)
                    dve.wait_ge(S["res_loaded"], tail.n * 16 + 16)
                    ge(dve, S["out_stored"], tail.n * 16)
                    ge(dve, S["out_normed"], tail.n)
                    rows, res = (t[:].rearrange("p (k c) -> p k c", k=KT) for t in (out_rows, res_rows))
                    dve.tensor_tensor(rows, backwards(out_bank[:]), res, ALU.add).then_inc(S["out_done"], 1)
                if front:
                    norm_mean_var(front, 0)
                if tail:
                    dve.wait_ge(S["out_done"], tail.n + 1)
                    norm_stats(tail, 1, out_rows[:])
                if out:
                    dve.wait_ge(S["z_hi_done"], out.n + 1)
                    dve.tensor_tensor(zT_lo[:], z_bank[:].rearrange("p (k t) -> p k t", k=KT), zT_hi[:].bitcast(F32),
                                      ALU.subtract).then_inc(S["z_lo_done"], 1)
                if tail:
                    norm_mean_var(tail, 1)
                if split:
                    products(split, 0)
                if front or tail:
                    guess(step, 0)
                if front or tail:
                    guess(step, 1)
                    guess(step, 2)

            conv_schedule(body)(dve)

        @block.tensor
        def _(pe):
            pe.wait_ge(S["gate_loaded"], 16)
            pe.wait_ge(S["const_built"], 1)
            for k in range(KT):
                ins = pe.transpose(z_bank[:, k * CI:(k + 1) * CI], gate_rows[:, k * P:(k + 1) * P], ident[0:CI, 0:CI])
            ins.then_inc(S["gate_turned"], 1)

            def turn(bank, rows, done):
                for k in range(KT):
                    ins = pe.transpose(bank[:, k * P:(k + 1) * P], rows[:, k * P:(k + 1) * P], ident[:])
                ins.then_inc(done, 1)

            def convolve(h, lb):
                if lb == 0:
                    pe.wait_ge(S["kv_lo0_done"], h.n + 1)
                    pe.wait_ge(S["kv_lo_done"], h.n + 1)
                    pe.wait_ge(taps_loaded[h.parity], h.k * 32 + 32)
                ge(pe, S["terms_done"], h.n * 4 + (lb - 1))
                for mb in range(lb + 1):
                    r = slice(C - (lb - mb + 1) * P, C - (lb - mb) * P)
                    hi, lo = taps_hi[h.parity][:, r], taps_lo[h.parity][:, r]
                    for bank, (c0, c1) in zip(y_bank[lb % 2], HALVES):
                        ins = split_product(pe, bank[:, 0:c1 - c0], (hi, lo),
                                            (kv_hi[h.parity][:, mb, c0:c1], kv_lo[h.parity][:, mb, c0:c1]),
                                            mb == 0, mb == lb)
                ins.then_inc(S["conv_done"], 1)

            def body(step):
                front, split, conv, tail, out, last = (step.head(d) for d in (2, 1, 0, -1, -2, -3))
                if conv:
                    convolve(conv, 1)
                if front:
                    pe.wait_ge(S["ctx_loaded"], front.n * 16 + 16)
                    ge(pe, S["squares_done"], front.n)
                    turn(kT_bank, ctx_rows, S["ctx_turned"])
                if last:
                    pe.wait_ge(S["z_lo_done"], last.n + 1)
                    for k in range(KT):
                        ins = split_product(pe, logit_bank[:, 0:CI], (zT_hi[:, k, :], zT_lo[:, k, :]),
                                            (gateT_hi[:, k, :], gateT_lo[:, k, :]), k == 0, k == KT - 1)
                    ins.then_inc(S["logits_done"], 1)
                if conv:
                    convolve(conv, 2)
                if conv:
                    convolve(conv, 3)
                if tail:
                    pe.wait_ge(S["half_summed"], tail.n * 4 + 4)
                    pe.wait_ge(S["acc_done"], tail.n + 1)
                    ge(pe, S["out_done"], tail.n)
                    for k in range(KT):
                        t = terms[tail.parity][:, k]
                        for n, rows in enumerate((t[:, 5 * P:6 * P], acc[:, k])):
                            ins = pe.matmul(out_bank[:, k * P:(k + 1) * P], rows, ident[:], start=(n == 0), stop=(n == 1))
                    ins.then_inc(S["acc_turned"], 1)
                if out:
                    if isinstance(out.n, int) and out.n == 0:
                        pe.wait_ge(S["gate_split"], 2)
                    pe.wait_ge(S["out_normed"], out.n + 1)
                    ge(pe, S["logits_out"], out.n)
                    turn(z_bank, z_rows, S["z_turned"])
                if split:
                    pe.wait_ge(S["mid_normed"], split.n + 1)
                    ge(pe, S["qT_out"], split.n * 2)
                    turn(qT_bank, q_rows, S["mid_turned"])
                if split:
                    convolve(split, 0)

            conv_schedule(body)(pe)


E = 8
F = 2048
FT = F // P
BLOCKS = B * T // 512
TB = 4


def experts(nc, logits, x_d, zT_d, w1, b1, w2, b2, out):
    with ExitStack() as ctx:
        def sb(name, shape, dt=F32):
            return ctx.enter_context(nc.sbuf_tensor(name, shape, dt))

        def sem(name):
            return ctx.enter_context(nc.semaphore("moe_" + name))

        w1_hi, w1_lo = sb("w1_hi", [P, FT, KT, P], F32R), sb("w1_lo", [P, FT, KT, P], F32R)
        w2_hi, w2_lo = sb("w2_hi", [P, FT, C], F32R), sb("w2_lo", [P, FT, C], F32R)
        w1_stage, w2_stage = sb("w1_stage", [P, 2, KT, P]), sb("w2_stage", [P, 2, C])
        z_hi, z_lo = ([sb(f"z_{w}{i}", [P, TB, KT, P], F32R) for i in range(2)] for w in ("hi", "lo"))
        hid = sb("hid", [P, 2, 512])
        h_hi, h_lo = sb("h_hi", [P, 2, 512], F32R), sb("h_lo", [P, 2, 512], F32R)
        x_rows = [sb(f"x_rows{i}", [P, TB, C]) for i in range(2)]
        b1_rows, b1_cols, b2_rows = sb("b1_rows", [FT, 2, P]), sb("b1_cols", [P, 2, FT]), sb("b2_rows", [P, 2, C])
        ident, ones, numbers = sb("moe_ident", [FT, FT]), sb("ones", [P, P]), sb("numbers", [P, E])
        tile_sum, total, top = sb("tile_sum", [P, E]), sb("total", [P, E]), sb("top", [P, E])
        chosen, chosen_f = sb("chosen", [P, E], U32), sb("chosen_f", [P, 2])
        is_chosen, picked = sb("is_chosen", [P, 2, E]), sb("picked", [P, CH, E])
        own, share, inv = sb("own", [P, 2, CH]), sb("share", [P, 2, CH]), sb("moe_inv", [P, CH])
        share_now = sb("share_now", [P, TB])

        psum = [ctx.enter_context(nc.psum_tensor(f"moe_bank{i}", [P, 512], F32)) for i in range(8)]
        h_bank, y_bank = psum[0:4], psum[4:8]

        ones_built = sem("ones_built")
        const_built, routed, total_done, exp_done = sem("const_built"), sem("routed"), sem("total_done"), sem("exp_done")
        b1_loaded, b2_loaded, b1_turned, b1_out = sem("b1_loaded"), sem("b2_loaded"), sem("b1_turned"), sem("b1_out")
        w_staged0, w_staged1 = ([sem(f"w_staged{e}_{i}") for i in range(2)] for e in range(2))
        w_high0, w_high1, w_ready = sem("w_high0"), sem("w_high1"), sem("w_ready")
        z_loaded = [sem(f"z_loaded{i}") for i in range(2)]
        x_loaded = [sem(f"x_loaded{i}") for i in range(2)]
        x_stored = [sem(f"x_stored{i}") for i in range(2)]
        h_done, h_bank_free = sem("h_done"), sem("h_bank_free")
        gelu_done, h_high, h_low = sem("gelu_done"), sem("h_high"), sem("h_low")
        y_part = sem("y_part")
        y_done, y_out = sem("y_done"), sem("y_out")
        share_out, x_biased = sem("share_out"), sem("x_biased")

        block = ctx.enter_context(nc.Block())

        def rounds(eng, body):
            for parity in range(2):
                body(0, 0, parity)
            for first, last, e in ((1, 4, 0), (4, 8, 1)):
                with eng.Fori(first, last) as k:
                    for parity in range(2):
                        body(e, k, parity)

        @block.sync
        def _(sp):
            def load(e, k, parity, z=True, x=True):
                it = k * 2 + parity
                at = it if isinstance(it, int) else sp.snap(it)
                blk = (at - e * BLOCKS) * TB
                blk = blk if isinstance(blk, int) else sp.snap(blk)
                if z:
                    ge(sp, h_done, it * FT - FT)
                    for w, dst in ((0, z_hi), (1, z_lo)):
                        src = zT_d[w, bass.ds(blk, TB)].rearrange("t p k c -> p t (k c)")
                        sp.dma_start(dst[parity][:].rearrange("p t k c -> p t (k c)").bitcast(F32), src).then_inc(z_loaded[parity], 16)
                if not x:
                    return
                ge(sp, x_stored[parity], k * 16 if e == 0 else k * 16 * TB + (64 - 4 * 16 * TB))
                sp.dma_start(x_rows[parity][:], x_d[bass.ds(blk, TB)].rearrange("t p c -> p t c")).then_inc(x_loaded[parity], 16)

            def store(e, it, parity):
                at = it if isinstance(it, int) else sp.snap(it)
                if e == 0:
                    blk = at * TB
                    blk = blk if isinstance(blk, int) else sp.snap(blk)
                    sp.wait_ge(y_out, it * TB + (TB + 4))
                    sp.dma_start(x_d[bass.ds(blk, TB)].rearrange("t p c -> p t c"), x_rows[parity][:]).then_inc(x_stored[parity], 16)
                    return
                for t in range(TB):
                    pos = ((at - BLOCKS) * TB + t) * CI
                    pos = pos if isinstance(pos, int) else sp.snap(pos)
                    sp.wait_ge(y_out, it * TB + (t + 1 + 4))
                    dst = out[:, bass.ds(pos, CI), :].rearrange("b i c -> i b c")
                    sp.dma_start(dst, x_rows[parity][:, t, :]).then_inc(x_stored[parity], 16)

            def pair(e, k, e_before):
                load(e, k, 0)
                if e_before is not None:
                    store(e_before, k * 2 - 1, 1)
                load(e, k, 1)
                store(e, k * 2, 0)

            load(0, 0, 0, x=False)
            sp.wait_ge(routed, 4)
            expert = [sp.value_load(chosen[0:1, n:n + 1], min_val=0, max_val=E - 1) for n in range(2)]

            def stage(n):
                e = expert[0]
                if n >= 2:
                    sp.wait_ge(w_ready, n - 1)
                src = w1[e, :, n * P:(n + 1) * P].rearrange("(k p) f -> p k f", p=P)
                sp.dma_start(w1_stage[:, n % 2], src).then_inc(w_staged0[n % 2], 16)
                sp.dma_start(w2_stage[:, n % 2, :], w2[e, n * P:(n + 1) * P, :]).then_inc(w_staged0[n % 2], 16)

            for n, e in enumerate(expert):
                sp.dma_start(b1_rows[:, n, :], b1[e, :].rearrange("(j p) -> j p", p=P)).then_inc(b1_loaded, 16)
            stage(0)
            for n, e in enumerate(expert):
                sp.dma_start(b2_rows[:, n, :], b2[e, :].partition_broadcast(P)).then_inc(b2_loaded, 16)
            for n in range(1, FT):
                stage(n)
                if n == 3:
                    load(0, 0, 0, z=False)
            load(0, 0, 1)
            store(0, 0, 0)
            with sp.Fori(1, 4) as k:
                pair(0, k, 0)
            pair(1, 4, 0)
            with sp.Fori(5, 8) as k:
                pair(1, k, 1)
            store(1, 2 * BLOCKS - 1, 1)
            for parity in range(2):
                sp.wait_ge(x_stored[parity], 4 * 16 + 4 * 16 * TB)

        @block.gpsimd
        def _(pool):
            pool.memset(ident[:], 0.0).then_inc(const_built, 1)
            pool.wait_ge(const_built, 1)
            pool.affine_select(out=ident[:], in_=ident[:], compare_op=ALU.not_equal, fill=1.0, base=0,
                               pattern=[[-1, FT]], channel_multiplier=1).then_inc(const_built, 1)
            pool.wait_ge(routed, 4)
            e = pool.value_load(chosen[0:1, 1:2], min_val=0, max_val=E - 1)

            def stage(j):
                pool.wait_ge(w_ready, FT + j - 1)
                src = w1[e, :, j * P:(j + 1) * P].rearrange("(k p) f -> p k f", p=P)
                pool.dma_start(w1_stage[:, j % 2], src).then_inc(w_staged1[j % 2], 16)
                pool.dma_start(w2_stage[:, j % 2, :], w2[e, j * P:(j + 1) * P, :]).then_inc(w_staged1[j % 2], 16)

            stage(0)
            stage(1)
            for j in range(FT):
                pool.wait_ge(w_staged1[j % 2], 32 * (j // 2 + 1))
                pool.wait_ge(y_part, FT * (BLOCKS - 1) + j + 1 + 2)
                pool.tensor_copy(w1_hi[:, j], w1_stage[:, j % 2]).then_inc(w_high1, 1)
                pool.tensor_copy(w2_hi[:, j], w2_stage[:, j % 2]).then_inc(w_high1, 1)
                pool.wait_ge(w_high1, 3 * j + 2)
                pool.tensor_tensor(w1_lo[:, j], w1_stage[:, j % 2], w1_hi[:, j].bitcast(F32), ALU.subtract).then_inc(w_high1, 1)
                pool.wait_ge(w_high1, 3 * j + 3)
                pool.tensor_tensor(w2_lo[:, j], w2_stage[:, j % 2], w2_hi[:, j].bitcast(F32), ALU.subtract).then_inc(w_ready, 1)
                if j + 2 < FT:
                    stage(j + 2)

        @block.scalar
        def _(act):
            act.sem_inc(h_bank_free, 4)
            act.wait_ge(routed, ROUTED_EXP)
            act.activation(own[:], own[:], ACT.Exp).then_inc(exp_done, 1)

            def high_weights(j):
                act.wait_ge(w_staged0[j % 2], 32 * (j // 2 + 1))
                act.activation(w1_hi[:, j], w1_stage[:, j % 2], ACT.Copy).then_inc(w_high0, 1)
                act.activation(w2_hi[:, j], w2_stage[:, j % 2], ACT.Copy).then_inc(w_high0, 1)

            high_weights(0)
            high_weights(1)
            act.wait_ge(b1_out, 1)

            def body(e, k, parity):
                it = k * 2 + parity
                for j in range(FT):
                    if isinstance(it, int) and it == 0 and j + 2 < FT:
                        high_weights(j + 2)
                    act.wait_ge(h_done, it * FT + (j + 1))
                    act.wait_ge(h_low, it * FT + (j + 1))
                    act.activation(hid[:, j % 2, :], h_bank[j % 4][:], ACT.Gelu_apprx_tanh,
                                   bias=b1_cols[:, e, j:j + 1]).then_inc(h_bank_free, 1)
                    act.wait_ge(h_bank_free, it * FT + (j + 1 + 4))
                    act.wait_ge(y_part, it * FT + (j + 1))
                    act.activation(h_hi[:, j % 2, :], hid[:, j % 2, :], ACT.Copy).then_inc(h_high, 1)

            rounds(act, body)

        @block.vector
        def _(dve):
            dve.sem_inc(h_low, 2)
            dve.sem_inc(y_out, 4)
            for n in range(E):
                dve.memset(numbers[:, n:n + 1], float(n)).then_inc(ones_built, 1)
            dve.memset(ones[:], 1.0).then_inc(ones_built, 1)
            dve.tensor_reduce(tile_sum[:], view(logits[:], 0, [[1, E], [E, CH]]), AX.X, ALU.add).then_inc(routed, 1)
            dve.wait_ge(total_done, 1)
            dve.tensor_copy(total[:], h_bank[0][:, 0:E]).then_inc(routed, 1)
            dve.wait_ge(routed, 2)
            dve.max(top[:], total[:]).then_inc(routed, 1)
            dve.wait_ge(routed, 3)
            dve.max_index(chosen[:], top[:], total[:]).then_inc(routed, 1)
            dve.wait_ge(routed, 4)
            dve.tensor_copy(chosen_f[:], chosen[:, 0:2]).then_inc(routed, 1)
            dve.wait_ge(routed, 5)
            dve.wait_ge(ones_built, E + 1)
            for n in range(2):
                dve.tensor_scalar(is_chosen[:, n, :], numbers[:], chosen_f[:, n:n + 1], None, ALU.is_equal).then_inc(routed, 1)
            for n in range(2):
                dve.wait_ge(routed, 7 + 2 * n)
                dve.tensor_tensor(picked[:], logits[:].rearrange("p (t e) -> p t e", e=E),
                                  view(is_chosen[:], n * E, [[0, CH], [1, E]]), ALU.mult).then_inc(routed, 1)
                dve.wait_ge(routed, 8 + 2 * n)
                dve.tensor_reduce(own[:, n, :], picked[:], AX.X, ALU.add).then_inc(routed, 1)
            dve.wait_ge(routed, 11)
            dve.tensor_tensor(inv[:], own[:, 0, :], own[:, 1, :], ALU.max).then_inc(routed, 1)
            dve.wait_ge(routed, 12)
            dve.tensor_tensor(own[:], own[:], view(inv[:], 0, [[0, 2], [1, CH]]), ALU.subtract).then_inc(routed, 1)
            dve.wait_ge(exp_done, 1)
            dve.tensor_tensor(inv[:], own[:, 0, :], own[:, 1, :], ALU.add).then_inc(routed, 1)
            dve.wait_ge(routed, 14)
            dve.reciprocal(inv[:], inv[:]).then_inc(routed, 1)
            dve.wait_ge(routed, 15)
            dve.tensor_tensor(share[:], own[:], view(inv[:], 0, [[0, 2], [1, CH]]), ALU.mult).then_inc(routed, 1)
            dve.wait_ge(b1_turned, 1)
            dve.tensor_copy(b1_cols[:], h_bank[1][:, 0:2 * FT].rearrange("p (n j) -> p n j", n=2)).then_inc(b1_out, 1)
            dve.wait_ge(routed, 16)

            def low_weights(j):
                for n, (hi, lo, stage) in enumerate(((w1_hi, w1_lo, w1_stage), (w2_hi, w2_lo, w2_stage))):
                    dve.wait_ge(w_high0, 2 * j + n + 1)
                    ins = dve.tensor_tensor(lo[:, j], stage[:, j % 2], hi[:, j].bitcast(F32), ALU.subtract)
                ins.then_inc(w_ready, 1)

            low_weights(0)
            low_weights(1)
            dve.wait_ge(b2_loaded, 32)

            def body(e, k, parity):
                it = k * 2 + parity
                for j in range(FT):
                    if isinstance(it, int) and it == 0 and j + 2 < FT:
                        low_weights(j + 2)
                    dve.wait_ge(h_high, it * FT + (j + 1))
                    dve.wait_ge(y_part, it * FT + (j + 1))
                    dve.tensor_tensor(h_lo[:, j % 2, :], hid[:, j % 2, :], h_hi[:, j % 2, :].bitcast(F32),
                                      ALU.subtract).then_inc(h_low, 1)
                    if j == 3:
                        at = dve.snap(it * TB)
                        dve.tensor_copy(share_now[:], share[:].rearrange("p n t -> p (n t)")[:, bass.ds(at, TB)]).then_inc(share_out, 1)
                    if j == 4:
                        dve.wait_ge(x_loaded[parity], k * 16 + 16)
                        dve.wait_ge(share_out, it + 1)
                        for t in range(TB):
                            dve.scalar_tensor_tensor(out=x_rows[parity][:, t, :], in0=b2_rows[:, e, :], scalar=share_now[:, t:t + 1],
                                                     in1=x_rows[parity][:, t, :], op0=ALU.mult, op1=ALU.add).then_inc(x_biased, 1)
                for t in range(TB):
                    if t < TB - 1:
                        dve.wait_ge(y_done, it * (TB - 1) + (t + 1))
                    else:
                        dve.wait_ge(y_part, it * FT + (FT + 2))
                    dve.wait_ge(x_biased, it * TB + (t + 1))
                    dve.scalar_tensor_tensor(out=x_rows[parity][:, t, :], in0=y_bank[t][:], scalar=share_now[:, t:t + 1],
                                             in1=x_rows[parity][:, t, :], op0=ALU.mult, op1=ALU.add).then_inc(y_out, 1)

            rounds(dve, body)

        @block.tensor
        def _(pe):
            pe.sem_inc(y_part, 2)
            pe.wait_ge(const_built, 2)
            pe.wait_ge(ones_built, E + 1)
            pe.wait_ge(routed, 1)
            pe.matmul(h_bank[0][:, 0:E], ones[:], tile_sum[:], start=True, stop=True).then_inc(total_done, 1)
            pe.wait_ge(b1_loaded, 32)
            for n in range(2):
                ins = pe.transpose(h_bank[1][:, n * FT:(n + 1) * FT], b1_rows[:, n, :], ident[:])
            ins.then_inc(b1_turned, 1)
            pe.wait_ge(b1_out, 1)
            pe.wait_ge(routed, 2)

            with pe.Fori(0, 2) as e, pe.Fori(0, 4) as b:
                for parity in range(2):
                    it = pe.snap(e * 8 + b * 2 + parity)

                    def hidden(j):
                        if parity == 0:
                            pe.wait_ge(w_ready, e * FT + (j + 1))
                        pe.wait_ge(h_bank_free, it * FT + (j + 1))
                        for k in range(KT):
                            ins = split_product(pe, h_bank[j % 4][:], (w1_hi[:, j, k, :], w1_lo[:, j, k, :]),
                                                (z_hi[parity][:, :, k, :], z_lo[parity][:, :, k, :]), k == 0, k == KT - 1)
                        ins.then_inc(h_done, 1)

                    def output(j):
                        pe.wait_ge(h_low, it * FT + (j + 1 + 2))
                        for t in range(TB):
                            if j == 0:
                                pe.wait_ge(y_out, it * TB + (t + 1))
                            rows = slice(t * P, (t + 1) * P)
                            ins = split_product(pe, y_bank[t][:], (h_hi[:, j % 2, rows], h_lo[:, j % 2, rows]),
                                                (w2_hi[:, j, :], w2_lo[:, j, :]), j == 0, j == FT - 1)
                            if j == FT - 1 and t < TB - 1:
                                ins.then_inc(y_done, 1)
                        ins.then_inc(y_part, 1)

                    pe.wait_ge(z_loaded[parity], (e * 4 + b) * 32 + 32)
                    hidden(0)
                    for j in range(FT):
                        if j + 1 < FT:
                            hidden(j + 1)
                        output(j)


ROUTED_EXP = 13


_INS = {"x": "x", "ctx": "ctx_2048", "wqkv": "L0_attn_Wqkv", "bqkv": "L0_attn_bqkv", "wo": "L0_attn_Wo", "bo": "L0_attn_bo",
        "taps": "L0_xattn_ssm_kernel", "D": "L0_xattn_D", "gate": "L0_ffn_gate_w", "w1": "L0_ffn_w1", "b1": "L0_ffn_b1",
        "w2": "L0_ffn_w2", "b2": "L0_ffn_b2"}


def decoder_layer(nc, a, out):
    x_mid = nc.dram_tensor("x_mid", (T, B, C), F32, kind="Internal").ap()
    taps_d = nc.dram_tensor("taps_d", (2, CH, TAPW), F32, kind="Internal").ap()
    x_d = nc.dram_tensor("x_d", (CH, P, C), F32, kind="Internal").ap()
    zT_d = nc.dram_tensor("zT_d", (2, CH, P, KT, P), F32, kind="Internal").ap()
    attention(nc, a["x"], a["wqkv"], a["bqkv"], a["wo"], a["bo"], a["cos"], a["sin"], a["taps"], a["D"], x_mid, taps_d)
    with nc.sbuf_tensor("logits", [P, CH * CI], F32) as logits:
        convolution(nc, x_mid, a["ctx"], taps_d, a["gate"], logits, x_d, zT_d)
        experts(nc, logits, x_d, zT_d, a["w1"], a["b1"], a["w2"], a["b2"], out)


def kernel(**inputs):
    import numpy as np
    import concourse.bacc as bacc
    from concourse.bass_utils import run_bass_kernel_spmd as run

    nc = bacc.Bacc("TRN2", target_bir_lowering=False, num_devices=1)
    cos_t, sin_t = rotary_tables()
    given = {short: np.asarray(inputs[name]) for short, name in _INS.items()}
    given.update(cos=cos_t, sin=sin_t)
    arrays, args = {}, {}
    for name, value in given.items():
        arrays[f"in_{name}"] = np.ascontiguousarray(value)
        args[name] = nc.dram_tensor(f"in_{name}", arrays[f"in_{name}"].shape, F32, kind="ExternalInput").ap()
    out = nc.dram_tensor("out_0", (B, T, C), F32, kind="ExternalOutput").ap()
    decoder_layer(nc, args, out)
    return run(nc, [arrays], core_ids=[0]).results[0]["out_0"]
```
